# Optimizing a Trainium2 kernel written in Bass

```python
import numpy as np
import jax
import jax.numpy as jnp

def _softmax(x, axis=-1):
    return jax.nn.softmax(x, axis=axis)

def _gelu(x):
    return jax.nn.gelu(x, approximate=True)

def _silu(x):
    return jax.nn.silu(x)

def _sigmoid(x):
    return jax.nn.sigmoid(x)

def _layernorm(x, axis=-1, eps=1e-05):
    m = jnp.mean(x, axis=axis, keepdims=True)
    v = jnp.var(x, axis=axis, keepdims=True)
    return (x - m) / jnp.sqrt(v + eps)

def _scatter_add(tgt, idx, src, axis=0):
    return tgt.at[idx].add(src)

def _segment_sum(src, seg, n):
    return jax.ops.segment_sum(src, seg, n)
kernel_name = 'mk_xattn_ffn_d2_seqx_r8_9b742b'

def setup_inputs(seed: int=0):
    np.random.seed(seed)
    _w = jnp.asarray

    def _rec_inputs():
        import jax
        import jax.numpy as jnp
        _rk = jax.random.key(seed)
        x = -0.0002928 + 1 * jax.random.normal(jax.random.fold_in(_rk, 1), (128, 64, 128), jnp.float32)
        _lenS = 64 - jax.random.randint(jax.random.fold_in(_rk, 7), (128,), 0, max(1, 64 // 4) + 1, jnp.int32)
        _lenS2 = 64 - jax.random.randint(jax.random.fold_in(_rk, 8), (128,), 0, max(1, 64 // 4) + 1, jnp.int32)
        _ctx_1024P = jax.random.normal(jax.random.fold_in(_rk, 11), (128, 16, 128), jnp.float32)
        _ctx_1024c = jax.random.dirichlet(jax.random.fold_in(_rk, 511), 0.3 * jnp.ones((16,), jnp.float32), (128, 64))
        _ctx_1024t = jnp.einsum('bsk,bkd->bsd', _ctx_1024c, _ctx_1024P)
        _ctx_1024t = _ctx_1024t * jax.lax.rsqrt(jnp.mean(jnp.square(_ctx_1024t)) + 1e-12) * 0.953939
        ctx_1024 = -0.000191848 + 0.999787 * (_ctx_1024t + 0.3 * jax.random.normal(jax.random.fold_in(_rk, 611), (128, 64, 128), jnp.float32))
        _validS = jnp.arange(64)[None, :] < _lenS[:, None]
        _validS2 = jnp.arange(64)[None, :] < _lenS2[:, None]
        _causal = jnp.tril(jnp.ones((64, 64), dtype=bool))
        mask_SxS2_ik0 = jnp.where(jnp.broadcast_to(_validS2[0:1, :], (64, 64)), 0, 1).astype(jnp.int32)
        mask_Bx1x1xS2_if1 = jnp.where(jnp.ones((128, 1, 1, 64), dtype=bool), 1, 0).astype(jnp.int32)
        return (x, ctx_1024, mask_SxS2_ik0, mask_Bx1x1xS2_if1)
    x, ctx_1024, mask_SxS2_ik0, mask_Bx1x1xS2_if1 = _rec_inputs()

    def _L0_xattn_setup():
        import jax, jax.numpy as jnp
        import numpy as np
        D_MODEL = 128
        NUM_HEADS = 16
        DEPTH = D_MODEL // NUM_HEADS
        key = jax.random.key(seed)
        ks = jax.random.split(key, 10)
        B, T, C = (2, 256, 384)
        s = 1.0 / np.sqrt(D_MODEL)
        inp = {'x': jax.random.normal(ks[0], (B, T, D_MODEL), dtype=jnp.float32), 'context': jax.random.normal(ks[1], (B, C, D_MODEL), dtype=jnp.float32), 'Wq': jax.random.normal(ks[2], (D_MODEL, D_MODEL), dtype=jnp.float32) * s, 'bq': jnp.zeros((D_MODEL,), dtype=jnp.float32), 'Wk': jax.random.normal(ks[3], (D_MODEL, D_MODEL), dtype=jnp.float32) * s, 'bk': jnp.zeros((D_MODEL,), dtype=jnp.float32), 'Wv': jax.random.normal(ks[4], (D_MODEL, D_MODEL), dtype=jnp.float32) * s, 'bv': jnp.zeros((D_MODEL,), dtype=jnp.float32), 'Wo': jax.random.normal(ks[5], (D_MODEL, D_MODEL), dtype=jnp.float32) * s, 'bo': jnp.zeros((D_MODEL,), dtype=jnp.float32)}
        return inp
    _L0_xattn_all = _L0_xattn_setup()
    _L0_xattn_in = {k: v for k, v in _L0_xattn_all.items() if k in ('Wq', 'bq', 'Wk', 'bk', 'Wv', 'bv', 'Wo', 'bo')}
    del _L0_xattn_all

    def _L0_ffn_setup():
        import math
        import jax, jax.numpy as jnp
        import numpy as np
        E = 8
        H = 128
        HP = 128
        SPARSITY = 8
        N_ROTATE = 64
        ROPE_BASE = 10000.0

        def _rope(x, pos):
            half = N_ROTATE // 2
            inv_freq = 1.0 / ROPE_BASE ** (jnp.arange(half, dtype=jnp.float32) * 2.0 / N_ROTATE)
            ang = pos.astype(jnp.float32)[..., None] * inv_freq
            sin, cos = (jnp.sin(ang), jnp.cos(ang))
            x1, x2 = (x[..., :half], x[..., half:])
            return jnp.concatenate([x1 * cos - x2 * sin, x2 * cos + x1 * sin], axis=-1)
        key = jax.random.key(seed)
        k1, k2, k3, k4 = jax.random.split(key, 4)
        B, T = (4, 1024)
        X = jax.random.normal(k1, (B, T, H), dtype=jnp.float32)
        Wr = jax.random.uniform(k2, (E, H), minval=-1 / math.sqrt(H), maxval=1 / math.sqrt(H), dtype=jnp.float32)
        bq = 1 / math.sqrt(3 * HP)
        Wqkv = jax.random.uniform(k3, (E, H, 3 * HP), minval=-bq, maxval=bq, dtype=jnp.float32)
        bo = 1 / math.sqrt(H * E)
        Wo = jax.random.uniform(k4, (E, HP, H), minval=-bo, maxval=bo, dtype=jnp.float32)
        return {'X': X, 'Wr': Wr, 'Wqkv': Wqkv, 'Wo': Wo}
    _L0_ffn_all = _L0_ffn_setup()
    _L0_ffn_in = {k: v for k, v in _L0_ffn_all.items() if k in ('Wr', 'Wqkv', 'Wo')}
    del _L0_ffn_all

    def _L1_xattn_setup():
        import jax, jax.numpy as jnp
        import numpy as np
        import math
        D_MODEL = 128
        N_HEADS = 16
        D_FF = 512
        D_K = D_MODEL // N_HEADS
        B, S_DEC, S_ENC = (2, 256, 256)
        EPS = 1e-05
        NEG = -1000000000.0

        def _linear(x, w, b):
            return jnp.einsum('bsi,io->bso', x, w) + b

        def _mha(xq, xkv, wq, bq, wk, bk, wv, bv, wo, bo, mask):
            b, sq, _ = xq.shape
            sk = xkv.shape[1]
            q = _linear(xq, wq, bq).reshape(b, sq, N_HEADS, D_K).transpose(0, 2, 1, 3)
            k = _linear(xkv, wk, bk).reshape(b, sk, N_HEADS, D_K).transpose(0, 2, 1, 3)
            v = _linear(xkv, wv, bv).reshape(b, sk, N_HEADS, D_K).transpose(0, 2, 1, 3)
            scores = jnp.einsum('bhqd,bhkd->bhqk', q, k) / math.sqrt(D_K)
            if mask is not None:
                scores = jnp.where(mask == 0, NEG, scores)
            attn = jax.nn.softmax(scores, axis=-1)
            out = jnp.einsum('bhqk,bhkd->bhqd', attn, v)
            out = out.transpose(0, 2, 1, 3).reshape(b, sq, D_MODEL)
            return _linear(out, wo, bo)

        def _layernorm(x, gamma, beta):
            mean = jnp.mean(x, axis=-1, keepdims=True)
            std = jnp.sqrt(jnp.mean((x - mean) ** 2, axis=-1, keepdims=True))
            return (x - mean) / (std + EPS) * gamma + beta
        key = jax.random.key(seed)
        ks = jax.random.split(key, 24)
        sc = 1.0 / math.sqrt(D_MODEL)

        def W(k, i, o):
            return jax.random.normal(k, (i, o), jnp.float32) * sc
        inp = {'x': jax.random.normal(ks[0], (B, S_DEC, D_MODEL), jnp.float32), 'encoder_output': jax.random.normal(ks[1], (B, S_ENC, D_MODEL), jnp.float32), 'causal_mask': jnp.tril(jnp.ones((S_DEC, S_DEC), jnp.int32)), 'padding_mask': jnp.ones((B, 1, 1, S_ENC), jnp.int32), 'sa_wq': W(ks[2], D_MODEL, D_MODEL), 'sa_bq': jnp.zeros(D_MODEL), 'sa_wk': W(ks[3], D_MODEL, D_MODEL), 'sa_bk': jnp.zeros(D_MODEL), 'sa_wv': W(ks[4], D_MODEL, D_MODEL), 'sa_bv': jnp.zeros(D_MODEL), 'sa_wo': W(ks[5], D_MODEL, D_MODEL), 'sa_bo': jnp.zeros(D_MODEL), 'ca_wq': W(ks[6], D_MODEL, D_MODEL), 'ca_bq': jnp.zeros(D_MODEL), 'ca_wk': W(ks[7], D_MODEL, D_MODEL), 'ca_bk': jnp.zeros(D_MODEL), 'ca_wv': W(ks[8], D_MODEL, D_MODEL), 'ca_bv': jnp.zeros(D_MODEL), 'ca_wo': W(ks[9], D_MODEL, D_MODEL), 'ca_bo': jnp.zeros(D_MODEL), 'ff_w1': W(ks[10], D_MODEL, D_FF), 'ff_b1': jnp.zeros(D_FF), 'ff_w2': jax.random.normal(ks[11], (D_FF, D_MODEL), jnp.float32) / math.sqrt(D_FF), 'ff_b2': jnp.zeros(D_MODEL), 'g1': jnp.ones(D_MODEL), 'b1': jnp.zeros(D_MODEL), 'g2': jnp.ones(D_MODEL), 'b2': jnp.zeros(D_MODEL), 'g3': jnp.ones(D_MODEL), 'b3': jnp.zeros(D_MODEL)}
        return inp
    _L1_xattn_all = _L1_xattn_setup()
    _L1_xattn_in = {k: v for k, v in _L1_xattn_all.items() if k in ('sa_wq', 'sa_bq', 'sa_wk', 'sa_bk', 'sa_wv', 'sa_bv', 'sa_wo', 'sa_bo', 'ca_wq', 'ca_bq', 'ca_wk', 'ca_bk', 'ca_wv', 'ca_bv', 'ca_wo', 'ca_bo', 'ff_w1', 'ff_b1', 'ff_w2', 'ff_b2', 'g1', 'b1', 'g2', 'b2', 'g3', 'b3')}
    del _L1_xattn_all

    def _L1_ffn_setup():
        import jax, jax.numpy as jnp
        import numpy as np
        B, S, D = (1, 256, 128)
        E, F = (16, 128)
        NG, TKG, K = (4, 2, 4)
        NSH = 2
        SCALE = 2.5
        STD = 0.02
        EPG = E // NG

        def _route(x_flat, router_w, bias):
            logits = x_flat.astype(jnp.float32) @ router_w.T
            scores = jax.nn.sigmoid(logits)
            s = scores + bias[None, :]
            sg = s.reshape(-1, NG, EPG)
            group_score = jax.lax.top_k(sg, 2)[0].sum(-1)
            gidx = jax.lax.top_k(group_score, TKG)[1]
            gmask = jnp.sum(jax.nn.one_hot(gidx, NG, dtype=jnp.float32), axis=1) > 0
            emask = jnp.repeat(gmask, EPG, axis=1)
            masked = jnp.where(emask, s, -1.0)
            topk_idx = jax.lax.top_k(masked, K)[1]
            tw = jnp.take_along_axis(scores, topk_idx, axis=1)
            tw = tw / (tw.sum(-1, keepdims=True) + 1e-20)
            tw = tw * SCALE
            return (topk_idx, tw)
        key = jax.random.key(seed)
        ks = jax.random.split(key, 8)
        return {'hidden_states': jax.random.normal(ks[0], (B, S, D), jnp.float32), 'router_w': jax.random.normal(ks[1], (E, D), jnp.float32) * STD, 'bias': jnp.zeros((E,), jnp.float32), 'gate_w': jax.random.normal(ks[2], (E, D, F), jnp.float32) * STD, 'up_w': jax.random.normal(ks[3], (E, D, F), jnp.float32) * STD, 'down_w': jax.random.normal(ks[4], (E, F, D), jnp.float32) * STD, 'sh_gate_w': jax.random.normal(ks[5], (D, NSH * F), jnp.float32) * STD, 'sh_up_w': jax.random.normal(ks[6], (D, NSH * F), jnp.float32) * STD, 'sh_down_w': jax.random.normal(ks[7], (NSH * F, D), jnp.float32) * STD}
    _L1_ffn_all = _L1_ffn_setup()
    _L1_ffn_in = {k: v for k, v in _L1_ffn_all.items() if k in ('router_w', 'bias', 'gate_w', 'up_w', 'down_w', 'sh_gate_w', 'sh_up_w', 'sh_down_w')}
    del _L1_ffn_all
    return {'x': x, 'ctx_1024': ctx_1024, 'mask_SxS2_ik0': mask_SxS2_ik0, 'mask_Bx1x1xS2_if1': mask_Bx1x1xS2_if1, 'L0_xattn_Wq': _L0_xattn_in['Wq'], 'L0_xattn_bq': _L0_xattn_in['bq'], 'L0_xattn_Wk': _L0_xattn_in['Wk'], 'L0_xattn_bk': _L0_xattn_in['bk'], 'L0_xattn_Wv': _L0_xattn_in['Wv'], 'L0_xattn_bv': _L0_xattn_in['bv'], 'L0_xattn_Wo': _L0_xattn_in['Wo'], 'L0_xattn_bo': _L0_xattn_in['bo'], 'L0_ffn_Wr': _L0_ffn_in['Wr'], 'L0_ffn_Wqkv': _L0_ffn_in['Wqkv'], 'L0_ffn_Wo': _L0_ffn_in['Wo'], 'L1_xattn_sa_wq': _L1_xattn_in['sa_wq'], 'L1_xattn_sa_bq': _L1_xattn_in['sa_bq'], 'L1_xattn_sa_wk': _L1_xattn_in['sa_wk'], 'L1_xattn_sa_bk': _L1_xattn_in['sa_bk'], 'L1_xattn_sa_wv': _L1_xattn_in['sa_wv'], 'L1_xattn_sa_bv': _L1_xattn_in['sa_bv'], 'L1_xattn_sa_wo': _L1_xattn_in['sa_wo'], 'L1_xattn_sa_bo': _L1_xattn_in['sa_bo'], 'L1_xattn_ca_wq': _L1_xattn_in['ca_wq'], 'L1_xattn_ca_bq': _L1_xattn_in['ca_bq'], 'L1_xattn_ca_wk': _L1_xattn_in['ca_wk'], 'L1_xattn_ca_bk': _L1_xattn_in['ca_bk'], 'L1_xattn_ca_wv': _L1_xattn_in['ca_wv'], 'L1_xattn_ca_bv': _L1_xattn_in['ca_bv'], 'L1_xattn_ca_wo': _L1_xattn_in['ca_wo'], 'L1_xattn_ca_bo': _L1_xattn_in['ca_bo'], 'L1_xattn_ff_w1': _L1_xattn_in['ff_w1'], 'L1_xattn_ff_b1': _L1_xattn_in['ff_b1'], 'L1_xattn_ff_w2': _L1_xattn_in['ff_w2'], 'L1_xattn_ff_b2': _L1_xattn_in['ff_b2'], 'L1_xattn_g1': _L1_xattn_in['g1'], 'L1_xattn_b1': _L1_xattn_in['b1'], 'L1_xattn_g2': _L1_xattn_in['g2'], 'L1_xattn_b2': _L1_xattn_in['b2'], 'L1_xattn_g3': _L1_xattn_in['g3'], 'L1_xattn_b3': _L1_xattn_in['b3'], 'L1_ffn_router_w': _L1_ffn_in['router_w'], 'L1_ffn_bias': _L1_ffn_in['bias'], 'L1_ffn_gate_w': _L1_ffn_in['gate_w'], 'L1_ffn_up_w': _L1_ffn_in['up_w'], 'L1_ffn_down_w': _L1_ffn_in['down_w'], 'L1_ffn_sh_gate_w': _L1_ffn_in['sh_gate_w'], 'L1_ffn_sh_up_w': _L1_ffn_in['sh_up_w'], 'L1_ffn_sh_down_w': _L1_ffn_in['sh_down_w']}

def reference(x, ctx_1024, mask_SxS2_ik0, mask_Bx1x1xS2_if1, L0_xattn_Wq, L0_xattn_bq, L0_xattn_Wk, L0_xattn_bk, L0_xattn_Wv, L0_xattn_bv, L0_xattn_Wo, L0_xattn_bo, L0_ffn_Wr, L0_ffn_Wqkv, L0_ffn_Wo, L1_xattn_sa_wq, L1_xattn_sa_bq, L1_xattn_sa_wk, L1_xattn_sa_bk, L1_xattn_sa_wv, L1_xattn_sa_bv, L1_xattn_sa_wo, L1_xattn_sa_bo, L1_xattn_ca_wq, L1_xattn_ca_bq, L1_xattn_ca_wk, L1_xattn_ca_bk, L1_xattn_ca_wv, L1_xattn_ca_bv, L1_xattn_ca_wo, L1_xattn_ca_bo, L1_xattn_ff_w1, L1_xattn_ff_b1, L1_xattn_ff_w2, L1_xattn_ff_b2, L1_xattn_g1, L1_xattn_b1, L1_xattn_g2, L1_xattn_b2, L1_xattn_g3, L1_xattn_b3, L1_ffn_router_w, L1_ffn_bias, L1_ffn_gate_w, L1_ffn_up_w, L1_ffn_down_w, L1_ffn_sh_gate_w, L1_ffn_sh_up_w, L1_ffn_sh_down_w):
    import jax
    import jax.numpy as jnp

    def _L0_xattn_ref(x, context, Wq, bq, Wk, bk, Wv, bv, Wo, bo):
        import jax, jax.numpy as jnp
        import numpy as np
        D_MODEL = 128
        NUM_HEADS = 16
        DEPTH = D_MODEL // NUM_HEADS
        B, T, D = x.shape
        C = context.shape[1]
        H, d = (NUM_HEADS, DEPTH)
        q = x @ Wq.T + bq
        k = context @ Wk.T + bk
        v = context @ Wv.T + bv
        q = q.reshape(B, T, H, d).transpose(0, 2, 1, 3)
        k = k.reshape(B, C, H, d).transpose(0, 2, 1, 3)
        v = v.reshape(B, C, H, d).transpose(0, 2, 1, 3)
        scores = jnp.einsum('bhtd,bhcd->bhtc', q, k) / jnp.sqrt(jnp.asarray(d, x.dtype))
        attn = jax.nn.softmax(scores, axis=-1)
        out = jnp.einsum('bhtc,bhcd->bhtd', attn, v)
        out = out.transpose(0, 2, 1, 3).reshape(B, T, D)
        return out @ Wo.T + bo

    def _L0_ffn_ref(X, Wr, Wqkv, Wo):
        import math
        import jax, jax.numpy as jnp
        import numpy as np
        E = 8
        H = 128
        HP = 128
        SPARSITY = 8
        N_ROTATE = 64
        ROPE_BASE = 10000.0

        def _rope(x, pos):
            half = N_ROTATE // 2
            inv_freq = 1.0 / ROPE_BASE ** (jnp.arange(half, dtype=jnp.float32) * 2.0 / N_ROTATE)
            ang = pos.astype(jnp.float32)[..., None] * inv_freq
            sin, cos = (jnp.sin(ang), jnp.cos(ang))
            x1, x2 = (x[..., :half], x[..., half:])
            return jnp.concatenate([x1 * cos - x2 * sin, x2 * cos + x1 * sin], axis=-1)
        B, T, _ = X.shape
        k = min(max(T // SPARSITY, 2), T)
        logits = jax.nn.sigmoid(jnp.einsum('bth,eh->bte', X, Wr))
        topk_vals, topk_I = jax.lax.top_k(logits.transpose(0, 2, 1), k)
        idx_flat = topk_I.reshape(B, E * k)
        Xg = jnp.take_along_axis(X, idx_flat[:, :, None], axis=1).reshape(B, E, k, H)
        QKV = jnp.einsum('beki,eij->bekj', Xg, Wqkv)
        Q, K, V = jnp.split(QKV, 3, axis=-1)
        Q = jnp.concatenate([_rope(Q[..., :N_ROTATE], topk_I), Q[..., N_ROTATE:]], axis=-1)
        K = jnp.concatenate([_rope(K[..., :N_ROTATE], topk_I), K[..., N_ROTATE:]], axis=-1)
        M = topk_I[..., :, None] >= topk_I[..., None, :]
        scores = jnp.einsum('bekd,bemd->bekm', Q, K) / math.sqrt(HP)
        scores = jnp.where(M, scores, -jnp.inf)
        A = jax.nn.softmax(scores, axis=-1)
        AV = jnp.einsum('bekm,bemd->bekd', A, V)
        AV = AV * topk_vals[..., None]
        Xpre = jnp.einsum('bekj,eji->beki', AV, Wo)
        out = jnp.zeros((B, T, H), dtype=X.dtype)
        out = out.at[jnp.arange(B)[:, None], idx_flat].add(Xpre.reshape(B, E * k, H))
        return out

    def _L1_xattn_ref(x, encoder_output, causal_mask, padding_mask, sa_wq, sa_bq, sa_wk, sa_bk, sa_wv, sa_bv, sa_wo, sa_bo, ca_wq, ca_bq, ca_wk, ca_bk, ca_wv, ca_bv, ca_wo, ca_bo, ff_w1, ff_b1, ff_w2, ff_b2, g1, b1, g2, b2, g3, b3):
        import jax, jax.numpy as jnp
        import numpy as np
        import math
        D_MODEL = 128
        N_HEADS = 16
        D_FF = 512
        D_K = D_MODEL // N_HEADS
        B, S_DEC, S_ENC = (2, 256, 256)
        EPS = 1e-05
        NEG = -1000000000.0

        def _linear(x, w, b):
            return jnp.einsum('bsi,io->bso', x, w) + b

        def _mha(xq, xkv, wq, bq, wk, bk, wv, bv, wo, bo, mask):
            b, sq, _ = xq.shape
            sk = xkv.shape[1]
            q = _linear(xq, wq, bq).reshape(b, sq, N_HEADS, D_K).transpose(0, 2, 1, 3)
            k = _linear(xkv, wk, bk).reshape(b, sk, N_HEADS, D_K).transpose(0, 2, 1, 3)
            v = _linear(xkv, wv, bv).reshape(b, sk, N_HEADS, D_K).transpose(0, 2, 1, 3)
            scores = jnp.einsum('bhqd,bhkd->bhqk', q, k) / math.sqrt(D_K)
            if mask is not None:
                scores = jnp.where(mask == 0, NEG, scores)
            attn = jax.nn.softmax(scores, axis=-1)
            out = jnp.einsum('bhqk,bhkd->bhqd', attn, v)
            out = out.transpose(0, 2, 1, 3).reshape(b, sq, D_MODEL)
            return _linear(out, wo, bo)

        def _layernorm(x, gamma, beta):
            mean = jnp.mean(x, axis=-1, keepdims=True)
            std = jnp.sqrt(jnp.mean((x - mean) ** 2, axis=-1, keepdims=True))
            return (x - mean) / (std + EPS) * gamma + beta
        sa = _mha(x, x, sa_wq, sa_bq, sa_wk, sa_bk, sa_wv, sa_bv, sa_wo, sa_bo, causal_mask)
        x = _layernorm(x + sa, g1, b1)
        ca = _mha(x, encoder_output, ca_wq, ca_bq, ca_wk, ca_bk, ca_wv, ca_bv, ca_wo, ca_bo, padding_mask)
        x = _layernorm(x + ca, g2, b2)
        h = jax.nn.relu(_linear(x, ff_w1, ff_b1))
        ff = _linear(h, ff_w2, ff_b2)
        x = _layernorm(x + ff, g3, b3)
        return x

    def _L1_ffn_ref(hidden_states, router_w, bias, gate_w, up_w, down_w, sh_gate_w, sh_up_w, sh_down_w):
        import jax, jax.numpy as jnp
        import numpy as np
        B, S, D = (1, 256, 128)
        E, F = (16, 128)
        NG, TKG, K = (4, 2, 4)
        NSH = 2
        SCALE = 2.5
        STD = 0.02
        EPG = E // NG

        def _route(x_flat, router_w, bias):
            logits = x_flat.astype(jnp.float32) @ router_w.T
            scores = jax.nn.sigmoid(logits)
            s = scores + bias[None, :]
            sg = s.reshape(-1, NG, EPG)
            group_score = jax.lax.top_k(sg, 2)[0].sum(-1)
            gidx = jax.lax.top_k(group_score, TKG)[1]
            gmask = jnp.sum(jax.nn.one_hot(gidx, NG, dtype=jnp.float32), axis=1) > 0
            emask = jnp.repeat(gmask, EPG, axis=1)
            masked = jnp.where(emask, s, -1.0)
            topk_idx = jax.lax.top_k(masked, K)[1]
            tw = jnp.take_along_axis(scores, topk_idx, axis=1)
            tw = tw / (tw.sum(-1, keepdims=True) + 1e-20)
            tw = tw * SCALE
            return (topk_idx, tw)
        x = hidden_states.reshape(-1, D)
        topk_idx, tw = _route(x, router_w, bias)
        combine = (jax.nn.one_hot(topk_idx, E, dtype=tw.dtype) * tw[..., None]).sum(1)
        h = jnp.einsum('td,edf->etf', x, gate_w)
        u = jnp.einsum('td,edf->etf', x, up_w)
        y = jnp.einsum('etf,efd->etd', jax.nn.silu(h) * u, down_w)
        routed = jnp.einsum('etd,te->td', y, combine)
        sh = jax.nn.silu(x @ sh_gate_w) * (x @ sh_up_w) @ sh_down_w
        return (routed + sh).reshape(hidden_states.shape)
    x = x + _L0_xattn_ref(_layernorm(x, axis=-1), ctx_1024, L0_xattn_Wq, L0_xattn_bq, L0_xattn_Wk, L0_xattn_bk, L0_xattn_Wv, L0_xattn_bv, L0_xattn_Wo, L0_xattn_bo)
    x = x + _L0_ffn_ref(_layernorm(x, axis=-1), L0_ffn_Wr, L0_ffn_Wqkv, L0_ffn_Wo)
    x = x + _L1_xattn_ref(_layernorm(x, axis=-1), ctx_1024, mask_SxS2_ik0, mask_Bx1x1xS2_if1, L1_xattn_sa_wq, L1_xattn_sa_bq, L1_xattn_sa_wk, L1_xattn_sa_bk, L1_xattn_sa_wv, L1_xattn_sa_bv, L1_xattn_sa_wo, L1_xattn_sa_bo, L1_xattn_ca_wq, L1_xattn_ca_bq, L1_xattn_ca_wk, L1_xattn_ca_bk, L1_xattn_ca_wv, L1_xattn_ca_bv, L1_xattn_ca_wo, L1_xattn_ca_bo, L1_xattn_ff_w1, L1_xattn_ff_b1, L1_xattn_ff_w2, L1_xattn_ff_b2, L1_xattn_g1, L1_xattn_b1, L1_xattn_g2, L1_xattn_b2, L1_xattn_g3, L1_xattn_b3)
    x = x + _L1_ffn_ref(_layernorm(x, axis=-1), L1_ffn_router_w, L1_ffn_bias, L1_ffn_gate_w, L1_ffn_up_w, L1_ffn_down_w, L1_ffn_sh_gate_w, L1_ffn_sh_up_w, L1_ffn_sh_down_w)
    return x

_drawn_inputs = setup_inputs


def setup_inputs(seed=0):
    import zlib

    import numpy as np

    out = dict(_drawn_inputs(seed))
    spreads = {'L0_xattn_bq': (0.0, 0.325),
     'L0_xattn_bk': (0.0, 0.8),
     'L0_xattn_bv': (0.0, 0.1),
     'L0_xattn_bo': (0.0, 0.1),
     'L1_xattn_sa_bq': (0.0, 0.71),
     'L1_xattn_sa_bk': (0.0, 0.8),
     'L1_xattn_sa_bv': (0.0, 0.1),
     'L1_xattn_sa_bo': (0.0, 0.1),
     'L1_xattn_ca_bq': (0.0, 0.676),
     'L1_xattn_ca_bk': (0.0, 0.8),
     'L1_xattn_ca_bv': (0.0, 0.1),
     'L1_xattn_ca_bo': (0.0, 0.1),
     'L1_xattn_ff_b1': (0.0, 0.268),
     'L1_xattn_ff_b2': (0.0, 0.1),
     'L1_xattn_g1': (1.0, 0.2),
     'L1_xattn_b1': (0.0, 0.1),
     'L1_xattn_g2': (1.0, 0.2),
     'L1_xattn_b2': (0.0, 0.1),
     'L1_xattn_g3': (1.0, 0.2),
     'L1_xattn_b3': (0.0, 0.1),
     'L1_ffn_bias': (0.0, 0.8)}
    factors = {'L1_ffn_router_w': 8.0,
     'L1_ffn_gate_w': 8.0,
     'L1_ffn_up_w': 8.0,
     'L1_ffn_down_w': 8.0,
     'L1_ffn_sh_gate_w': 8.0,
     'L1_ffn_sh_up_w': 8.0,
     'L1_ffn_sh_down_w': 8.0}
    for name, (base, spread) in spreads.items():
        noise = np.random.default_rng([zlib.crc32(name.encode()), seed]).standard_normal(out[name].shape)
        drawn = base * np.exp(spread * noise) if base else spread * noise
        out[name] = jnp.asarray(drawn.astype(out[name].dtype))
    for name, factor in factors.items():
        out[name] = (out[name] * factor).astype(out[name].dtype)
    return out
```

```python
from contextlib import ExitStack

import numpy as np

import concourse.bass as bass
from concourse import mybir

F32 = mybir.dt.float32
BF16 = mybir.dt.bfloat16
I32 = mybir.dt.int32
ALU = mybir.AluOpType
ACT = mybir.ActivationFunctionType
AX = mybir.AxisListType

P = 128
D = 128
S = 64
BATCH = 128
H = 16
DH = D // H
TILES = 4
GB = 2 * TILES
TOK = TILES * P
NG = BATCH // GB
UNITS = 2 * TILES
HH = H // 2
NEG = -1.0e9
SCALE = float(DH) ** -0.5
EPS = 1e-5

ATTN_W = 3 * D + 2 * D + 4
COLS = {}
_at = 0
for _n, _w in [("a0", ATTN_W), ("a1", ATTN_W), ("a2", ATTN_W), ("ident", P), ("sel", P), ("headmask", HH),
               ("g1", D), ("b1", D), ("g2", D), ("b2", D), ("g3", D), ("b3", D), ("ff2b", D),
               ("negmask", P), ("kiota", 64), ("resetmask", 256), ("trig", P), ("wr", 32),
               ("ff1", 4 * D), ("ff1b", 4), ("ff2", 4 * D), ("router", 16), ("rbias", 64),
               ("lowmask", 256), ("glowmask", 16)]:
    COLS[_n] = (_at, _w)
    _at += _w
PACK = _at


class Signals:

    def __init__(self, nc, prefix):
        self.nc, self.prefix, self.taken = nc, prefix, []

    def __enter__(self):
        return self

    def __exit__(self, *_):
        self.nc.clear_and_free_semaphores(self.taken)
        self.nc.all_engine_barrier()

    def __call__(self, name):
        self.taken.append(self.nc.alloc_semaphore(self.prefix + name))
        return self.taken[-1]


def attention_phase(nc, ps, C, x_res, y_res, x_in, ctx_in, q_mask, key_mask, a):
    cross = a != 1
    load_x = a == 0
    pre_norm = a != 2
    post_norm = a != 0

    with ExitStack() as ctx:
        def sb(name, shape, dt=F32):
            return ctx.enter_context(nc.sbuf_tensor(f"{name}{a}", shape, dt))

        sem = ctx.enter_context(Signals(nc, f"a{a}_"))

        base = COLS[f"a{a}"][0]
        pk = C["pack"]
        wq, wk, wv = (pk[:, base + i * D:base + (i + 1) * D] for i in range(3))
        wo = pk[:, base + 3 * D:base + 5 * D].rearrange("p (r n) -> p r n", r=2)
        bq, bk = (pk[:, base + 5 * D + i:base + 5 * D + i + 1] for i in range(2))
        ident, sel = C["ident"], C["sel"]

        xn = sb("xn", [P, 2, TILES, D])
        qT = sb("qT", [P, 2, TOK])
        kblk = sb("kblk", [P, 2, GB, HH, S])
        vblk = sb("vblk", [P, 2, GB, HH, 32])
        srcT = sb("srcT", [P, TOK])
        ctxT = sb("ctxT", [P, TOK]) if cross else srcT
        ksb = sb("ksb", [P, TOK])
        stats = sb("stats", [P, TILES, 6])
        mv = sb("mv", [P, TILES, 2])
        veps = sb("veps", [P, TILES])
        rstd = sb("rstd", [P, TILES])
        mx = sb("mx", [P, 2, HH])
        sh = sb("sh", [P, 2, HH * S])
        ex = sb("ex", [P, 2, 4, P])
        osb = sb("osb", [P, 2, 2 * 2 * P])
        on = sb("on", [P, 2, 2, 2, P])
        inv = sb("inv", [P, 2, 2 * 2 * P])
        if cross:
            cin = sb("cin", [P, 2, TILES, D])
        if a == 2:
            kmi = sb("kmi", [P, 2, GB, S], I32)
            kmb = sb("kmb", [P, 2, GB, S], BF16)
            kany = sb("kany", [P, 2, GB])
            qsc = sb("qsc", [P, 2, GB])
        if post_norm:
            t1 = sb("t1", [P, 2, 2, D])
            st2 = sb("st2", [P, 2, 2, 6])
            mv2 = sb("mv2", [P, 2, 2, 2])
            sd2 = sb("sd2", [P, 2, 2])
            se2 = sb("se2", [P, 2, 2])
            rs2 = sb("rs2", [P, 2, 2])
            z2 = sb("z2", [P, 2, 2, D])
            zg2 = sb("zg2", [P, 2, 2, D])
            gam, bet = C[f"g{a}"], C[f"b{a}"]

        SB = [ps[:, i, :] for i in (0, 1)]
        TB = [ps[:, i, :] for i in (2, 3)]
        OB = [ps[:, i, :] for i in (4, 5)]
        PREP = ps[:, 6, :]
        PROJ = ps[:, 7, :]

        x_loaded = [sem(f"x_loaded{s}_") for s in (0, 1)]
        c_loaded = [sem(f"c_loaded{s}_") for s in (0, 1)]
        m_loaded = [sem(f"m_loaded{s}_") for s in (0, 1)]
        vblk_set = sem("vblk_set")
        stats_done = sem("stats_done")
        moments = sem("moments")
        var_eps = sem("var_eps")
        rstd_done = sem("rstd_done")
        xn_ready = sem("xn_ready")
        kmask_bias = sem("kmask_bias")
        kmask_any = sem("kmask_any")
        kmask_ready = sem("kmask_ready")
        xT_ready = sem("xT_ready")
        xT_copied = sem("xT_copied")
        cT_ready = sem("cT_ready")
        cT_copied = sem("cT_copied")
        k_ready = sem("k_ready")
        k_copied = sem("k_copied")
        kblk_ready = sem("kblk_ready")
        q_ready = sem("q_ready")
        q_copied = sem("q_copied")
        v_ready = sem("v_ready")
        v_copied = sem("v_copied")
        s_ready = sem("s_ready")
        max_done = sem("max_done")
        shifted = sem("shifted")
        t_ready = sem("t_ready")
        e_ready = sem("e_ready")
        o_ready = sem("o_ready")
        o_copied = sem("o_copied")
        den_ready = sem("den_ready")
        inverted = sem("inverted")
        divided = sem("divided")
        proj_ready = sem("proj_ready")
        resid_done = sem("resid_done")
        stats2_done = sem("stats2_done")
        moments2 = sem("moments2")
        std2 = sem("std2")
        std2_eps = sem("std2_eps")
        rstd2 = sem("rstd2")
        z_done = sem("z_done")
        zg_done = sem("zg_done")
        y_done = sem("y_done")

        def loaded(g, s):
            return g * 8 + (16 - 8 * s)

        passed = sem("passed")
        block = ctx.enter_context(nc.Block())

        @block.sync
        def _(sp):
            def loads(g, s):
                if load_x:
                    sp.dma_start(tiles_of(x_res, g),
                                 x_in[bass.ds(g * TOK, TOK), :].rearrange("(t p) d -> p t d", p=P)
                                 ).then_inc(x_loaded[s], 16)
                if cross:
                    sp.dma_start(cin[:, s], ctx_in[bass.ds(g * TOK, TOK), :].rearrange("(t p) d -> p t d", p=P)
                                 ).then_inc(c_loaded[s], 16)
                if a == 2:
                    sp.dma_start(kmi[:, s], key_mask[bass.ds(g * GB, GB), :].partition_broadcast(P)
                                 ).then_inc(m_loaded[s], 16)

            if cross:
                loads(0, 0)
                loads(1, 1)
                with sp.Fori(0, NG // 2 - 1) as i:
                    for s in (0, 1):
                        sp.wait_ge(cT_ready, nth(i * 2 + s))
                        if a == 2:
                            sp.wait_ge(kmask_bias, nth(i * 2 + s))
                        loads(i * 2 + (s + 2), s)

        @block.gpsimd
        def _(pool):
            def rstd_of_next(g, s):
                if pre_norm:
                    pool.wait_ge(var_eps, nth(g))
                    nc.gpsimd.tensor_tensor(rstd[:, :], veps[:, :], C["mhalf"][:, 0:TILES], ALU.pow).then_inc(rstd_done, 1)
                else:
                    nc.gpsimd.tensor_copy(xn[:, s], tiles_of(y_res, g)).then_inc(xn_ready, 1)

            def kblk_of_next(g, s):
                pool.wait_ge(k_copied, g + 1)
                pool.sem_inc(passed, 1)
                for j in range(HH):
                    last = nc.gpsimd.tensor_scalar(kblk[:, s, :, j, :], ksb[:, :].rearrange("p (b k) -> p b k", k=S),
                                                   C["headmask"][:, j:j + 1], None, ALU.mult)
                last.then_inc(kblk_ready, 1)

            def prep(g, s):
                rstd_of_next(g, s)
                kblk_of_next(g, s)

            def finish(g, s, m):
                if post_norm:
                    pool.wait_ge(moments2, nth(g, 2, m))
                    nc.gpsimd.tensor_tensor(sd2[:, m, :], mv2[:, m, :, 1], C["half"][:, 0:2], ALU.pow).then_inc(std2, 1)
                    pool.wait_ge(z_done, nth(g, 2, m))
                    nc.gpsimd.tensor_tensor(zg2[:, m], z2[:, m], gam.unsqueeze(1).broadcast_to((P, 2, D)), ALU.mult).then_inc(zg_done, 1)
                    pool.wait_ge(zg_done, g * 2 + (m + 1))
                    pool.sem_inc(passed, 1)
                    nc.gpsimd.tensor_tensor(tiles_of(y_res, g, 2 * m, 2), zg2[:, m],
                                            bet.unsqueeze(1).broadcast_to((P, 2, D)), ALU.add).then_inc(y_done, 1)

            def step(g, s, more):
                if more:
                    prep(g + 1, 1 - s)
                finish(g, s, 0)
                finish(g, s, 1)

            two_halves(pool, NG, prep, step)

        @block.scalar
        def _(act):
            def copy_xT(g, s):
                act.wait_ge(xT_ready, nth(g))
                nc.scalar.copy(srcT[:, :], PREP).then_inc(xT_copied, 1)

            def copy_cT(g, s):
                if cross:
                    act.wait_ge(cT_ready, nth(g))
                    nc.scalar.copy(ctxT[:, :], PREP).then_inc(cT_copied, 1)

            def copy_k(g, s):
                act.wait_ge(k_ready, nth(g))
                act.wait_ge(kblk_ready, g)
                nc.scalar.activation(ksb[:, :], PREP, ACT.Identity, bias=bk).then_inc(k_copied, 1)

            def copy_v(g, s, h):
                act.wait_ge(v_ready, nth(g, 2, h))
                for j in (0, 1):
                    rows = slice(64 * j, 64 * j + 64)
                    last = nc.scalar.copy(
                        vblk[rows, s, 4 * h:4 * h + 4, :, 16 * j:16 * j + DH].rearrange("p b r e -> p (b r) e"),
                        PREP[rows, :].rearrange("p (b e) -> p b e", e=2 * DH)[:, :, DH * j:DH * j + DH])
                last.then_inc(v_copied, 1)

            def exps(g, u):
                act.wait_ge(t_ready, nth(g, UNITS, u))
                nc.scalar.activation(ex[:, u % 2], TB[u % 2].rearrange("p (c n) -> p c n", n=P), ACT.Exp).then_inc(e_ready, 1)

            def copy_o(g, m):
                act.wait_ge(o_ready, nth(g, 2, m))
                nc.scalar.copy(osb[:, m], OB[m]).then_inc(o_copied, 1)

            def prep(g, s):
                copy_xT(g, s)
                copy_cT(g, s)
                copy_k(g, s)
                copy_v(g, s, 0)
                copy_v(g, s, 1)

            def step(g, s, more):
                for u in range(UNITS):
                    exps(g, u)
                    if more and u == 1:
                        copy_xT(g + 1, 1 - s)
                    if more and u == 2:
                        copy_cT(g + 1, 1 - s)
                    if more and u == 3:
                        copy_k(g + 1, 1 - s)
                    if u == 4:
                        copy_o(g, 0)
                    if more and u == 5:
                        copy_v(g + 1, 1 - s, 0)
                if more:
                    copy_v(g + 1, 1 - s, 1)
                copy_o(g, 1)

            act.wait_ge(vblk_set, 3)
            two_halves(act, NG, prep, step)

        @block.vector
        def _(dve):
            def norm_stats(g, s):
                if not pre_norm:
                    return
                if load_x:
                    dve.wait_ge(x_loaded[s], loaded(g, s))
                src = x_res
                for t in range(TILES):
                    last = nc.vector.bn_stats(stats[:, t, :], tiles_of(src, g, t, 1))
                last.then_inc(stats_done, 1)
                dve.wait_ge(stats_done, g + 1)
                dve.sem_inc(passed, 1)
                for t in range(TILES):
                    last = nc.vector.bn_aggr(mv[:, t, :], stats[:, t, :])
                last.then_inc(moments, 1)
                dve.wait_ge(moments, nth(g))
                nc.vector.tensor_scalar(veps[:, :], mv[:, :, 1], EPS, None, ALU.add).then_inc(var_eps, 1)

            def norm_apply(g, s):
                if not pre_norm:
                    return
                dve.wait_ge(rstd_done, nth(g))
                for t in range(TILES):
                    last = nc.vector.tensor_scalar(xn[:, s, t:t + 1, :], tiles_of(x_res, g, t, 1), mv[:, t, 0:1],
                                                   rstd[:, t:t + 1], ALU.subtract, ALU.mult)
                last.then_inc(xn_ready, 1)

            def key_mask_of_next(g, s):
                if a != 2:
                    return
                dve.wait_ge(m_loaded[s], loaded(g, s))
                nc.vector.tensor_scalar(kmb[:, s], kmi[:, s], 0.0, NEG, ALU.is_equal, ALU.mult).then_inc(kmask_bias, 1)
                dve.wait_ge(kmask_bias, nth(g))
                nc.vector.tensor_reduce(kany[:, s], kmb[:, s], AX.X, ALU.max).then_inc(kmask_any, 1)
                dve.wait_ge(kmask_any, nth(g))
                nc.vector.tensor_scalar(qsc[:, s], kany[:, s], 0.0, SCALE, ALU.is_equal, ALU.mult).then_inc(kmask_ready, 1)

            def copy_q(g, s):
                dve.wait_ge(q_ready, nth(g))
                if a == 0:
                    nc.vector.tensor_scalar(qT[:, s], PREP, bq, SCALE, ALU.add, ALU.mult).then_inc(q_copied, 1)
                else:
                    if a == 1:
                        sc = C["qscale"][:, :].unsqueeze(1).broadcast_to((P, GB, S))
                    else:
                        dve.wait_ge(kmask_ready, nth(g))
                        sc = qsc[:, s].unsqueeze(2).broadcast_to((P, GB, S))
                    nc.vector.scalar_tensor_tensor(qT[:, s].rearrange("p (b k) -> p b k", k=S),
                                                   PREP.rearrange("p (b k) -> p b k", k=S), bq, sc,
                                                   ALU.add, ALU.mult).then_inc(q_copied, 1)

            def shift(g, u):
                dve.wait_ge(s_ready, nth(g, UNITS, u))
                sc = SB[u % 2].rearrange("p (h k) -> p h k", k=S)
                nc.vector.tensor_reduce(mx[:, u % 2], sc, AX.X, ALU.max).then_inc(max_done, 1)
                dve.wait_ge(max_done, nth(g, UNITS, u))
                nc.vector.tensor_tensor(sh[:, u % 2].rearrange("p (h k) -> p h k", k=S), sc,
                                        mx[:, u % 2].unsqueeze(2).broadcast_to((P, HH, S)), ALU.subtract
                                        ).then_inc(shifted, 1)

            def divide(g, m):
                dve.wait_ge(den_ready, nth(g, 2, m))
                nc.vector.reciprocal(inv[:, m], OB[m]).then_inc(inverted, 1)
                dve.wait_ge(inverted, nth(g, 2, m))
                nc.vector.tensor_tensor(on[:, m].rearrange("p t r n -> p (t r n)"), osb[:, m], inv[:, m], ALU.mult
                                        ).then_inc(divided, 1)

            def residual(g, s, m):
                dve.wait_ge(proj_ready, nth(g, 2, m))
                pr = PROJ[:, 256 * m:256 * m + 256].rearrange("p (t d) -> p t d", d=D)
                if not post_norm:
                    xs = tiles_of(x_res, g, 2 * m, 2)
                    nc.vector.tensor_tensor(xs, pr, xs, ALU.add).then_inc(resid_done, 1)
                    return
                nc.vector.tensor_tensor(t1[:, m], pr, xn[:, s, 2 * m:2 * m + 2, :], ALU.add).then_inc(resid_done, 1)
                dve.wait_ge(resid_done, nth(g, 2, m))
                for t in (0, 1):
                    last = nc.vector.bn_stats(st2[:, m, t, :], t1[:, m, t, :])
                last.then_inc(stats2_done, 1)
                dve.wait_ge(stats2_done, g * 2 + (m + 1))
                dve.wait_ge(std2, g * 2)
                dve.sem_inc(passed, 1)
                for t in (0, 1):
                    last = nc.vector.bn_aggr(mv2[:, m, t, :], st2[:, m, t, :])
                last.then_inc(moments2, 1)

            def normalise(g, m):
                if not post_norm:
                    return
                dve.wait_ge(std2, nth(g, 2, m))
                nc.vector.tensor_scalar(se2[:, m], sd2[:, m], EPS, None, ALU.add).then_inc(std2_eps, 1)
                dve.wait_ge(std2_eps, nth(g, 2, m))
                nc.vector.reciprocal(rs2[:, m], se2[:, m]).then_inc(rstd2, 1)
                dve.wait_ge(rstd2, nth(g, 2, m))
                dve.wait_ge(zg_done, g * 2)
                for t in (0, 1):
                    last = nc.vector.tensor_scalar(z2[:, m, t, :], t1[:, m, t, :], mv2[:, m, t, 0:1],
                                                   rs2[:, m, t:t + 1], ALU.subtract, ALU.mult)
                last.then_inc(z_done, 1)

            def prep(g, s):
                norm_stats(g, s)
                key_mask_of_next(g, s)
                norm_apply(g, s)
                copy_q(g, s)

            def step(g, s, more):
                for u in range(UNITS):
                    shift(g, u)
                    if more and u == 0:
                        norm_stats(g + 1, 1 - s)
                        key_mask_of_next(g + 1, 1 - s)
                    if more and u == 1:
                        norm_apply(g + 1, 1 - s)
                    if more and u == 5:
                        copy_q(g + 1, 1 - s)
                    if u == 6:
                        divide(g, 0)
                    if u == 7:
                        residual(g, s, 0)
                divide(g, 1)
                normalise(g, 0)
                residual(g, s, 1)
                normalise(g, 1)

            nc.vector.memset(vblk[:, :, :, :, :], 0.0).then_inc(vblk_set, 1)
            dve.wait_ge(vblk_set, 1)
            nc.vector.memset(vblk[0:64, :, :, :, 8:9], 1.0).then_inc(vblk_set, 1)
            nc.vector.memset(vblk[64:128, :, :, :, 24:25], 1.0).then_inc(vblk_set, 1)
            two_halves(dve, NG, prep, step)

        @block.tensor
        def _(pe):
            def free_prep(g, k):
                if k == 0:
                    pe.wait_ge(v_copied, g * 2)

            def make_xT(g, s):
                free_prep(g, 0)
                pe.wait_ge(xn_ready, nth(g))
                for t in range(TILES):
                    last = nc.tensor.transpose(PREP[:, t * P:(t + 1) * P], xn[:, s, t, :], ident)
                last.then_inc(xT_ready, 1)

            def make_cT(g, s):
                if cross:
                    pe.wait_ge(xT_copied, nth(g))
                    pe.wait_ge(c_loaded[s], loaded(g, s))
                    for t in range(TILES):
                        last = nc.tensor.transpose(PREP[:, t * P:(t + 1) * P], cin[:, s, t, :], ident)
                    last.then_inc(cT_ready, 1)

            def make_k(g, s):
                if cross:
                    pe.wait_ge(cT_copied, nth(g))
                else:
                    pe.wait_ge(xT_copied, nth(g))
                nc.tensor.matmul(PREP, wk, ctxT[:, :], start=True, stop=True).then_inc(k_ready, 1)

            def make_q(g, s):
                pe.wait_ge(k_copied, nth(g))
                nc.tensor.matmul(PREP, wq, srcT[:, :], start=True, stop=True).then_inc(q_ready, 1)

            def make_v(g, s, h):
                if h == 0:
                    pe.wait_ge(q_copied, nth(g))
                else:
                    pe.wait_ge(v_copied, nth(g, 2, 0))
                for b in range(4):
                    for j in (0, 1):
                        last = nc.tensor.matmul(PREP[64 * j:64 * j + 64, b * D:(b + 1) * D],
                                                ctxT[:, (4 * h + b) * S:(4 * h + b + 1) * S], wv, start=True, stop=True)
                last.then_inc(v_ready, 1)

            def scores(g, s, u):
                t, r = u // 2, u % 2
                rows = slice(64 * r, 64 * r + 64)
                if u == 0:
                    pe.wait_ge(kblk_ready, g + 1)
                    pe.wait_ge(q_copied, g + 1)
                    pe.sem_inc(passed, 1)
                for bb in (0, 1):
                    b = 2 * t + bb
                    out = SB[u % 2][64 * bb:64 * bb + 64, :]
                    last = nc.tensor.matmul(out, qT[rows, s, b * S:(b + 1) * S],
                                            kblk[rows, s, b].rearrange("p h k -> p (h k)"), start=True, stop=a == 0)
                    if a == 1:
                        last = nc.tensor.matmul(out, C["identb"][rows, rows],
                                                C["qmask"][rows, :].unsqueeze(1).broadcast_to((64, HH, S)),
                                                start=False, stop=True)
                    if a == 2:
                        last = nc.tensor.matmul(out, C["oneb"][rows, :],
                                                kmb[rows, s, b, :].unsqueeze(1).broadcast_to((64, HH, S)),
                                                start=False, stop=True)
                last.then_inc(s_ready, 1)

            def transposes(g, u):
                pe.wait_ge(shifted, nth(g, UNITS, u))
                for c in range(4):
                    last = nc.tensor.transpose(TB[u % 2][:, c * P:(c + 1) * P], sh[:, u % 2, c * P:(c + 1) * P], ident)
                last.then_inc(t_ready, 1)

            def weigh(g, s, u):
                t, r = u // 2, u % 2
                m = t // 2
                pe.wait_ge(e_ready, nth(g, UNITS, u))
                if u == 0:
                    pe.wait_ge(v_copied, nth(g, 2, 1))
                if u % 4 == 0:
                    pe.wait_ge(divided, g * 2)
                for bb in (0, 1):
                    col = (t % 2) * 2 * P + r * P + bb * S
                    for c in range(4):
                        last = nc.tensor.matmul(OB[m][32 * c:32 * c + 32, col:col + S],
                                                vblk[:, s, 2 * t + bb, 4 * r + c, :],
                                                ex[:, u % 2, c, bb * S:(bb + 1) * S], start=True, stop=True)
                if u % 4 == 3:
                    last.then_inc(o_ready, 1)

            def denominators(g, m):
                pe.wait_ge(o_copied, nth(g, 2, m))
                nc.tensor.matmul(OB[m], sel, osb[:, m], start=True, stop=True).then_inc(den_ready, 1)

            def project(g, m):
                pe.wait_ge(divided, nth(g, 2, m))
                if m == 0:
                    pe.wait_ge(resid_done, g * 2)
                else:
                    pe.wait_ge(resid_done, nth(g, 2, 0))
                for t in (0, 1):
                    for r in (0, 1):
                        last = nc.tensor.matmul(PROJ[:, (2 * m + t) * D:(2 * m + t + 1) * D], on[:, m, t, r, :],
                                                wo[:, r, :], start=(r == 0), stop=(r == 1))
                last.then_inc(proj_ready, 1)

            def prep(g, s):
                make_xT(g, s)
                make_cT(g, s)
                make_k(g, s)
                make_q(g, s)
                make_v(g, s, 0)
                make_v(g, s, 1)

            def step(g, s, more):
                for v in range(UNITS + 2):
                    if v < UNITS:
                        scores(g, s, v)
                    if 1 <= v <= UNITS:
                        transposes(g, v - 1)
                    if v >= 2:
                        weigh(g, s, v - 2)
                    if more and v == 2:
                        make_xT(g + 1, 1 - s)
                    if more and v == 3:
                        make_cT(g + 1, 1 - s)
                    if more and v == 4:
                        make_k(g + 1, 1 - s)
                    if more and v == 5:
                        make_q(g + 1, 1 - s)
                    if v == 6:
                        denominators(g, 0)
                        if more:
                            make_v(g + 1, 1 - s, 0)
                    if v == 7:
                        project(g, 0)
                    if more and v == 8:
                        make_v(g + 1, 1 - s, 1)
                denominators(g, 1)
                project(g, 1)

            two_halves(pe, NG, prep, step)


def two_halves(eng, n, prep, step):
    prep(0, 0)
    step(0, 0, True)
    with eng.Fori(0, n // 2 - 1) as i:
        for s in (1, 0):
            step(i * 2 + (2 - s), s, True)
    step(n - 1, 1, False)


def nth(g, n=1, k=0):
    return g * n + (k + 1)


def tiles_of(t, g, k=0, n=TILES):
    return t[:, bass.ds(g * TILES + k, n), :]


def across(row, n):
    return row.unsqueeze(1).broadcast_to((P, n, D))


def relu_phase(nc, ps, C, x_res, y_res):
    F = 4
    with ExitStack() as ctx:
        def sb(name, shape, dt=F32):
            return ctx.enter_context(nc.sbuf_tensor("ff_" + name, shape, dt))

        sem = ctx.enter_context(Signals(nc, "ff_"))

        w1 = C["ff1"].rearrange("p (c n) -> p c n", c=F)
        b1 = C["ff1b"]
        w2 = C["ff2"].rearrange("p (c n) -> p c n", c=F)
        yn = sb("yn", [P, 2, TILES, D])
        yT = sb("yT", [P, 2, TOK])
        hT = sb("hT", [P, F, TOK])
        yb = sb("yb", [P, TILES, D])
        t1 = sb("t1", [P, TILES, D])
        st = sb("st", [P, TILES, 6])
        mv = sb("mv", [P, TILES, 2])
        sd = sb("sd", [P, TILES])
        se = sb("se", [P, TILES])
        rs = sb("rs", [P, TILES])
        z = sb("z", [P, TILES, D])
        zg = sb("zg", [P, TILES, D])
        zb = sb("zb", [P, TILES, D])
        HB = [ps[:, i, :] for i in range(4)]
        OUTB = [ps[:, i, :] for i in (4, 5)]
        XB = [ps[:, i, :] for i in (6, 7)]

        yn_ready = sem("yn_ready")
        yb_ready = sem("yb_ready")
        yT_ready = sem("yT_ready")
        yT_copied = sem("yT_copied")
        h_ready = sem("h_ready")
        relu_done = sem("relu_done")
        out_ready = sem("out_ready")
        summed = sem("summed")
        stats_done = sem("stats_done")
        moments = sem("moments")
        std_done = sem("std_done")
        std_eps = sem("std_eps")
        rstd_done = sem("rstd_done")
        z_done = sem("z_done")
        zg_done = sem("zg_done")
        zb_done = sem("zb_done")
        x_done = sem("x_done")
        passed = sem("passed")
        block = ctx.enter_context(nc.Block())

        @block.gpsimd
        def _(pool):
            def prep(g, s):
                nc.gpsimd.tensor_copy(yn[:, s], tiles_of(y_res, g)).then_inc(yn_ready, 1)

            def step(g, s, more):
                pool.wait_ge(summed, g)
                pool.sem_inc(passed, 1)
                nc.gpsimd.tensor_tensor(yb[:, :, :], tiles_of(y_res, g), across(C["ff2b"], TILES), ALU.add
                                        ).then_inc(yb_ready, 1)
                if more:
                    pool.wait_ge(yT_ready, g)
                    prep(g + 1, 1 - s)
                pool.wait_ge(moments, nth(g))
                nc.gpsimd.tensor_tensor(sd[:, :], mv[:, :, 1], C["half"][:, 0:TILES], ALU.pow).then_inc(std_done, 1)
                pool.wait_ge(z_done, nth(g))
                nc.gpsimd.tensor_tensor(zg[:, :, :], z[:, :, :], across(C["g3"], TILES), ALU.mult).then_inc(zg_done, 1)
                pool.wait_ge(zg_done, nth(g))
                pool.wait_ge(x_done, g)
                nc.gpsimd.tensor_tensor(zb[:, :, :], zg[:, :, :], across(C["b3"], TILES), ALU.add).then_inc(zb_done, 1)

            two_halves(pool, NG, prep, step)

        @block.scalar
        def _(act):
            def prep(g, s):
                act.wait_ge(yT_ready, nth(g))
                nc.scalar.copy(yT[:, s], XB[s]).then_inc(yT_copied, 1)

            def step(g, s, more):
                for c in range(F):
                    act.wait_ge(h_ready, nth(g, F, c))
                    if c == 0:
                        act.wait_ge(out_ready, g)
                    nc.scalar.activation(hT[:, c], HB[c], ACT.Relu, bias=b1[:, c:c + 1]).then_inc(relu_done, 1)
                if more:
                    prep(g + 1, 1 - s)

            two_halves(act, NG, prep, step)

        @block.tensor
        def _(pe):
            def prep(g, s):
                pe.wait_ge(yn_ready, nth(g))
                for t in range(TILES):
                    last = nc.tensor.transpose(XB[s][:, t * P:(t + 1) * P], yn[:, s, t, :], C["ident"])
                last.then_inc(yT_ready, 1)

            def step(g, s, more):
                pe.wait_ge(yT_copied, nth(g))
                pe.wait_ge(relu_done, g * F)
                for c in range(F):
                    nc.tensor.matmul(HB[c], w1[:, c], yT[:, s], start=True, stop=True).then_inc(h_ready, 1)
                if more:
                    prep(g + 1, 1 - s)
                pe.wait_ge(relu_done, nth(g, F, F - 1))
                for t in range(TILES):
                    for c in range(F):
                        last = nc.tensor.matmul(OUTB[s][:, t * D:(t + 1) * D], hT[:, c, t * P:(t + 1) * P], w2[:, c],
                                                start=(c == 0), stop=(c == F - 1))
                last.then_inc(out_ready, 1)

            two_halves(pe, NG, prep, step)

        @block.vector
        def _(dve):
            def step(g, s, more):
                dve.wait_ge(out_ready, nth(g))
                dve.wait_ge(yb_ready, nth(g))
                nc.vector.tensor_tensor(t1[:, :, :], OUTB[s].rearrange("p (t d) -> p t d", d=D), yb[:, :, :], ALU.add
                                        ).then_inc(summed, 1)
                dve.wait_ge(summed, nth(g))
                for t in range(TILES):
                    last = nc.vector.bn_stats(st[:, t, :], t1[:, t, :])
                last.then_inc(stats_done, 1)
                dve.wait_ge(stats_done, g + 1)
                dve.sem_inc(passed, 1)
                for t in range(TILES):
                    last = nc.vector.bn_aggr(mv[:, t, :], st[:, t, :])
                last.then_inc(moments, 1)
                dve.wait_ge(std_done, nth(g))
                nc.vector.tensor_scalar(se[:, :], sd[:, :], EPS, None, ALU.add).then_inc(std_eps, 1)
                dve.wait_ge(std_eps, nth(g))
                nc.vector.reciprocal(rs[:, :], se[:, :]).then_inc(rstd_done, 1)
                dve.wait_ge(rstd_done, nth(g))
                for t in range(TILES):
                    last = nc.vector.tensor_scalar(z[:, t, :], t1[:, t, :], mv[:, t, 0:1], rs[:, t:t + 1],
                                                   ALU.subtract, ALU.mult)
                last.then_inc(z_done, 1)
                dve.wait_ge(zb_done, nth(g))
                xs = tiles_of(x_res, g)
                nc.vector.tensor_tensor(xs, zb[:, :, :], xs, ALU.add).then_inc(x_done, 1)

            two_halves(dve, NG, lambda g, s: None, step)


def experts_phase(nc, ps, C, x_res, gate_in, up_in, down_in, out):
    E, SH = 16, 2
    K = E + SH
    with ExitStack() as ctx:
        def sb(name, shape, dt=F32):
            return ctx.enter_context(nc.sbuf_tensor("moe_" + name, shape, dt))

        sem = ctx.enter_context(Signals(nc, "moe_"))

        gate = sb("gate", [P, K, D])
        up = sb("up", [P, K, D])
        down = sb("down", [P, K, D])
        xn = sb("xn", [P, 2, TILES, D])
        xnT = sb("xnT", [P, 2, TOK])
        stats = sb("stats", [P, TILES, 6])
        mv = sb("mv", [P, TILES, 2])
        veps = sb("veps", [P, TILES])
        rstd = sb("rstd", [P, TILES])
        sg = sb("sg", [P, 2, TOK])
        act_ = sb("act", [P, 2, TOK])
        acc = sb("acc", [P, 2, TILES, D])
        TE = TILES * E
        ex = sb("ex", [P, TE])
        one_ex = sb("one_ex", [P, TE])
        score = sb("score", [P, TE])
        biased = sb("biased", [P, TE])
        hi2 = sb("hi2", [P, TE // 2])
        lo2 = sb("lo2", [P, TE // 2])
        top = sb("top", [P, TILES * 4])
        mid = sb("mid", [P, TILES * 4])
        low = sb("low", [P, TILES * 4])
        sec = sb("sec", [P, TILES * 4])
        gsc = sb("gsc", [P, TILES * 4])
        ggt = sb("ggt", [P, TILES * 4 * 4])
        geq = sb("geq", [P, TILES * 4 * 4])
        gtie = sb("gtie", [P, TILES * 4 * 4])
        gall = sb("gall", [P, TILES * 4 * 4])
        grank = sb("grank", [P, TILES * 4])
        gin = sb("gin", [P, TILES * 4])
        gout = sb("gout", [P, TILES * 4])
        kept = sb("kept", [P, TE])
        masked = sb("masked", [P, TE])
        egt = sb("egt", [P, TILES, E, E])
        eeq = sb("eeq", [P, TILES, E, E])
        rank = sb("rank", [P, TE])
        w = sb("w", [P, TE])
        wsum = sb("wsum", [P, TILES])
        wsume = sb("wsume", [P, TILES])
        winv = sb("winv", [P, TILES])
        comb = sb("comb", [P, 2, TILES, E])

        GB_ = [ps[:, i, :] for i in (0, 1)]
        UB = [ps[:, i, :] for i in (2, 3)]
        YB = [ps[:, i, :] for i in (4, 5)]
        XB = ps[:, 6, :]
        RB = ps[:, 7, 0:TE]
        CH = 3
        w_loaded = [sem(f"w_loaded{i}") for i in range(K // CH)]
        stats_done = sem("stats_done")
        moments = sem("moments")
        var_eps = sem("var_eps")
        rstd_done = sem("rstd_done")
        xn_ready = sem("xn_ready")
        xT_ready = sem("xT_ready")
        xT_copied = sem("xT_copied")
        logits_ready = sem("logits_ready")
        exp_done = sem("exp_done")
        NR = 29
        routing = sem("routing")
        comb_ready = sem("comb_ready")
        g_ready = sem("g_ready")
        u_ready = sem("u_ready")
        silu_done = sem("silu_done")
        act_ready = sem("act_ready")
        y_ready = sem("y_ready")
        acc_done = sem("acc_done")
        stored = [sem(f"stored{s}_") for s in (0, 1)]
        passed = sem("passed")
        block = ctx.enter_context(nc.Block())

        @block.sync
        def _(sp):
            for i in range(K // CH):
                part = slice(i * CH, (i + 1) * CH)
                sp.dma_start(gate[:, part, :], gate_in[:, part, :]).then_inc(w_loaded[i], 16)
                sp.dma_start(up[:, part, :], up_in[:, part, :]).then_inc(w_loaded[i], 16)
                sp.dma_start(down[:, part, :], down_in[:, part, :]).then_inc(w_loaded[i], 16)
            for s in (0, 1):
                sp.sem_inc(stored[s], 1)
            with sp.Fori(0, NG // 2) as i:
                for s in (0, 1):
                    g = i * 2 + s
                    sp.wait_ge(acc_done, nth(g, K - 1, K - 2))
                    sp.dma_start(out[bass.ds(g * TOK, TOK), :].rearrange("(t p) d -> p t d", p=P), acc[:, s]
                                 ).then_inc(stored[s], 16)
            for s in (0, 1):
                sp.wait_ge(stored[s], 16 * (NG // 2) + 1)

        @block.gpsimd
        def _(pool):
            def prep(g, s):
                pool.wait_ge(var_eps, nth(g))
                nc.gpsimd.tensor_tensor(rstd[:, :], veps[:, :], C["mhalf"][:, 0:TILES], ALU.pow).then_inc(rstd_done, 1)

            two_halves(pool, NG, prep, lambda g, s, more: prep(g + 1, 1 - s) if more else None)

        @block.scalar
        def _(act):
            def copy_xT(g, s):
                act.wait_ge(xT_ready, nth(g))
                nc.scalar.copy(xnT[:, s], XB).then_inc(xT_copied, 1)

            def route_exp(g, s):
                act.wait_ge(logits_ready, nth(g))
                nc.scalar.activation(ex[:, :], RB, ACT.Exp, scale=-1.0).then_inc(exp_done, 1)

            def prep(g, s):
                copy_xT(g, s)
                route_exp(g, s)

            def step(g, s, more):
                for k in range(K):
                    act.wait_ge(g_ready, nth(g, K, k))
                    nc.scalar.activation(sg[:, k % 2], GB_[k % 2], ACT.Silu).then_inc(silu_done, 1)
                    if more and k == 6:
                        copy_xT(g + 1, 1 - s)
                    if more and k == 8:
                        route_exp(g + 1, 1 - s)

            two_halves(act, NG, prep, step)

        @block.tensor
        def _(pe):
            def make_xT(g, s):
                pe.wait_ge(xn_ready, nth(g))
                for t in range(TILES):
                    last = nc.tensor.transpose(XB[:, t * P:(t + 1) * P], xn[:, s, t, :], C["ident"])
                last.then_inc(xT_ready, 1)

            def logits(g, s):
                pe.wait_ge(xT_copied, nth(g))
                for t in range(TILES):
                    last = nc.tensor.matmul(RB[:, t * E:(t + 1) * E], xnT[:, s, t * P:(t + 1) * P], C["router"],
                                            start=True, stop=True)
                last.then_inc(logits_ready, 1)

            def prep(g, s):
                make_xT(g, s)
                logits(g, s)

            def down_proj(g, k):
                pe.wait_ge(act_ready, nth(g, K, k))
                if k >= SH:
                    if k >= SH + 1:
                        pe.wait_ge(acc_done, nth(g, K - 1, k - SH - 1))
                    for t in range(TILES):
                        last = nc.tensor.matmul(YB[k % 2][:, t * D:(t + 1) * D], act_[:, k % 2, t * P:(t + 1) * P],
                                                down[:, k, :], start=True, stop=True)
                    last.then_inc(y_ready, 1)
                elif k == SH - 1:
                    pe.wait_ge(acc_done, g * (K - 1))
                    for t in range(TILES):
                        for j in range(SH):
                            last = nc.tensor.matmul(YB[1][:, t * D:(t + 1) * D], act_[:, j, t * P:(t + 1) * P],
                                                    down[:, j, :], start=(j == 0), stop=(j == SH - 1))
                    last.then_inc(y_ready, 1)

            def step(g, s, more):
                pe.wait_ge(xT_copied, nth(g))
                for k in range(K + 1):
                    if k < K:
                        if isinstance(g, int) and g == 0 or k % CH == 0:
                            pe.wait_ge(w_loaded[k // CH], 48)
                        if k >= 2:
                            pe.wait_ge(act_ready, nth(g, K, k - 2))
                        else:
                            pe.wait_ge(act_ready, g * K)
                        nc.tensor.matmul(GB_[k % 2], gate[:, k], xnT[:, s], start=True, stop=True).then_inc(g_ready, 1)
                        nc.tensor.matmul(UB[k % 2], up[:, k], xnT[:, s], start=True, stop=True).then_inc(u_ready, 1)
                    if k >= 1:
                        down_proj(g, k - 1)
                    if more and k == 6:
                        make_xT(g + 1, 1 - s)
                    if more and k == 8:
                        logits(g + 1, 1 - s)

            two_halves(pe, NG, prep, step)

        @block.vector
        def _(dve):
            V = nc.vector

            def norm_stats(g, s):
                for t in range(TILES):
                    last = V.bn_stats(stats[:, t, :], tiles_of(x_res, g, t, 1))
                last.then_inc(stats_done, 1)
                dve.wait_ge(stats_done, g + 1)
                dve.sem_inc(passed, 1)
                for t in range(TILES):
                    last = V.bn_aggr(mv[:, t, :], stats[:, t, :])
                last.then_inc(moments, 1)
                dve.wait_ge(moments, nth(g))
                V.tensor_scalar(veps[:, :], mv[:, :, 1], EPS, None, ALU.add).then_inc(var_eps, 1)

            def norm_apply(g, s):
                dve.wait_ge(rstd_done, nth(g))
                for t in range(TILES):
                    last = V.tensor_scalar(xn[:, s, t:t + 1, :], tiles_of(x_res, g, t, 1), mv[:, t, 0:1],
                                           rstd[:, t:t + 1], ALU.subtract, ALU.mult)
                last.then_inc(xn_ready, 1)

            def g4(t):
                return t[:, :].rearrange("p (t g) -> p t g", t=TILES)

            def groups_of(t):
                return t[:, :].rearrange("p (n c) -> p n c", c=4)

            def pairs(t, k):
                return t[:, :].rearrange("p (n c) -> p n c", c=2)[:, :, k]

            def route(g, s, parts):
                TG = TILES * 4

                def ge4(t):
                    return t[:, :].rearrange("p (n g j) -> p n g j", g=4, j=4)

                inner = lambda t: g4(t).unsqueeze(3).broadcast_to((P, TILES, 4, 4))
                other = lambda t: g4(t).unsqueeze(2).broadcast_to((P, TILES, 4, 4))
                t16 = lambda t: t[:, :].rearrange("p (t e) -> p t e", e=E)
                einner = lambda t: t16(t).unsqueeze(3).broadcast_to((P, TILES, E, E))
                eother = lambda t: t16(t).unsqueeze(2).broadcast_to((P, TILES, E, E))
                spread = lambda t: t[:, :].unsqueeze(2).broadcast_to((P, TG, 4))
                glow = C["glowmask"].rearrange("p (g j) -> p g j", j=4).unsqueeze(1).broadcast_to((P, TILES, 4, 4))
                elow = C["lowmask"].unsqueeze(1).broadcast_to((P, TILES, E * E))
                flat = lambda t: t[:, :, :, :].rearrange("p t e j -> p t (e j)")
                def before(n):
                    return nth(g, NR, n - 1)

                if 0 in parts:
                    dve.wait_ge(exp_done, nth(g))
                    V.tensor_scalar(one_ex[:, :], ex[:, :], 1.0, None, ALU.add).then_inc(routing, 1)
                    dve.wait_ge(routing, before(1))
                    V.reciprocal(score[:, :], one_ex[:, :]).then_inc(routing, 1)
                    dve.wait_ge(routing, before(2))
                    V.tensor_tensor(biased[:, :], score[:, :], C["rbias"], ALU.add).then_inc(routing, 1)
                    dve.wait_ge(routing, before(3))
                    V.tensor_tensor(hi2[:, :], pairs(biased, 0), pairs(biased, 1), ALU.max).then_inc(routing, 1)
                if 1 in parts:
                    dve.wait_ge(routing, before(4))
                    V.tensor_tensor(lo2[:, :], pairs(biased, 0), pairs(biased, 1), ALU.min).then_inc(routing, 1)
                    dve.wait_ge(routing, before(5))
                    V.tensor_tensor(top[:, :], pairs(hi2, 0), pairs(hi2, 1), ALU.max).then_inc(routing, 1)
                    dve.wait_ge(routing, before(6))
                    V.tensor_tensor(mid[:, :], pairs(hi2, 0), pairs(hi2, 1), ALU.min).then_inc(routing, 1)
                    dve.wait_ge(routing, before(7))
                    V.tensor_tensor(low[:, :], pairs(lo2, 0), pairs(lo2, 1), ALU.max).then_inc(routing, 1)
                if 2 in parts:
                    dve.wait_ge(routing, before(8))
                    V.tensor_tensor(sec[:, :], mid[:, :], low[:, :], ALU.max).then_inc(routing, 1)
                    dve.wait_ge(routing, before(9))
                    V.tensor_tensor(gsc[:, :], top[:, :], sec[:, :], ALU.add).then_inc(routing, 1)
                    dve.wait_ge(routing, before(10))
                    V.tensor_tensor(ge4(ggt), other(gsc), inner(gsc), ALU.is_gt).then_inc(routing, 1)
                    dve.wait_ge(routing, before(11))
                    V.tensor_tensor(ge4(geq), other(gsc), inner(gsc), ALU.is_equal).then_inc(routing, 1)
                if 3 in parts:
                    dve.wait_ge(routing, before(12))
                    V.tensor_tensor(ge4(gtie), ge4(geq), glow, ALU.mult).then_inc(routing, 1)
                    dve.wait_ge(routing, before(13))
                    V.tensor_tensor(gall[:, :], ggt[:, :], gtie[:, :], ALU.add).then_inc(routing, 1)
                    dve.wait_ge(routing, before(14))
                    V.tensor_reduce(grank[:, :], groups_of(gall), AX.X, ALU.add).then_inc(routing, 1)
                    dve.wait_ge(routing, before(15))
                    V.tensor_scalar(gin[:, :], grank[:, :], 2.0, None, ALU.is_lt).then_inc(routing, 1)
                if 4 in parts:
                    dve.wait_ge(routing, before(16))
                    V.tensor_scalar(gout[:, :], gin[:, :], -1.0, None, ALU.add).then_inc(routing, 1)
                    dve.wait_ge(routing, before(17))
                    V.tensor_tensor(groups_of(kept), groups_of(biased), spread(gin), ALU.mult).then_inc(routing, 1)
                    dve.wait_ge(routing, before(18))
                    V.tensor_tensor(groups_of(masked), groups_of(kept), spread(gout), ALU.add).then_inc(routing, 1)
                    dve.wait_ge(routing, before(19))
                    V.tensor_tensor(egt[:, :, :, :], eother(masked), einner(masked), ALU.is_gt).then_inc(routing, 1)
                if 5 in parts:
                    dve.wait_ge(routing, before(20))
                    V.tensor_tensor(eeq[:, :, :, :], eother(masked), einner(masked), ALU.is_equal).then_inc(routing, 1)
                    dve.wait_ge(routing, before(21))
                    V.tensor_tensor(flat(eeq), flat(eeq), elow, ALU.mult).then_inc(routing, 1)
                    dve.wait_ge(routing, before(22))
                    V.tensor_tensor(flat(egt), flat(egt), flat(eeq), ALU.add).then_inc(routing, 1)
                    dve.wait_ge(routing, before(23))
                    V.tensor_reduce(rank[:, :], egt[:, :, :, :].rearrange("p t e j -> p (t e) j"), AX.X,
                                    ALU.add).then_inc(routing, 1)
                if 6 in parts:
                    dve.wait_ge(routing, before(24))
                    V.scalar_tensor_tensor(w[:, :], rank[:, :], 4.0, score[:, :], ALU.is_lt,
                                           ALU.mult).then_inc(routing, 1)
                    dve.wait_ge(routing, before(25))
                    V.tensor_reduce(wsum[:, :], t16(w), AX.X, ALU.add).then_inc(routing, 1)
                    dve.wait_ge(routing, before(26))
                    V.tensor_scalar(wsume[:, :], wsum[:, :], 1e-20, None, ALU.add).then_inc(routing, 1)
                    dve.wait_ge(routing, before(27))
                    V.reciprocal(winv[:, :], wsume[:, :]).then_inc(routing, 1)
                if 7 in parts:
                    dve.wait_ge(routing, before(28))
                    V.scalar_tensor_tensor(comb[:, s], t16(w), 2.5, winv[:, :].unsqueeze(2).broadcast_to((P, TILES, E)), ALU.mult,
                                           ALU.mult).then_inc(routing, 1)

            def prep(g, s):
                norm_stats(g, s)
                norm_apply(g, s)
                route(g, s, range(8))

            def product(g, k):
                dve.wait_ge(u_ready, nth(g, K, k))
                dve.wait_ge(silu_done, nth(g, K, k))
                if k >= SH + 2:
                    dve.wait_ge(y_ready, nth(g, K - 1, k - SH - 1))
                elif k >= 2:
                    dve.wait_ge(y_ready, nth(g, K - 1, 0))
                else:
                    dve.wait_ge(y_ready, g * (K - 1))
                V.tensor_tensor(act_[:, k % 2], UB[k % 2], sg[:, k % 2], ALU.mult).then_inc(act_ready, 1)

            def accumulate(g, s, k):
                if k < SH - 1:
                    return
                n = k - SH + 1
                dve.wait_ge(y_ready, nth(g, K - 1, n))
                y = YB[k % 2].rearrange("p (t d) -> p t d", d=D)
                if n == 0:
                    dve.wait_ge(stored[s], g * 8 + (1 - 8 * s))
                    V.tensor_tensor(acc[:, s], y, tiles_of(x_res, g), ALU.add).then_inc(acc_done, 1)
                    return
                dve.wait_ge(acc_done, nth(g, K - 1, n - 1))
                if n == 1:
                    dve.wait_ge(routing, nth(g, NR, NR - 1))
                for t in range(TILES):
                    last = V.scalar_tensor_tensor(acc[:, s, t], y[:, t], comb[:, s, t, k - SH:k - SH + 1], acc[:, s, t],
                                                  ALU.mult, ALU.add)
                last.then_inc(acc_done, 1)

            def step(g, s, more):
                for k in range(K + 1):
                    if k < K:
                        product(g, k)
                    if k >= 1:
                        accumulate(g, s, k - 1)
                    if more and k == 3:
                        norm_stats(g + 1, 1 - s)
                    if more and k == 4:
                        norm_apply(g + 1, 1 - s)
                    if more and k >= 10:
                        route(g + 1, 1 - s, [k - 10])

            two_halves(dve, NG, prep, step)


def choice_phase(nc, ps, C, x_res, wqkv_in, woe_in):
    E, KC = 8, 8
    GT = 8
    NB = 2 * GT
    N = BATCH // NB
    ASCALE = float(D) ** -0.5

    with ExitStack() as ctx:
        def sb(name, shape, dt=F32):
            return ctx.enter_context(nc.sbuf_tensor("ch_" + name, shape, dt))

        sem = ctx.enter_context(Signals(nc, "ch_"))

        wqkv = sb("wqkv", [P, E, 3 * D])
        woe = sb("woe", [P, E, D])
        xn = sb("xn", [P, GT, D])
        stats = sb("stats", [P, GT, 6])
        mv = sb("mv", [P, GT, 2])
        veps = sb("veps", [P, GT])
        rstd = sb("rstd", [P, GT])
        xnT = sb("xnT", [P, GT * P])
        ex = sb("ex", [P, 4 * S])
        ex1 = sb("ex1", [P, 4 * S])
        gatev = sb("gatev", [P, 4 * S])
        m8 = sb("m8", [P, 4, 8])
        gt = sb("gt", [P, 4 * S])
        eq = sb("eq", [P, 4 * S])
        ngt = sb("ngt", [P, 4])
        ceq = sb("ceq", [P, 4 * S])
        tot = sb("tot", [P, 4 * S])
        tied = sb("tied", [P, 4 * S])
        chosen = sb("chosen", [P, 4 * S])
        count = sb("count", [P, 4 * S])
        slot = sb("slot", [P, 4 * S])
        slotT = sb("slotT", [P, GT, E])
        gateT = sb("gateT", [P, GT, E])
        pick = sb("pick", [P, GT, 2, E * KC])
        pickw = sb("pickw", [P, GT, 2, E * KC])
        trigT = sb("trigT", [P, E, NB, KC])
        xg = sb("xg", [P, 2, E, NB, KC])
        trig = sb("trig", [P, 2, E, P])
        pickT = sb("pickT", [P, 2, GT, P])
        qkv = sb("qkv", [P, E, 3, D])
        rot1 = sb("rot1", [P, 2, 4, 2, 64])
        rot2 = sb("rot2", [P, 2, 4, 2, 64])
        qT = sb("qT", [P, 2, 4 * P])
        kT = sb("kT", [P, 2, 4 * P])
        sm = sb("sm", [P, 2, 4, P])
        mx = sb("mx", [P, 2, 4])
        dif = sb("dif", [P, 2, 4, P])
        pe_ = sb("pe", [P, 2, 4, P])
        sums = sb("sums", [P, 2, 4])
        inv = sb("inv", [P, 2, 4])
        prob = sb("prob", [P, 2, 4, P])
        probT = sb("probT", [P, 2, 4, P])
        avT = sb("avT", [P, 2, 4, P])
        xpT = sb("xpT", [P, NB, E, KC])
        xp = sb("xp", [P, GT, D])

        def prep_bank(n):
            return ps[:, n % 2, :]

        def bank(n):
            return ps[:, 2 + n % 6, :]

        w_loaded = sem("w_loaded")
        pick_set = sem("pick_set")
        stats_done = sem("stats_done")
        moments = sem("moments")
        var_eps = sem("var_eps")
        rstd_done = sem("rstd_done")
        xn_ready = sem("xn_ready")
        NP = 13
        prep_ready = sem("prep_ready")
        prep_copied = sem("prep_copied")
        NC = 12
        choosing = sem("choosing")
        pick_ready = sem("pick_ready")
        pickw_ready = sem("pickw_ready")
        qkv_ready = sem("qkv_ready")
        qkv_copied = sem("qkv_copied")
        rotated1 = sem("rotated1")
        rotated2 = sem("rotated2")
        rotated = sem("rotated")
        qkT_ready = sem("qkT_ready")
        qkT_copied = sem("qkT_copied")
        s_ready = sem("s_ready")
        s_masked = sem("s_masked")
        max_done = sem("max_done")
        shifted = sem("shifted")
        e_ready = sem("e_ready")
        sum_done = sem("sum_done")
        inv_done = sem("inv_done")
        prob_ready = sem("prob_ready")
        probT_ready = sem("probT_ready")
        probT_copied = sem("probT_copied")
        av_ready = sem("av_ready")
        av_copied = sem("av_copied")
        xpT_ready = sem("xpT_ready")
        xpT_copied = sem("xpT_copied")
        xp_ready = sem("xp_ready")
        xp_copied = sem("xp_copied")
        out_ready = sem("out_ready")
        out_added = sem("out_added")

        def tiles(g, k=0, n=GT):
            return x_res[:, bass.ds(g * GT + k, n), :]

        passed = sem("passed")
        block = ctx.enter_context(nc.Block())

        @block.sync
        def _(sp):
            sp.dma_start(wqkv[:, :, :], wqkv_in).then_inc(w_loaded, 16)
            sp.dma_start(woe[:, :, :], woe_in).then_inc(w_loaded, 16)

        @block.gpsimd
        def _(pool):
            def prep(g, s):
                pool.wait_ge(var_eps, nth(g))
                nc.gpsimd.tensor_tensor(rstd[:, :], veps[:, :], C["mhalf"][:, :], ALU.pow).then_inc(rstd_done, 1)

            two_halves(pool, N, prep, lambda g, s, more: prep(g + 1, 1 - s) if more else None)

        @block.tensor
        def _(pe):
            def transpose4(out, tiles4, width=P):
                for n, t in enumerate(tiles4):
                    last = nc.tensor.transpose(out[0:width, n * P:(n + 1) * P], t, C["ident"])
                return last

            def round_(g, n):
                if n >= 2:
                    pe.wait_ge(prep_copied, nth(g, NP, n - 2))

            def make_xT(g, s):
                pe.wait_ge(xn_ready, nth(g))
                pe.wait_ge(prep_copied, g * NP)
                for n in (0, 1):
                    transpose4(prep_bank(n), [xn[:, 4 * n + t, :] for t in range(4)]).then_inc(prep_ready, 1)

            def make_logits(g, s):
                pe.wait_ge(prep_copied, nth(g, NP, 1))
                for q in range(4):
                    last = nc.tensor.matmul(prep_bank(2)[32 * q:32 * q + 32, 0:4 * S], C["wr"],
                                            xnT[:, :].rearrange("p (r q k) -> p q r k", q=4, k=S)[:, q],
                                            start=True, stop=True)
                last.then_inc(prep_ready, 1)

            def make_token_rows(g, s):
                pe.wait_ge(choosing, (g + 1) * NC)
                pe.wait_ge(prep_copied, g * NP + 2)
                pe.sem_inc(passed, 1)
                transpose4(prep_bank(3), [slot[:, r * S:(r + 1) * S] for r in range(4)], S).then_inc(prep_ready, 1)
                pe.wait_ge(prep_copied, g * NP + 3)
                pe.sem_inc(passed, 1)
                transpose4(prep_bank(4), [gatev[:, r * S:(r + 1) * S] for r in range(4)], S).then_inc(prep_ready, 1)

            def make_gathered(g, s):
                pe.wait_ge(pick_ready, nth(g))
                for n in (5, 6):
                    round_(g, n)
                    for t in range(4):
                        last = nc.tensor.matmul(prep_bank(n)[:, t * P:(t + 1) * P], xn[:, 4 * (n - 5) + t, :],
                                                pick[:, 4 * (n - 5) + t].rearrange("p b n -> p (b n)"),
                                                start=True, stop=True)
                    last.then_inc(prep_ready, 1)

            def make_trig(g, s):
                for n in (7, 8):
                    round_(g, n)
                    for t in range(4):
                        last = nc.tensor.matmul(prep_bank(n)[:, t * P:(t + 1) * P], C["trig"],
                                                pick[:, 4 * (n - 7) + t].rearrange("p b n -> p (b n)"),
                                                start=True, stop=True)
                    last.then_inc(prep_ready, 1)
                for n in (9, 10):
                    pe.wait_ge(prep_copied, nth(g, NP, 8))
                    round_(g, n)
                    transpose4(prep_bank(n), [trigT[:, 4 * (n - 9) + e].rearrange("p b k -> p (b k)") for e in range(4)]
                               ).then_inc(prep_ready, 1)

            def make_pickT(g, s):
                pe.wait_ge(pickw_ready, nth(g))
                for n in (11, 12):
                    round_(g, n)
                    transpose4(prep_bank(n), [pickw[:, 4 * (n - 11) + t].rearrange("p b n -> p (b n)") for t in range(4)]
                               ).then_inc(prep_ready, 1)

            def prep(g, s):
                make_xT(g, s)
                make_logits(g, s)
                make_token_rows(g, s)
                make_gathered(g, s)
                make_trig(g, s)
                make_pickT(g, s)

            def make_qkv(g, s, h):
                for e in range(4):
                    nc.tensor.matmul(bank(6 * h + e)[:, 0:3 * D], xg[:, s, 4 * h + e].rearrange("p b k -> p (b k)"),
                                     wqkv[:, 4 * h + e, :], start=True, stop=True).then_inc(qkv_ready, 1)

            def make_qkT(g, s, h):
                pe.wait_ge(rotated, nth(g, 2, h))
                if h == 0:
                    pe.wait_ge(out_added, g * 2)
                else:
                    pe.wait_ge(qkT_copied, nth(g, 2, 0))
                for n in (0, 1):
                    last = transpose4(bank(4 + 6 * h + n), [qkv[:, 4 * h + e, n, :] for e in range(4)])
                last.then_inc(qkT_ready, 1)

            def make_scores(g, s, h):
                pe.wait_ge(qkT_copied, nth(g, 2, h))
                for e in range(4):
                    cols = slice(e * P, (e + 1) * P)
                    last = nc.tensor.matmul(bank(12 + h)[:, cols], qT[:, h, cols], kT[:, h, cols], start=True, stop=True)
                last.then_inc(s_ready, 1)

            def make_probT(g, s, h):
                pe.wait_ge(prob_ready, nth(g, 2, h))
                transpose4(bank(14 + h), [prob[:, h, e] for e in range(4)]).then_inc(probT_ready, 1)

            def make_av(g, s, h):
                pe.wait_ge(probT_copied, nth(g, 2, h))
                for e in range(4):
                    last = nc.tensor.matmul(bank(16 + h)[:, e * P:(e + 1) * P], qkv[:, 4 * h + e, 2, :], probT[:, h, e],
                                            start=True, stop=True)
                last.then_inc(av_ready, 1)

            def make_xpT(g, s, h):
                pe.wait_ge(av_copied, nth(g, 2, h))
                for e in range(4):
                    last = nc.tensor.matmul(bank(18 + h)[:, e * P:(e + 1) * P], woe[:, 4 * h + e, :], avT[:, h, e],
                                            start=True, stop=True)
                last.then_inc(xpT_ready, 1)

            def make_xp(g, s):
                pe.wait_ge(xpT_copied, nth(g, 2, 1))
                for n in (0, 1):
                    transpose4(bank(20 + n), [xpT[:, 2 * (4 * n + t):2 * (4 * n + t) + 2].rearrange("p b e k -> p (b e k)")
                                              for t in range(4)]).then_inc(xp_ready, 1)

            def make_out(g, s):
                for n in (0, 1):
                    pe.wait_ge(xp_copied, nth(g, 2, n))
                    for t in range(4):
                        last = nc.tensor.matmul(bank(22 + n)[:, t * D:(t + 1) * D], pickT[:, s, 4 * n + t], xp[:, 4 * n + t],
                                                start=True, stop=True)
                    last.then_inc(out_ready, 1)

            def step(g, s, more):
                make_qkv(g, s, 0)
                if more:
                    make_xT(g + 1, 1 - s)
                make_qkT(g, s, 0)
                make_qkv(g, s, 1)
                if more:
                    make_logits(g + 1, 1 - s)
                make_qkT(g, s, 1)
                make_scores(g, s, 0)
                make_scores(g, s, 1)
                make_probT(g, s, 0)
                make_probT(g, s, 1)
                make_av(g, s, 0)
                make_av(g, s, 1)
                make_xpT(g, s, 0)
                make_xpT(g, s, 1)
                if more:
                    make_token_rows(g + 1, 1 - s)
                make_xp(g, s)
                if more:
                    make_gathered(g + 1, 1 - s)
                make_out(g, s)
                if more:
                    make_trig(g + 1, 1 - s)
                    make_pickT(g + 1, 1 - s)

            pe.wait_ge(w_loaded, 32)
            two_halves(pe, N, prep, step)

        @block.scalar
        def _(act):
            A = nc.scalar

            def copy_round(g, n, out, rows=P):
                act.wait_ge(prep_ready, nth(g, NP, n))
                return A.copy(out, prep_bank(n)[0:rows, :])

            def prep_front(g, s):
                for n in (0, 1):
                    copy_round(g, n, xnT[:, n * 512:(n + 1) * 512]).then_inc(prep_copied, 1)

            def prep_exp(g, s):
                act.wait_ge(prep_ready, nth(g, NP, 2))
                A.activation(ex[:, :], prep_bank(2)[:, 0:4 * S], ACT.Exp, scale=-1.0).then_inc(prep_copied, 1)

            def prep_token_rows(g, s):
                for n, dst in ((3, slotT), (4, gateT)):
                    act.wait_ge(prep_ready, nth(g, NP, n))
                    for bb in (0, 1):
                        last = A.copy(dst[64 * bb:64 * bb + 64, :, :],
                                      prep_bank(n)[0:S, :].rearrange("p (t b e) -> p t b e", b=2, e=32)[:, :, bb, 0:E])
                    last.then_inc(prep_copied, 1)

            def by_expert(dst, n):
                return dst.rearrange("p e b k -> p b e k")[:, 8 * n:8 * n + 8]

            def prep_gathered(g, s):
                for n in (5, 6):
                    act.wait_ge(prep_ready, nth(g, NP, n))
                    A.copy(by_expert(xg[:, s], n - 5), prep_bank(n).rearrange("p (b e k) -> p b e k", e=E, k=KC)
                           ).then_inc(prep_copied, 1)

            def prep_trig(g, s):
                for n in (7, 8):
                    act.wait_ge(prep_ready, nth(g, NP, n))
                    A.copy(by_expert(trigT[:, :, :, :], n - 7), prep_bank(n).rearrange("p (b e k) -> p b e k", e=E, k=KC)
                           ).then_inc(prep_copied, 1)
                for n in (9, 10):
                    copy_round(g, n, trig[:, s, 4 * (n - 9):4 * (n - 9) + 4].rearrange("p e n -> p (e n)")
                               ).then_inc(prep_copied, 1)
                for n in (11, 12):
                    copy_round(g, n, pickT[:, s, 4 * (n - 11):4 * (n - 11) + 4].rearrange("p t n -> p (t n)")
                               ).then_inc(prep_copied, 1)

            def prep(g, s):
                prep_front(g, s)
                prep_exp(g, s)
                prep_token_rows(g, s)
                prep_gathered(g, s)
                prep_trig(g, s)

            def copy_qkv(g, h):
                for e in range(4):
                    act.wait_ge(qkv_ready, nth(g, 8, 4 * h + e))
                    last = A.copy(qkv[:, 4 * h + e].rearrange("p c n -> p (c n)"), bank(6 * h + e)[:, 0:3 * D])
                    last.then_inc(qkv_copied, 1)

            def copy_qkT(g, h):
                act.wait_ge(qkT_ready, nth(g, 2, h))
                A.copy(qT[:, h], bank(4 + 6 * h))
                A.copy(kT[:, h], bank(5 + 6 * h)).then_inc(qkT_copied, 1)

            def exps(g, h):
                act.wait_ge(shifted, nth(g, 2, h))
                A.activation(pe_[:, h], dif[:, h], ACT.Exp, scale=ASCALE).then_inc(e_ready, 1)

            def copy4(g, h, ready, out, n, copied):
                act.wait_ge(ready, nth(g, 2, h))
                A.copy(out.rearrange("p e n -> p (e n)"), bank(n)).then_inc(copied, 1)

            def copy_xpT(g, h):
                act.wait_ge(xpT_ready, nth(g, 2, h))
                A.copy(xpT[:, :, :, :].rearrange("p b e k -> p e b k")[:, 4 * h:4 * h + 4],
                       bank(18 + h).rearrange("p (e b k) -> p e b k", e=4, k=KC)).then_inc(xpT_copied, 1)

            def step(g, s, more):
                copy_qkv(g, 0)
                if more:
                    prep_front(g + 1, 1 - s)
                copy_qkT(g, 0)
                copy_qkv(g, 1)
                if more:
                    prep_exp(g + 1, 1 - s)
                copy_qkT(g, 1)
                for h in (0, 1):
                    exps(g, h)
                for h in (0, 1):
                    copy4(g, h, probT_ready, probT[:, h], 14 + h, probT_copied)
                for h in (0, 1):
                    copy4(g, h, av_ready, avT[:, h], 16 + h, av_copied)
                for h in (0, 1):
                    copy_xpT(g, h)
                if more:
                    prep_token_rows(g + 1, 1 - s)
                for n in (0, 1):
                    copy4(g, n, xp_ready, xp[:, 4 * n:4 * n + 4], 20 + n, xp_copied)
                if more:
                    prep_gathered(g + 1, 1 - s)
                    prep_trig(g + 1, 1 - s)

            two_halves(act, N, prep, step)

        @block.vector
        def _(dve):
            V = nc.vector

            def norm(g, s):
                for t in range(GT):
                    last = V.bn_stats(stats[:, t, :], tiles(g, t, 1))
                last.then_inc(stats_done, 1)
                dve.wait_ge(stats_done, g + 1)
                dve.sem_inc(passed, 1)
                for t in range(GT):
                    last = V.bn_aggr(mv[:, t, :], stats[:, t, :])
                last.then_inc(moments, 1)
                dve.wait_ge(moments, nth(g))
                V.tensor_scalar(veps[:, :], mv[:, :, 1], EPS, None, ALU.add).then_inc(var_eps, 1)
                dve.wait_ge(rstd_done, nth(g))
                dve.wait_ge(prep_ready, g * NP)
                for t in range(GT):
                    last = V.tensor_scalar(xn[:, t:t + 1, :], tiles(g, t, 1), mv[:, t, 0:1], rstd[:, t:t + 1],
                                           ALU.subtract, ALU.mult)
                last.then_inc(xn_ready, 1)

            def choose(g, s):
                by_r = lambda t: t[:, :].rearrange("p (r k) -> p r k", k=S)
                wide = lambda t: t.unsqueeze(2).broadcast_to((P, 4, S))
                dve.wait_ge(prep_copied, nth(g, NP, 2))
                V.tensor_scalar(ex1[:, :], ex[:, :], 1.0, None, ALU.add).then_inc(choosing, 1)
                dve.wait_ge(choosing, nth(g, NC, 0))
                V.reciprocal(gatev[:, :], ex1[:, :]).then_inc(choosing, 1)
                dve.wait_ge(choosing, nth(g, NC, 1))
                dve.sem_inc(passed, 1)
                for r in range(4):
                    last = V.max(m8[:, r, :], gatev[:, r * S:(r + 1) * S])
                last.then_inc(choosing, 1)
                dve.wait_ge(choosing, nth(g, NC, 2))
                V.tensor_tensor(by_r(gt), by_r(gatev), wide(m8[:, :, 7]), ALU.is_gt).then_inc(choosing, 1)
                dve.wait_ge(choosing, nth(g, NC, 3))
                V.tensor_tensor(by_r(eq), by_r(gatev), wide(m8[:, :, 7]), ALU.is_equal).then_inc(choosing, 1)
                dve.wait_ge(choosing, nth(g, NC, 4))
                V.tensor_reduce(ngt[:, :], by_r(gt), AX.X, ALU.add).then_inc(choosing, 1)
                dve.wait_ge(choosing, nth(g, NC, 5))
                V.tensor_tensor_scan(ceq[:, :], C["resetmask"], eq[:, :], 0.0, ALU.mult, ALU.add).then_inc(choosing, 1)
                dve.wait_ge(choosing, nth(g, NC, 6))
                V.tensor_tensor(by_r(tot), by_r(ceq), wide(ngt[:, :]), ALU.add).then_inc(choosing, 1)
                dve.wait_ge(choosing, nth(g, NC, 7))
                V.scalar_tensor_tensor(tied[:, :], tot[:, :], float(KC), eq[:, :], ALU.is_le, ALU.mult).then_inc(choosing, 1)
                dve.wait_ge(choosing, nth(g, NC, 8))
                V.tensor_tensor(chosen[:, :], tied[:, :], gt[:, :], ALU.add).then_inc(choosing, 1)
                dve.wait_ge(choosing, nth(g, NC, 9))
                V.tensor_tensor_scan(count[:, :], C["resetmask"], chosen[:, :], 0.0, ALU.mult, ALU.add).then_inc(choosing, 1)
                dve.wait_ge(choosing, nth(g, NC, 10))
                V.tensor_tensor(slot[:, :], count[:, :], chosen[:, :], ALU.mult).then_inc(choosing, 1)

            def make_pick(g, s):
                dve.wait_ge(prep_copied, nth(g, NP, 4))
                iota = C["kiota"].rearrange("p (e k) -> p e k", k=KC).unsqueeze(1).broadcast_to((P, GT, E, KC))
                view = lambda t, b, r: t[r, :, b, :].rearrange("p t (e k) -> p t e k", k=KC)
                wide = lambda t, r: t[r].unsqueeze(3).broadcast_to((64, GT, E, KC))
                for b in (0, 1):
                    r = slice(64 * b, 64 * b + 64)
                    last = V.tensor_tensor(view(pick, b, r), wide(slotT, r), iota[r], ALU.is_equal)
                last.then_inc(pick_ready, 1)
                dve.wait_ge(pick_ready, nth(g))
                for b in (0, 1):
                    r = slice(64 * b, 64 * b + 64)
                    last = V.tensor_tensor(view(pickw, b, r), view(pick, b, r), wide(gateT, r), ALU.mult)
                last.then_inc(pickw_ready, 1)

            def prep(g, s):
                norm(g, s)
                choose(g, s)
                make_pick(g, s)

            def rotate(g, s, h):
                dve.wait_ge(qkv_copied, nth(g, 8, 4 * h + 3))
                es = slice(4 * h, 4 * h + 4)
                cos2 = trig[:, s, es, 0:64].unsqueeze(2).broadcast_to((P, 4, 2, 64))
                sins = [trig[:, s, es, 64 + 32 * j:96 + 32 * j].unsqueeze(2).broadcast_to((P, 4, 2, 32)) for j in (0, 1)]
                V.tensor_tensor(rot1[:, h], qkv[:, es, 0:2, 0:64], cos2, ALU.mult).then_inc(rotated1, 1)
                V.tensor_tensor(rot2[:, h, :, :, 0:32], qkv[:, es, 0:2, 32:64], sins[0], ALU.mult)
                V.tensor_tensor(rot2[:, h, :, :, 32:64], qkv[:, es, 0:2, 0:32], sins[1], ALU.mult).then_inc(rotated2, 1)
                dve.wait_ge(rotated1, nth(g, 2, h))
                dve.wait_ge(rotated2, nth(g, 2, h))
                V.tensor_tensor(qkv[:, es, 0:2, 0:64], rot1[:, h], rot2[:, h], ALU.add).then_inc(rotated, 1)

            def shift(g, h):
                dve.wait_ge(s_ready, nth(g, 2, h))
                V.tensor_tensor(sm[:, h], bank(12 + h).rearrange("p (e n) -> p e n", n=P),
                                C["negmask"].unsqueeze(1).broadcast_to((P, 4, P)), ALU.add).then_inc(s_masked, 1)
                dve.wait_ge(s_masked, nth(g, 2, h))
                V.tensor_reduce(mx[:, h], sm[:, h], AX.X, ALU.max).then_inc(max_done, 1)
                dve.wait_ge(max_done, nth(g, 2, h))
                V.tensor_tensor(dif[:, h], sm[:, h], mx[:, h].unsqueeze(2).broadcast_to((P, 4, P)), ALU.subtract
                                ).then_inc(shifted, 1)

            def normalise(g, h):
                dve.wait_ge(e_ready, nth(g, 2, h))
                V.tensor_reduce(sums[:, h], pe_[:, h], AX.X, ALU.add).then_inc(sum_done, 1)
                dve.wait_ge(sum_done, nth(g, 2, h))
                V.reciprocal(inv[:, h], sums[:, h]).then_inc(inv_done, 1)
                dve.wait_ge(inv_done, nth(g, 2, h))
                V.tensor_tensor(prob[:, h], pe_[:, h], inv[:, h].unsqueeze(2).broadcast_to((P, 4, P)), ALU.mult
                                ).then_inc(prob_ready, 1)

            def add_out(g, s):
                for n in (0, 1):
                    dve.wait_ge(out_ready, nth(g, 2, n))
                    xs = tiles(g, 4 * n, 4)
                    V.tensor_tensor(xs, bank(22 + n).rearrange("p (t d) -> p t d", d=D), xs, ALU.add
                                    ).then_inc(out_added, 1)

            def step(g, s, more):
                if more:
                    norm(g + 1, 1 - s)
                dve.wait_ge(prep_copied, nth(g, NP, 10))
                rotate(g, s, 0)
                rotate(g, s, 1)
                shift(g, 0)
                shift(g, 1)
                normalise(g, 0)
                normalise(g, 1)
                if more:
                    choose(g + 1, 1 - s)
                    make_pick(g + 1, 1 - s)
                add_out(g, s)

            V.memset(pick[:, :, :, :], 0.0)
            V.memset(pickw[:, :, :, :], 0.0).then_inc(pick_set, 1)
            dve.wait_ge(pick_set, 1)
            two_halves(dve, N, prep, step)


def setup_phase(nc, ps, C, pack_in, bo_in, q_mask, pack, rows, work):
    with ExitStack() as ctx:
        sem = ctx.enter_context(Signals(nc, "setup_"))

        pack_loaded = sem("pack_loaded")
        bo_loaded = sem("bo_loaded")
        qmask_loaded = sem("qmask_loaded")
        consts_set = sem("consts_set")
        bias_product = sem("bias_product")
        bias_rows = sem("bias_rows")
        bias_stored = sem("bias_stored")
        qbias_done = sem("qbias_done")
        qany_done = sem("qany_done")
        qscale_diag = sem("qscale_diag")
        qscale_ready = sem("qscale_ready")
        qscale_copied = sem("qscale_copied")
        block = ctx.enter_context(nc.Block())

        @block.sync
        def _(sp):
            sp.dma_start(pack[:, :], pack_in).then_inc(pack_loaded, 16)
            sp.dma_start(rows[0:1, 0, :], bo_in).then_inc(bo_loaded, 16)
            for r in (0, 1):
                sp.dma_start(work["qmi"][64 * r:64 * r + 64, :], q_mask).then_inc(qmask_loaded, 16)
            sp.wait_ge(bias_rows, 1)
            for a in range(3):
                base = COLS[f"a{a}"][0] + 3 * D
                sp.dma_start(pack[DH:DH + 1, base:base + D], rows[0:1, 1, a * D:(a + 1) * D]).then_inc(bias_stored, 16)
            sp.wait_ge(bias_stored, 48)

        @block.tensor
        def _(pe):
            pe.wait_ge(pack_loaded, 16)
            for a in range(3):
                base = COLS[f"a{a}"][0]
                for r in (0, 1):
                    last = nc.tensor.matmul(ps[0:1, 0, a * D:(a + 1) * D],
                                            pack[:, base + 5 * D + 2 + r:base + 5 * D + 3 + r],
                                            pack[:, base + (3 + r) * D:base + (4 + r) * D],
                                            start=(r == 0), stop=(r == 1))
            last.then_inc(bias_product, 1)
            pe.wait_ge(qscale_diag, 1)
            nc.tensor.matmul(ps[:, 1, 0:64], work["ones"][0:64, :], work["diag"][0:64, :], start=True, stop=True
                             ).then_inc(qscale_ready, 1)

        @block.vector
        def _(dve):
            nc.vector.memset(C["mhalf"][:, :], -0.5)
            nc.vector.memset(C["half"][:, :], 0.5)
            nc.vector.memset(C["oneb"][:, :], 1.0 / 64)
            nc.vector.memset(work["ones"][:, :], 1.0).then_inc(consts_set, 1)
            dve.wait_ge(pack_loaded, 16)
            nc.vector.tensor_copy(C["identb"][:, :], C["ident"]).then_inc(consts_set, 1)
            dve.wait_ge(bias_product, 1)
            dve.wait_ge(bo_loaded, 16)
            nc.vector.tensor_tensor(rows[0:1, 1, :], ps[0:1, 0, 0:3 * D], rows[0:1, 0, :], ALU.add).then_inc(bias_rows, 1)
            dve.wait_ge(qmask_loaded, 32)
            nc.vector.tensor_scalar(C["qmask"][:, :], work["qmi"][:, :], 0.0, NEG, ALU.is_equal, ALU.mult
                                    ).then_inc(qbias_done, 1)
            dve.wait_ge(qbias_done, 1)
            nc.vector.tensor_reduce(work["any"][:, 0:1], C["qmask"][:, :], AX.X, ALU.max).then_inc(qany_done, 1)
            dve.wait_ge(qany_done, 1)
            nc.vector.tensor_scalar(work["any"][:, 1:2], work["any"][:, 0:1], 0.0, SCALE, ALU.is_equal, ALU.mult
                                    ).then_inc(qany_done, 1)
            dve.wait_ge(qany_done, 2)
            nc.vector.tensor_scalar(work["diag"][0:64, :], C["ident"][0:64, 0:64], work["any"][0:64, 1:2], None, ALU.mult
                                    ).then_inc(qscale_diag, 1)
            dve.wait_ge(qscale_ready, 1)
            nc.vector.tensor_copy(C["qscale"][:, :], ps[:, 1, 0:64]).then_inc(qscale_copied, 1)


def build(nc, x_in, ctx_in, q_mask, key_mask, pack_in, bo_in, wqkv_in, woe_in, gate_in, up_in, down_in, out):
    with ExitStack() as ctx:
        def sb(name, shape, dt=F32):
            return ctx.enter_context(nc.sbuf_tensor(name, shape, dt))

        ps = ctx.enter_context(nc.psum_tensor("ps", [P, 8, 512], F32))
        pack = sb("pack", [P, PACK])
        rows = sb("rows", [1, 2, 3 * D])
        x_res = sb("x_res", [P, NG * TILES, D])
        C = {"pack": pack}
        for n, (at, w) in COLS.items():
            C[n] = pack[:, at:at + w]
        C["identb"] = sb("identb", [P, P], BF16)
        C["oneb"] = sb("oneb", [P, 64], BF16)
        C["mhalf"] = sb("mhalf", [P, 8])
        C["half"] = sb("half", [P, 8])
        C["qmask"] = sb("qmask", [P, S], BF16)
        C["qscale"] = sb("qscale", [P, S])
        work = {"qmi": sb("qmi", [P, S], I32), "ones": sb("ones", [P, P]), "any": sb("qany", [P, 2]),
                "diag": sb("qdiag", [P, S])}
        setup_phase(nc, ps, C, pack_in, bo_in, q_mask, pack, rows, work)
        attention_phase(nc, ps, C, x_res, None, x_in, ctx_in, q_mask, key_mask, 0)
        choice_phase(nc, ps, C, x_res, wqkv_in, woe_in)
        y_res = sb("y_res", [P, NG * TILES, D])
        attention_phase(nc, ps, C, x_res, y_res, x_in, ctx_in, q_mask, key_mask, 1)
        attention_phase(nc, ps, C, x_res, y_res, x_in, ctx_in, q_mask, key_mask, 2)
        relu_phase(nc, ps, C, x_res, y_res)
        experts_phase(nc, ps, C, x_res, gate_in, up_in, down_in, out)


def padded_heads(w):
    out = np.zeros((P, 2) + w.shape[1:], np.float32)
    for h in range(H):
        r, c, j = h // HH, h % HH // 2, h % 2
        out[32 * c + 16 * j:32 * c + 16 * j + DH, r] = w[h * DH:(h + 1) * DH]
    return out


def kernel(**inputs):
    import concourse.bacc as bacc
    from concourse.bass_utils import run_bass_kernel_spmd

    a = {k: np.ascontiguousarray(v) for k, v in inputs.items()}
    pack = np.zeros((P, PACK), np.float32)

    def put(name, v, off=0):
        v = np.asarray(v, np.float32)
        v = v.reshape(v.shape[0], -1)
        at = COLS[name][0] + off
        pack[:v.shape[0], at:at + v.shape[1]] = v

    attn = [("L0_xattn_W{}", "L0_xattn_b{}", True), ("L1_xattn_sa_w{}", "L1_xattn_sa_b{}", False),
            ("L1_xattn_ca_w{}", "L1_xattn_ca_b{}", False)]
    for i, (w, b, flip) in enumerate(attn):
        for n, c in enumerate("qkv"):
            m = a[w.format(c)]
            put(f"a{i}", m.T if flip else m, n * D)
        m = a[w.format("o")]
        put(f"a{i}", padded_heads(m.T if flip else m), 3 * D)
        put(f"a{i}", a[b.format("q")][:, None], 5 * D)
        put(f"a{i}", a[b.format("k")][:, None], 5 * D + 1)
        put(f"a{i}", padded_heads(a[b.format("v")]), 5 * D + 2)
    put("ident", np.eye(P))
    sel = np.zeros((P, P))
    for m in range(P):
        sel[m // 16 * 16 + DH, m] = 1
    put("sel", sel)
    put("headmask", (np.arange(P)[:, None] // DH % HH == np.arange(HH)[None]) * 1.0)
    for n in ("g1", "b1", "g2", "b2", "g3", "b3"):
        put(n, np.broadcast_to(a["L1_xattn_" + n], (P, D)))
    put("wr", a["L0_ffn_Wr"].T)
    row = np.arange(P)
    put("negmask", np.where((row[:, None] // 8 == row // 8) & (row[:, None] >= row), 0.0, -1e30))
    put("kiota", np.broadcast_to(np.arange(64) % 8 + 1, (P, 64)))
    put("resetmask", np.broadcast_to(np.arange(256) % 64 > 0, (P, 256)))
    angle = ((row % S)[:, None].astype(np.float32)
             * (1.0 / 10000.0 ** (np.arange(32, dtype=np.float32) * 2.0 / 64)).astype(np.float32))
    put("trig", np.concatenate([np.cos(angle), np.cos(angle), -np.sin(angle), np.sin(angle)], 1))
    put("ff2b", np.broadcast_to(a["L1_xattn_ff_b2"], (P, D)))
    put("ff1", a["L1_xattn_ff_w1"])
    put("ff1b", a["L1_xattn_ff_b1"].reshape(4, P).T)
    put("ff2", a["L1_xattn_ff_w2"].reshape(4, P, D).transpose(1, 0, 2))
    put("router", a["L1_ffn_router_w"].T)
    put("rbias", np.broadcast_to(np.tile(a["L1_ffn_bias"], TILES), (P, 64)))
    put("lowmask", np.broadcast_to(np.tril(np.ones((16, 16)), -1).reshape(1, -1), (P, 256)))
    put("glowmask", np.broadcast_to(np.tril(np.ones((4, 4)), -1).reshape(1, -1), (P, 16)))

    def experts(name, shared):
        return np.concatenate([shared, a["L1_ffn_" + name]]).transpose(1, 0, 2).copy()

    bo = np.concatenate([a["L0_xattn_bo"], a["L1_xattn_sa_bo"], a["L1_xattn_ca_bo"]])[None]
    arrays = {
        "x": a["x"].reshape(-1, D), "ctx": a["ctx_1024"].reshape(-1, D), "q_mask": a["mask_SxS2_ik0"],
        "key_mask": a["mask_Bx1x1xS2_if1"].reshape(BATCH, S), "pack": pack, "bo": bo,
        "wqkv": a["L0_ffn_Wqkv"].transpose(1, 0, 2).copy(), "woe": a["L0_ffn_Wo"].transpose(1, 0, 2).copy(),
        "gate": experts("gate_w", a["L1_ffn_sh_gate_w"].reshape(D, 2, D).transpose(1, 0, 2)),
        "up": experts("up_w", a["L1_ffn_sh_up_w"].reshape(D, 2, D).transpose(1, 0, 2)),
        "down": experts("down_w", a["L1_ffn_sh_down_w"].reshape(2, D, D)),
    }
    nc = bacc.Bacc("TRN2", target_bir_lowering=False, num_devices=1)
    args = [nc.dram_tensor("in_" + n, v.shape, mybir.dt.from_np(v.dtype), kind="ExternalInput").ap() for n, v in arrays.items()]
    out = nc.dram_tensor("out", (BATCH * S, D), F32, kind="ExternalOutput").ap()
    build(nc, *args, out)
    r = run_bass_kernel_spmd(nc, [{"in_" + n: v for n, v in arrays.items()}], core_ids=[0])
    return r.results[0]["out"].reshape(BATCH, S, D)
```

```python
from contextlib import ExitStack

import numpy as np

import concourse.bass as bass
from concourse import mybir

F32 = mybir.dt.float32
BF16 = mybir.dt.bfloat16
I32 = mybir.dt.int32
ALU = mybir.AluOpType
ACT = mybir.ActivationFunctionType
AX = mybir.AxisListType

P = 128
D = 128
S = 64
BATCH = 128
H = 16
DH = D // H
TILES = 4
GB = 2 * TILES
TOK = TILES * P
NG = BATCH // GB
UNITS = 2 * TILES
HH = H // 2
NEG = -1.0e9
SCALE = float(DH) ** -0.5
EPS = 1e-5

ATTN_W = 5 * D + 3
COLS = {}
_at = 0
for _n, _w in [("a0", ATTN_W), ("a1", ATTN_W), ("a2", ATTN_W), ("ident", P), ("headmask", HH),
               ("g1", D), ("b1", D), ("g2", D), ("b2", D), ("g3", D), ("b3", D), ("ff2b", D),
               ("negmask", P), ("kiota", 64), ("resetmask", 256), ("trig", P), ("wr", 32),
               ("ff1", 4 * D), ("ff1b", 4), ("ff2", 4 * D), ("router", 16), ("rbias", 64),
               ("lowmask", 256), ("glowmask", 16)]:
    COLS[_n] = (_at, _w)
    _at += _w
PACK = _at


class Signals:

    def __init__(self, nc, prefix):
        self.nc, self.prefix, self.taken = nc, prefix, []

    def __enter__(self):
        return self

    def __exit__(self, *_):
        self.nc.clear_and_free_semaphores(self.taken)
        self.nc.all_engine_barrier()

    def __call__(self, name):
        self.taken.append(self.nc.alloc_semaphore(self.prefix + name))
        return self.taken[-1]


def attention_phase(nc, ps, C, x_res, y_res, x_in, ctx_in, q_mask, key_mask, a):
    cross = a != 1
    load_x = a == 0
    pre_norm = a != 2
    post_norm = a != 0

    with ExitStack() as ctx:
        def sb(name, shape, dt=F32):
            return ctx.enter_context(nc.sbuf_tensor(f"{name}{a}", shape, dt))

        sem = ctx.enter_context(Signals(nc, f"a{a}_"))

        base = COLS[f"a{a}"][0]
        pk = C["pack"]
        wq, wk, wv, wo, bo = (pk[:, base + i * D:base + (i + 1) * D] for i in range(5))
        bq, bk, bv = (pk[:, base + 5 * D + i:base + 5 * D + i + 1] for i in range(3))
        ident, headmask = C["ident"], C["headmask"]

        xn = sb("xn", [P, 2, TILES, D])
        xb = sb("xb", [P, 2, TILES, D])
        qd = sb("qd", [P, 2, 2, TOK])
        kblk = sb("kblk", [P, 2, GB, HH, S])
        vblk = sb("vblk", [P, 2, GB, HH, 32])
        srcT = sb("srcT", [P, TOK])
        ctxT = sb("ctxT", [P, TOK]) if cross else srcT
        ksb = sb("ksb", [P, TOK])
        stats = sb("stats", [P, TILES, 6])
        mv = sb("mv", [P, TILES, 2])
        veps = sb("veps", [P, TILES])
        rstd = sb("rstd", [P, TILES])
        mx = sb("mx", [P, 2, HH])
        sh = sb("sh", [P, 2, HH * S])
        ex = sb("ex", [P, 2, 4, P])
        inv = sb("inv", [P, 2, 2 * H])
        on = sb("on", [P, 2, 2, D])
        onT = sb("onT", [P, 2, 2 * P])
        if cross:
            cin = sb("cin", [P, 2, TILES, D])
        if a == 2:
            kmi = sb("kmi", [P, 2, GB, S], I32)
            kmb = sb("kmb", [P, 2, GB, S], BF16)
            kany = sb("kany", [P, 2, GB])
            qsc = sb("qsc", [P, 2, GB])
        if post_norm:
            t1 = sb("t1", [P, 2, 2, D])
            st2 = sb("st2", [P, 2, 2, 6])
            mv2 = sb("mv2", [P, 2, 2, 2])
            sd2 = sb("sd2", [P, 2, 2])
            se2 = sb("se2", [P, 2, 2])
            rs2 = sb("rs2", [P, 2, 2])
            z2 = sb("z2", [P, 2, 2, D])
            zg2 = sb("zg2", [P, 2, 2, D])
            gam, bet = C[f"g{a}"], C[f"b{a}"]

        SB = [ps[:, i, :] for i in (0, 1)]
        TB = [ps[:, i, :] for i in (2, 3)]
        OB = [ps[:, i, :] for i in (4, 5)]
        PREP = ps[:, 6, :]
        PROJ = ps[:, 7, :]

        rounds = ["cT", "k", "v0", "v1", "xT", "q"] if cross else ["xT", "k", "q", "v0", "v1"]
        slots = dict(zip(rounds, (0, 1, 2, 3, 4, 5) if cross else (2, 3, 4, 5, 6)))
        NP = len(rounds)
        k_slot = slots["k"]
        spread_by_act = {j: k_slot + 1 + j for j in range(4)}
        spread_by_dve = {4: k_slot + 2, 5: k_slot + 3, 6: k_slot + 4}
        spread_by_pool = (7,)
        nr = rounds.index

        x_loaded = [sem(f"x_loaded{s}_") for s in (0, 1)]
        c_loaded = [sem(f"c_loaded{s}_") for s in (0, 1)]
        m_loaded = [sem(f"m_loaded{s}_") for s in (0, 1)]
        vblk_set = sem("vblk_set")
        act_spread = sem("act_spread")
        dve_spread = sem("dve_spread")
        pool_spread = sem("pool_spread")
        stats_done = sem("stats_done")
        moments = sem("moments")
        var_eps = sem("var_eps")
        rstd_done = sem("rstd_done")
        xn_ready = sem("xn_ready")
        xb_ready = sem("xb_ready")
        kmask_bias = sem("kmask_bias")
        kmask_any = sem("kmask_any")
        kmask_ready = sem("kmask_ready")
        prep_ready = sem("prep_ready")
        prep_copied = sem("prep_copied")
        s_ready = sem("s_ready")
        max_done = sem("max_done")
        shifted = sem("shifted")
        t_ready = sem("t_ready")
        e_ready = sem("e_ready")
        o_ready = sem("o_ready")
        inverted = sem("inverted")
        divided = sem("divided")
        onT_ready = sem("onT_ready")
        onT_copied = sem("onT_copied")
        proj_ready = sem("proj_ready")
        resid_done = sem("resid_done")
        stats2_done = sem("stats2_done")
        moments2 = sem("moments2")
        std2 = sem("std2")
        std2_eps = sem("std2_eps")
        rstd2 = sem("rstd2")
        z_done = sem("z_done")
        zg_done = sem("zg_done")
        y_done = sem("y_done")

        def by_batch(t):
            return t.rearrange("p (b k) -> p b k", k=S)

        def swapped(t, b):
            return t.rearrange("p (t b) k -> p b t k", b=2)[:, 1 - b]

        def loaded(g, s):
            return g * 8 + (16 - 8 * s)

        passed = sem("passed")
        block = ctx.enter_context(nc.Block())

        @block.sync
        def _(sp):
            def loads(g, s):
                if load_x:
                    sp.dma_start(tiles_of(x_res, g),
                                 x_in[bass.ds(g * TOK, TOK), :].rearrange("(t p) d -> p t d", p=P)
                                 ).then_inc(x_loaded[s], 16)
                if cross:
                    sp.dma_start(cin[:, s], ctx_in[bass.ds(g * TOK, TOK), :].rearrange("(t p) d -> p t d", p=P)
                                 ).then_inc(c_loaded[s], 16)
                if a == 2:
                    km = key_mask[bass.ds(g * GB, GB), :]
                    sp.dma_start(kmi[0:64, s], km.partition_broadcast(64)).then_inc(m_loaded[s], 16)
                    for b in (0, 1):
                        sp.dma_start(swapped(kmi[64:128, s], b),
                                     km.rearrange("(t b) k -> b t k", b=2)[b].partition_broadcast(64)
                                     ).then_inc(m_loaded[s], 16)

            if cross:
                loads(0, 0)
                loads(1, 1)
                with sp.Fori(0, NG // 2 - 1) as i:
                    for s in (0, 1):
                        sp.wait_ge(prep_ready, nth(i * 2 + s, NP, nr("cT")))
                        sp.sem_inc(passed, 1)
                        if a == 2:
                            sp.wait_ge(kmask_bias, nth(i * 2 + s))
                            sp.sem_inc(passed, 1)
                        loads(i * 2 + (s + 2), s)

        @block.gpsimd
        def _(pool):
            def rows_of(g):
                return tiles_of(x_res if a == 0 else y_res, g)

            def inputs_of(g, s, first):
                if pre_norm:
                    pool.wait_ge(var_eps, nth(g))
                    nc.gpsimd.tensor_tensor(rstd[:, :], veps[:, :], C["mhalf"][:, 0:TILES], ALU.pow
                                            ).then_inc(rstd_done, 1)
                else:
                    if not first:
                        pool.wait_ge(prep_ready, nth(g - 2, NP, nr("xT")))
                        pool.sem_inc(passed, 1)
                    nc.gpsimd.tensor_copy(xn[:, s], rows_of(g)).then_inc(xn_ready, 1)

            def with_bias(g, s, first):
                if a == 1:
                    pool.wait_ge(xn_ready, nth(g))
                if not first:
                    pool.wait_ge(resid_done, g * 2 - 2)
                if a == 1 or not first:
                    pool.sem_inc(passed, 1)
                nc.gpsimd.tensor_tensor(xb[:, s], xn[:, s] if a == 1 else rows_of(g), across(bo, TILES), ALU.add
                                        ).then_inc(xb_ready, 1)

            def spread_keys(g, s):
                pool.wait_ge(prep_copied, nth(g, NP, nr("k")))
                pool.sem_inc(passed, 1)
                for j in spread_by_pool:
                    last = nc.gpsimd.tensor_scalar(kblk[:, s, :, j, :], by_batch(ksb[:, :]), headmask[:, j:j + 1],
                                                   None, ALU.mult)
                last.then_inc(pool_spread, 1)

            def finish(g, m):
                if post_norm:
                    pool.wait_ge(moments2, nth(g, 2, m))
                    nc.gpsimd.tensor_tensor(sd2[:, m, :], mv2[:, m, :, 1], C["half"][:, 0:2], ALU.pow
                                            ).then_inc(std2, 1)
                    pool.wait_ge(z_done, nth(g, 2, m))
                    nc.gpsimd.tensor_tensor(zg2[:, m], z2[:, m], across(gam, 2), ALU.mult).then_inc(zg_done, 1)
                    pool.wait_ge(zg_done, nth(g, 2, m))
                    pool.sem_inc(passed, 1)
                    nc.gpsimd.tensor_tensor(tiles_of(y_res, g, 2 * m, 2), zg2[:, m], across(bet, 2), ALU.add
                                            ).then_inc(y_done, 1)

            def step(g, s, first, more):
                if more:
                    inputs_of(g + 1, 1 - s, first)
                if not first:
                    finish(g - 1, 0)
                if more:
                    spread_keys(g + 1, 1 - s)
                    with_bias(g + 1, 1 - s, first)
                if not first:
                    finish(g - 1, 1)
                if not more:
                    finish(g, 0)
                    finish(g, 1)

            def prep(g, s):
                inputs_of(g, s, True)
                spread_keys(g, s)
                with_bias(g, s, True)

            pipelined(pool, NG, prep, step)

        @block.scalar
        def _(act):
            def copy_round(g, n, out):
                act.wait_ge(prep_ready, nth(g, NP, n))
                nc.scalar.copy(out, PREP).then_inc(prep_copied, 1)

            def copy_k(g, s):
                act.wait_ge(prep_ready, nth(g, NP, nr("k")))
                nc.scalar.activation(ksb[:, :], PREP, ACT.Identity, bias=bk).then_inc(prep_copied, 1)

            def spread_key(g, s, j):
                if j == 0:
                    act.wait_ge(prep_copied, nth(g, NP, nr("k")))
                nc.scalar.activation(kblk[:, s, :, j, :], by_batch(ksb[:, :]), ACT.Copy, scale=headmask[:, j:j + 1]
                                     ).then_inc(act_spread, 1)

            def copy_v(g, s, h):
                act.wait_ge(prep_ready, nth(g, NP, nr(f"v{h}")))
                for j in (0, 1):
                    rows = slice(64 * j, 64 * j + 64)
                    last = nc.scalar.copy(
                        vblk[rows, s, 4 * h:4 * h + 4, :, 16 * j:16 * j + DH].rearrange("p b r e -> p (b r) e"),
                        PREP[rows, :].rearrange("p (b e) -> p b e", e=2 * DH)[:, :, DH * j:DH * j + DH])
                last.then_inc(prep_copied, 1)

            def prep_slot(g, s, v):
                if v == slots.get("cT"):
                    copy_round(g, nr("cT"), ctxT[:, :])
                if v == slots["xT"]:
                    copy_round(g, nr("xT"), srcT[:, :])
                if v == slots["k"]:
                    copy_k(g, s)
                for j in spread_by_act:
                    if v == spread_by_act[j]:
                        spread_key(g, s, j)
                for h in (0, 1):
                    if v == slots[f"v{h}"]:
                        copy_v(g, s, h)

            def exps(g, u):
                act.wait_ge(t_ready, nth(g, UNITS, u))
                nc.scalar.activation(ex[:, u % 2], TB[u % 2].rearrange("p (c n) -> p c n", n=P), ACT.Exp
                                     ).then_inc(e_ready, 1)

            def copy_onT(g, m):
                act.wait_ge(onT_ready, nth(g, 2, m))
                nc.scalar.activation(onT[:, m], OB[m][:, 0:2 * P], ACT.Identity, bias=bv).then_inc(onT_copied, 1)

            def prep(g, s):
                for v in range(UNITS):
                    prep_slot(g, s, v)

            def step(g, s, first, more):
                for v in range(UNITS):
                    if v > 0:
                        exps(g, v - 1)
                    elif not first:
                        exps(g - 1, UNITS - 1)
                    if v == 2 and not first:
                        copy_onT(g - 1, 1)
                    if v == 6:
                        copy_onT(g, 0)
                    if more:
                        prep_slot(g + 1, 1 - s, v)
                if not more:
                    exps(g, UNITS - 1)
                    copy_onT(g, 1)

            act.wait_ge(vblk_set, 3)
            pipelined(act, NG, prep, step)

        @block.vector
        def _(dve):
            def norm_stats(g, s):
                if not pre_norm:
                    return
                if load_x:
                    dve.wait_ge(x_loaded[s], loaded(g, s))
                for t in range(TILES):
                    last = nc.vector.bn_stats(stats[:, t, :], tiles_of(x_res, g, t, 1))
                last.then_inc(stats_done, 1)
                dve.wait_ge(stats_done, nth(g))
                dve.sem_inc(passed, 1)
                for t in range(TILES):
                    last = nc.vector.bn_aggr(mv[:, t, :], stats[:, t, :])
                last.then_inc(moments, 1)
                dve.wait_ge(moments, nth(g))
                nc.vector.tensor_scalar(veps[:, :], mv[:, :, 1], EPS, None, ALU.add).then_inc(var_eps, 1)

            def norm_apply(g, s):
                if not pre_norm:
                    return
                dve.wait_ge(rstd_done, nth(g))
                for t in range(TILES):
                    last = nc.vector.tensor_scalar(xn[:, s, t:t + 1, :], tiles_of(x_res, g, t, 1), mv[:, t, 0:1],
                                                   rstd[:, t:t + 1], ALU.subtract, ALU.mult)
                last.then_inc(xn_ready, 1)

            def key_mask_of_next(g, s):
                if a != 2:
                    return
                dve.wait_ge(m_loaded[s], loaded(g, s) * 3)
                nc.vector.tensor_scalar(kmb[:, s], kmi[:, s], 0.0, NEG, ALU.is_equal, ALU.mult).then_inc(kmask_bias, 1)
                dve.wait_ge(kmask_bias, nth(g))
                nc.vector.tensor_reduce(kany[:, s], kmb[:, s], AX.X, ALU.max).then_inc(kmask_any, 1)
                dve.wait_ge(kmask_any, nth(g))
                nc.vector.tensor_scalar(qsc[:, s], kany[:, s], 0.0, SCALE, ALU.is_equal, ALU.mult
                                        ).then_inc(kmask_ready, 1)

            def copy_q(g, s):
                if a == 2:
                    dve.wait_ge(kmask_ready, nth(g))
                dve.wait_ge(prep_ready, nth(g, NP, nr("q")))
                pr = PREP.rearrange("p (t b k) -> p b t k", b=2, k=S)
                for half in (0, 1):
                    rows = slice(64 * half, 64 * half + 64)
                    for w in (0, 1):
                        b = w ^ half
                        out = qd[rows, s, w].rearrange("p (t b k) -> p b t k", b=2, k=S)[:, b]
                        if a == 0:
                            last = nc.vector.tensor_scalar(out, pr[rows, b], bq[rows], SCALE, ALU.add, ALU.mult)
                            continue
                        if a == 1:
                            sc = C["qscale"][rows, :].unsqueeze(1).broadcast_to((64, TILES, S))
                        else:
                            sc = qsc[rows, s].rearrange("p (t b) -> p b t", b=2)[:, w].unsqueeze(2
                                                                                   ).broadcast_to((64, TILES, S))
                        last = nc.vector.scalar_tensor_tensor(out, pr[rows, b], bq[rows], sc, ALU.add, ALU.mult)
                last.then_inc(prep_copied, 1)

            def spread_key(g, s, j):
                if j == min(spread_by_dve):
                    dve.wait_ge(prep_copied, nth(g, NP, nr("k")))
                    dve.sem_inc(passed, 1)
                nc.vector.tensor_scalar(kblk[:, s, :, j, :], by_batch(ksb[:, :]), headmask[:, j:j + 1], None, ALU.mult
                                        ).then_inc(dve_spread, 1)

            def shift(g, u):
                dve.wait_ge(s_ready, nth(g, UNITS, u))
                sc = SB[u % 2].rearrange("p (h k) -> p h k", k=S)
                nc.vector.tensor_reduce(mx[:, u % 2], sc, AX.X, ALU.max).then_inc(max_done, 1)
                dve.wait_ge(max_done, nth(g, UNITS, u))
                nc.vector.tensor_tensor(sh[:, u % 2].rearrange("p (h k) -> p h k", k=S), sc,
                                        mx[:, u % 2].unsqueeze(2).broadcast_to((P, HH, S)), ALU.subtract
                                        ).then_inc(shifted, 1)

            def divide(g, m):
                o = OB[m].rearrange("p (h e) -> p h e", e=16)
                dve.wait_ge(o_ready, nth(g, 2, m))
                nc.vector.reciprocal(inv[:, m], o[:, :, DH]).then_inc(inverted, 1)
                dve.wait_ge(inverted, nth(g, 2, m))
                nc.vector.tensor_tensor(on[:, m].rearrange("p t (h e) -> p (t h) e", e=DH), o[:, :, 0:DH],
                                        inv[:, m].unsqueeze(2).broadcast_to((P, 2 * H, DH)), ALU.mult
                                        ).then_inc(divided, 1)

            def residual(g, s, m):
                if m == 0:
                    dve.wait_ge(xb_ready, nth(g))
                dve.wait_ge(proj_ready, nth(g, 2, m))
                pr = PROJ[:, 256 * m:256 * m + 256].rearrange("p (t d) -> p t d", d=D)
                xs = xb[:, s, 2 * m:2 * m + 2, :]
                if not post_norm:
                    nc.vector.tensor_tensor(tiles_of(x_res, g, 2 * m, 2), pr, xs, ALU.add).then_inc(resid_done, 1)
                    return
                nc.vector.tensor_tensor(t1[:, m], pr, xs, ALU.add).then_inc(resid_done, 1)
                dve.wait_ge(resid_done, nth(g, 2, m))
                for t in (0, 1):
                    last = nc.vector.bn_stats(st2[:, m, t, :], t1[:, m, t, :])
                last.then_inc(stats2_done, 1)
                dve.wait_ge(stats2_done, nth(g, 2, m))
                dve.sem_inc(passed, 1)
                for t in (0, 1):
                    last = nc.vector.bn_aggr(mv2[:, m, t, :], st2[:, m, t, :])
                last.then_inc(moments2, 1)

            def normalise(g, m):
                if not post_norm:
                    return
                dve.wait_ge(std2, nth(g, 2, m))
                nc.vector.tensor_scalar(se2[:, m], sd2[:, m], EPS, None, ALU.add).then_inc(std2_eps, 1)
                dve.wait_ge(std2_eps, nth(g, 2, m))
                nc.vector.reciprocal(rs2[:, m], se2[:, m]).then_inc(rstd2, 1)
                dve.wait_ge(rstd2, nth(g, 2, m))
                for t in (0, 1):
                    last = nc.vector.tensor_scalar(z2[:, m, t, :], t1[:, m, t, :], mv2[:, m, t, 0:1],
                                                   rs2[:, m, t:t + 1], ALU.subtract, ALU.mult)
                last.then_inc(z_done, 1)

            def prep(g, s):
                norm_stats(g, s)
                key_mask_of_next(g, s)
                norm_apply(g, s)
                for j in spread_by_dve:
                    spread_key(g, s, j)
                copy_q(g, s)

            def step(g, s, first, more):
                for v in range(UNITS):
                    if not first:
                        if v == 0:
                            residual(g - 1, 1 - s, 0)
                        if v == 2:
                            divide(g - 1, 1)
                        if v == 4:
                            residual(g - 1, 1 - s, 1)
                    if v == 6:
                        divide(g, 0)
                    if more and v == slots["q"] + 1:
                        copy_q(g + 1, 1 - s)
                    shift(g, v)
                    if more and v == 0:
                        norm_stats(g + 1, 1 - s)
                        key_mask_of_next(g + 1, 1 - s)
                    if more and v == 1:
                        norm_apply(g + 1, 1 - s)
                    for j in spread_by_dve:
                        if more and v == spread_by_dve[j]:
                            spread_key(g + 1, 1 - s, j)
                    if not first:
                        if v == 1:
                            normalise(g - 1, 0)
                        if v == 5:
                            normalise(g - 1, 1)
                if not more:
                    divide(g, 1)
                    residual(g, s, 0)
                    normalise(g, 0)
                    residual(g, s, 1)
                    normalise(g, 1)

            nc.vector.memset(qd[:, :, :, :], 0.0)
            nc.vector.memset(vblk[:, :, :, :, :], 0.0).then_inc(vblk_set, 1)
            dve.wait_ge(vblk_set, 1)
            nc.vector.memset(vblk[0:64, :, :, :, DH:DH + 1], 1.0).then_inc(vblk_set, 1)
            nc.vector.memset(vblk[64:128, :, :, :, 16 + DH:17 + DH], 1.0).then_inc(vblk_set, 1)
            pipelined(dve, NG, prep, step)

        @block.tensor
        def _(pe):
            def prep_slot(g, s, v, start):
                n = [nr(r) for r in rounds if slots[r] == v]
                if not n:
                    return
                n = n[0]
                what = rounds[n]
                if n > 0:
                    pe.wait_ge(prep_copied, nth(g, NP, n - 1))
                elif not start:
                    pe.wait_ge(prep_copied, g * NP)
                if what == "xT":
                    pe.wait_ge(xn_ready, nth(g))
                    for t in range(TILES):
                        last = nc.tensor.transpose(PREP[:, t * P:(t + 1) * P], xn[:, s, t, :], ident)
                elif what == "cT":
                    pe.wait_ge(c_loaded[s], loaded(g, s))
                    for t in range(TILES):
                        last = nc.tensor.transpose(PREP[:, t * P:(t + 1) * P], cin[:, s, t, :], ident)
                elif what == "k":
                    nc.tensor.matmul(PREP[0:64, :], wk[:, 0:64], ctxT[:, :], start=True, stop=True)
                    for b in (0, 1):
                        last = nc.tensor.matmul(PREP[64:128, :].rearrange("p (t b k) -> p b t k", b=2, k=S)[:, 1 - b],
                                                wk[:, 64:128],
                                                ctxT[:, :].rearrange("p (t b k) -> p b t k", b=2, k=S)[:, b],
                                                start=True, stop=True)
                elif what == "q":
                    last = nc.tensor.matmul(PREP, wq, srcT[:, :], start=True, stop=True)
                else:
                    h = int(what[1])
                    for b in range(4):
                        for j in (0, 1):
                            last = nc.tensor.matmul(PREP[64 * j:64 * j + 64, b * D:(b + 1) * D],
                                                    ctxT[:, (4 * h + b) * S:(4 * h + b + 1) * S], wv,
                                                    start=True, stop=True)
                last.then_inc(prep_ready, 1)

            def scores(g, s, u):
                t, w = u // 2, u % 2
                if u == 0:
                    pe.wait_ge(prep_copied, (g + 1) * NP)
                    pe.sem_inc(passed, 1)
                    pe.wait_ge(act_spread, (g + 1) * len(spread_by_act))
                    pe.sem_inc(passed, 1)
                    pe.wait_ge(dve_spread, (g + 1) * len(spread_by_dve))
                    pe.sem_inc(passed, 1)
                    pe.wait_ge(pool_spread, g + 1)
                    pe.sem_inc(passed, 1)
                last = nc.tensor.matmul(SB[w], qd[:, s, w, t * P:(t + 1) * P],
                                        kblk[:, s, 2 * t + w].rearrange("p h k -> p (h k)"), start=True, stop=a == 0)
                if a == 1:
                    last = nc.tensor.matmul(SB[w], C["identb"][:, :],
                                            C["qmask"][0:S, :].unsqueeze(1).broadcast_to((S, HH, S)),
                                            start=False, stop=True)
                if a == 2:
                    last = nc.tensor.matmul(SB[w], C["oneb"][:, :],
                                            kmb[:, s, 2 * t, :].unsqueeze(1).broadcast_to((P, HH, S)),
                                            start=False, stop=True)
                last.then_inc(s_ready, 1)

            def transposes(g, u):
                pe.wait_ge(shifted, nth(g, UNITS, u))
                for c in range(4):
                    last = nc.tensor.transpose(TB[u % 2][:, c * P:(c + 1) * P], sh[:, u % 2, c * P:(c + 1) * P], ident)
                last.then_inc(t_ready, 1)

            def weigh(g, s, u, first):
                t, w = u // 2, u % 2
                m = t // 2
                if u % 4 == 0 and not (first and m == 0):
                    pe.wait_ge(onT_copied, g * 2 + (m - 1))
                pe.wait_ge(e_ready, nth(g, UNITS, u))
                for c in range(4):
                    for bb in (0, 1):
                        r = w ^ bb
                        col = ((t % 2) * H + r * HH + 2 * c) * 16
                        last = nc.tensor.matmul(OB[m][64 * bb:64 * bb + 64, col:col + 32],
                                                ex[:, u % 2, c, bb * S:(bb + 1) * S],
                                                vblk[:, s, 2 * t + bb, 4 * r + c, :], start=True, stop=True)
                if u % 4 == 3:
                    last.then_inc(o_ready, 1)

            def make_onT(g, m):
                pe.wait_ge(divided, nth(g, 2, m))
                for t in (0, 1):
                    last = nc.tensor.transpose(OB[m][:, t * P:(t + 1) * P], on[:, m, t, :], ident)
                last.then_inc(onT_ready, 1)

            def project(g, m, first=False):
                if not (first and m == 0):
                    pe.wait_ge(resid_done, g * 2 + m)
                pe.wait_ge(onT_copied, nth(g, 2, m))
                for t in (0, 1):
                    last = nc.tensor.matmul(PROJ[:, (2 * m + t) * D:(2 * m + t + 1) * D], onT[:, m, t * P:(t + 1) * P],
                                            wo, start=True, stop=True)
                last.then_inc(proj_ready, 1)

            def prep(g, s):
                for v in range(UNITS):
                    prep_slot(g, s, v, True)

            def step(g, s, first, more):
                for v in range(UNITS):
                    scores(g, s, v)
                    if v > 0:
                        transposes(g, v - 1)
                    elif not first:
                        transposes(g - 1, UNITS - 1)
                    if v > 1:
                        weigh(g, s, v - 2, first)
                    elif not first:
                        weigh(g - 1, 1 - s, UNITS - 2 + v, False)
                    if more:
                        prep_slot(g + 1, 1 - s, v, False)
                    if not first:
                        if v == 2:
                            make_onT(g - 1, 1)
                        if v == 3:
                            project(g - 1, 1)
                    if v == 6:
                        make_onT(g, 0)
                    if v == 7:
                        project(g, 0, first)
                if not more:
                    transposes(g, UNITS - 1)
                    weigh(g, s, UNITS - 2, False)
                    weigh(g, s, UNITS - 1, False)
                    make_onT(g, 1)
                    project(g, 1)

            pipelined(pe, NG, prep, step)


def pipelined(eng, n, prep, step):
    prep(0, 0)
    step(0, 0, True, True)
    with eng.Fori(0, n // 2 - 1) as i:
        for s in (1, 0):
            step(i * 2 + (2 - s), s, False, True)
    step(n - 1, 1, False, False)


def two_halves(eng, n, prep, step):
    prep(0, 0)
    step(0, 0, True)
    with eng.Fori(0, n // 2 - 1) as i:
        for s in (1, 0):
            step(i * 2 + (2 - s), s, True)
    step(n - 1, 1, False)


def nth(g, n=1, k=0):
    return g * n + (k + 1)


def tiles_of(t, g, k=0, n=TILES):
    return t[:, bass.ds(g * TILES + k, n), :]


def across(row, n):
    return row.unsqueeze(1).broadcast_to((P, n, D))


def relu_phase(nc, ps, C, x_res, y_res):
    F = 4
    with ExitStack() as ctx:
        def sb(name, shape, dt=F32):
            return ctx.enter_context(nc.sbuf_tensor("ff_" + name, shape, dt))

        sem = ctx.enter_context(Signals(nc, "ff_"))

        w1 = C["ff1"].rearrange("p (c n) -> p c n", c=F)
        b1 = C["ff1b"]
        w2 = C["ff2"].rearrange("p (c n) -> p c n", c=F)
        yn = sb("yn", [P, 2, TILES, D])
        yT = sb("yT", [P, 2, TOK])
        hT = sb("hT", [P, F, TOK])
        yb = sb("yb", [P, TILES, D])
        t1 = sb("t1", [P, TILES, D])
        st = sb("st", [P, TILES, 6])
        mv = sb("mv", [P, TILES, 2])
        sd = sb("sd", [P, TILES])
        se = sb("se", [P, TILES])
        rs = sb("rs", [P, TILES])
        z = sb("z", [P, TILES, D])
        zg = sb("zg", [P, TILES, D])
        zb = sb("zb", [P, TILES, D])
        HB = [ps[:, i, :] for i in range(4)]
        OUTB = [ps[:, i, :] for i in (4, 5)]
        XB = [ps[:, i, :] for i in (6, 7)]

        yn_ready = sem("yn_ready")
        yb_ready = sem("yb_ready")
        yT_ready = sem("yT_ready")
        yT_copied = sem("yT_copied")
        h_ready = sem("h_ready")
        relu_done = sem("relu_done")
        out_ready = sem("out_ready")
        summed = sem("summed")
        stats_done = sem("stats_done")
        moments = sem("moments")
        std_done = sem("std_done")
        std_eps = sem("std_eps")
        rstd_done = sem("rstd_done")
        z_done = sem("z_done")
        zg_done = sem("zg_done")
        zb_done = sem("zb_done")
        x_done = sem("x_done")
        passed = sem("passed")
        block = ctx.enter_context(nc.Block())

        @block.gpsimd
        def _(pool):
            def prep(g, s):
                nc.gpsimd.tensor_copy(yn[:, s], tiles_of(y_res, g)).then_inc(yn_ready, 1)

            def step(g, s, more):
                pool.wait_ge(summed, g)
                pool.sem_inc(passed, 1)
                nc.gpsimd.tensor_tensor(yb[:, :, :], tiles_of(y_res, g), across(C["ff2b"], TILES), ALU.add
                                        ).then_inc(yb_ready, 1)
                if more:
                    pool.wait_ge(yT_ready, g)
                    prep(g + 1, 1 - s)
                pool.wait_ge(moments, nth(g))
                nc.gpsimd.tensor_tensor(sd[:, :], mv[:, :, 1], C["half"][:, 0:TILES], ALU.pow).then_inc(std_done, 1)
                pool.wait_ge(z_done, nth(g))
                nc.gpsimd.tensor_tensor(zg[:, :, :], z[:, :, :], across(C["g3"], TILES), ALU.mult).then_inc(zg_done, 1)
                pool.wait_ge(zg_done, nth(g))
                pool.wait_ge(x_done, g)
                nc.gpsimd.tensor_tensor(zb[:, :, :], zg[:, :, :], across(C["b3"], TILES), ALU.add).then_inc(zb_done, 1)

            two_halves(pool, NG, prep, step)

        @block.scalar
        def _(act):
            def prep(g, s):
                act.wait_ge(yT_ready, nth(g))
                nc.scalar.copy(yT[:, s], XB[s]).then_inc(yT_copied, 1)

            def step(g, s, more):
                for c in range(F):
                    act.wait_ge(h_ready, nth(g, F, c))
                    if c == 0:
                        act.wait_ge(out_ready, g)
                    nc.scalar.activation(hT[:, c], HB[c], ACT.Relu, bias=b1[:, c:c + 1]).then_inc(relu_done, 1)
                if more:
                    prep(g + 1, 1 - s)

            two_halves(act, NG, prep, step)

        @block.tensor
        def _(pe):
            def prep(g, s):
                pe.wait_ge(yn_ready, nth(g))
                for t in range(TILES):
                    last = nc.tensor.transpose(XB[s][:, t * P:(t + 1) * P], yn[:, s, t, :], C["ident"])
                last.then_inc(yT_ready, 1)

            def step(g, s, more):
                pe.wait_ge(yT_copied, nth(g))
                pe.wait_ge(relu_done, g * F)
                for c in range(F):
                    nc.tensor.matmul(HB[c], w1[:, c], yT[:, s], start=True, stop=True).then_inc(h_ready, 1)
                if more:
                    prep(g + 1, 1 - s)
                pe.wait_ge(relu_done, nth(g, F, F - 1))
                for t in range(TILES):
                    for c in range(F):
                        last = nc.tensor.matmul(OUTB[s][:, t * D:(t + 1) * D], hT[:, c, t * P:(t + 1) * P], w2[:, c],
                                                start=(c == 0), stop=(c == F - 1))
                last.then_inc(out_ready, 1)

            two_halves(pe, NG, prep, step)

        @block.vector
        def _(dve):
            def step(g, s, more):
                dve.wait_ge(out_ready, nth(g))
                dve.wait_ge(yb_ready, nth(g))
                nc.vector.tensor_tensor(t1[:, :, :], OUTB[s].rearrange("p (t d) -> p t d", d=D), yb[:, :, :], ALU.add
                                        ).then_inc(summed, 1)
                dve.wait_ge(summed, nth(g))
                for t in range(TILES):
                    last = nc.vector.bn_stats(st[:, t, :], t1[:, t, :])
                last.then_inc(stats_done, 1)
                dve.wait_ge(stats_done, g + 1)
                dve.sem_inc(passed, 1)
                for t in range(TILES):
                    last = nc.vector.bn_aggr(mv[:, t, :], st[:, t, :])
                last.then_inc(moments, 1)
                dve.wait_ge(std_done, nth(g))
                nc.vector.tensor_scalar(se[:, :], sd[:, :], EPS, None, ALU.add).then_inc(std_eps, 1)
                dve.wait_ge(std_eps, nth(g))
                nc.vector.reciprocal(rs[:, :], se[:, :]).then_inc(rstd_done, 1)
                dve.wait_ge(rstd_done, nth(g))
                for t in range(TILES):
                    last = nc.vector.tensor_scalar(z[:, t, :], t1[:, t, :], mv[:, t, 0:1], rs[:, t:t + 1],
                                                   ALU.subtract, ALU.mult)
                last.then_inc(z_done, 1)
                dve.wait_ge(zb_done, nth(g))
                xs = tiles_of(x_res, g)
                nc.vector.tensor_tensor(xs, zb[:, :, :], xs, ALU.add).then_inc(x_done, 1)

            two_halves(dve, NG, lambda g, s: None, step)


def experts_phase(nc, ps, C, x_res, gate_in, up_in, down_in, out):
    E, SH = 16, 2
    K = E + SH
    with ExitStack() as ctx:
        def sb(name, shape, dt=F32):
            return ctx.enter_context(nc.sbuf_tensor("moe_" + name, shape, dt))

        sem = ctx.enter_context(Signals(nc, "moe_"))

        gate = sb("gate", [P, K, D])
        up = sb("up", [P, K, D])
        down = sb("down", [P, K, D])
        xn = sb("xn", [P, 2, TILES, D])
        xnT = sb("xnT", [P, 2, TOK])
        stats = sb("stats", [P, TILES, 6])
        mv = sb("mv", [P, TILES, 2])
        veps = sb("veps", [P, TILES])
        rstd = sb("rstd", [P, TILES])
        sg = sb("sg", [P, 2, TOK])
        act_ = sb("act", [P, 2, TOK])
        acc = sb("acc", [P, 2, TILES, D])
        TE = TILES * E
        ex = sb("ex", [P, TE])
        one_ex = sb("one_ex", [P, TE])
        score = sb("score", [P, TE])
        biased = sb("biased", [P, TE])
        hi2 = sb("hi2", [P, TE // 2])
        lo2 = sb("lo2", [P, TE // 2])
        top = sb("top", [P, TILES * 4])
        mid = sb("mid", [P, TILES * 4])
        low = sb("low", [P, TILES * 4])
        sec = sb("sec", [P, TILES * 4])
        gsc = sb("gsc", [P, TILES * 4])
        ggt = sb("ggt", [P, TILES * 4 * 4])
        geq = sb("geq", [P, TILES * 4 * 4])
        gtie = sb("gtie", [P, TILES * 4 * 4])
        gall = sb("gall", [P, TILES * 4 * 4])
        grank = sb("grank", [P, TILES * 4])
        gin = sb("gin", [P, TILES * 4])
        gout = sb("gout", [P, TILES * 4])
        kept = sb("kept", [P, TE])
        masked = sb("masked", [P, TE])
        egt = sb("egt", [P, TILES, E, E])
        eeq = sb("eeq", [P, TILES, E, E])
        rank = sb("rank", [P, TE])
        w = sb("w", [P, TE])
        wsum = sb("wsum", [P, TILES])
        wsume = sb("wsume", [P, TILES])
        winv = sb("winv", [P, TILES])
        comb = sb("comb", [P, 2, TILES, E])

        GB_ = [ps[:, i, :] for i in (0, 1)]
        UB = [ps[:, i, :] for i in (2, 3)]
        YB = [ps[:, i, :] for i in (4, 5)]
        XB = ps[:, 6, :]
        RB = ps[:, 7, 0:TE]
        CH = 3
        w_loaded = [sem(f"w_loaded{i}") for i in range(K // CH)]
        stats_done = sem("stats_done")
        moments = sem("moments")
        var_eps = sem("var_eps")
        rstd_done = sem("rstd_done")
        xn_ready = sem("xn_ready")
        xT_ready = sem("xT_ready")
        xT_copied = sem("xT_copied")
        logits_ready = sem("logits_ready")
        exp_done = sem("exp_done")
        NR = 29
        routing = sem("routing")
        comb_ready = sem("comb_ready")
        g_ready = sem("g_ready")
        u_ready = sem("u_ready")
        silu_done = sem("silu_done")
        act_ready = sem("act_ready")
        y_ready = sem("y_ready")
        acc_done = sem("acc_done")
        stored = [sem(f"stored{s}_") for s in (0, 1)]
        passed = sem("passed")
        block = ctx.enter_context(nc.Block())

        @block.sync
        def _(sp):
            for i in range(K // CH):
                part = slice(i * CH, (i + 1) * CH)
                sp.dma_start(gate[:, part, :], gate_in[:, part, :]).then_inc(w_loaded[i], 16)
                sp.dma_start(up[:, part, :], up_in[:, part, :]).then_inc(w_loaded[i], 16)
                sp.dma_start(down[:, part, :], down_in[:, part, :]).then_inc(w_loaded[i], 16)
            for s in (0, 1):
                sp.sem_inc(stored[s], 1)
            with sp.Fori(0, NG // 2) as i:
                for s in (0, 1):
                    g = i * 2 + s
                    sp.wait_ge(acc_done, nth(g, K - 1, K - 2))
                    sp.dma_start(out[bass.ds(g * TOK, TOK), :].rearrange("(t p) d -> p t d", p=P), acc[:, s]
                                 ).then_inc(stored[s], 16)
            for s in (0, 1):
                sp.wait_ge(stored[s], 16 * (NG // 2) + 1)

        @block.gpsimd
        def _(pool):
            def prep(g, s):
                pool.wait_ge(var_eps, nth(g))
                nc.gpsimd.tensor_tensor(rstd[:, :], veps[:, :], C["mhalf"][:, 0:TILES], ALU.pow).then_inc(rstd_done, 1)

            two_halves(pool, NG, prep, lambda g, s, more: prep(g + 1, 1 - s) if more else None)

        @block.scalar
        def _(act):
            def copy_xT(g, s):
                act.wait_ge(xT_ready, nth(g))
                nc.scalar.copy(xnT[:, s], XB).then_inc(xT_copied, 1)

            def route_exp(g, s):
                act.wait_ge(logits_ready, nth(g))
                nc.scalar.activation(ex[:, :], RB, ACT.Exp, scale=-1.0).then_inc(exp_done, 1)

            def prep(g, s):
                copy_xT(g, s)
                route_exp(g, s)

            def step(g, s, more):
                for k in range(K):
                    act.wait_ge(g_ready, nth(g, K, k))
                    nc.scalar.activation(sg[:, k % 2], GB_[k % 2], ACT.Silu).then_inc(silu_done, 1)
                    if more and k == 6:
                        copy_xT(g + 1, 1 - s)
                    if more and k == 8:
                        route_exp(g + 1, 1 - s)

            two_halves(act, NG, prep, step)

        @block.tensor
        def _(pe):
            def make_xT(g, s):
                pe.wait_ge(xn_ready, nth(g))
                for t in range(TILES):
                    last = nc.tensor.transpose(XB[:, t * P:(t + 1) * P], xn[:, s, t, :], C["ident"])
                last.then_inc(xT_ready, 1)

            def logits(g, s):
                pe.wait_ge(xT_copied, nth(g))
                for t in range(TILES):
                    last = nc.tensor.matmul(RB[:, t * E:(t + 1) * E], xnT[:, s, t * P:(t + 1) * P], C["router"],
                                            start=True, stop=True)
                last.then_inc(logits_ready, 1)

            def prep(g, s):
                make_xT(g, s)
                logits(g, s)

            def down_proj(g, k):
                pe.wait_ge(act_ready, nth(g, K, k))
                if k >= SH:
                    if k >= SH + 1:
                        pe.wait_ge(acc_done, nth(g, K - 1, k - SH - 1))
                    for t in range(TILES):
                        last = nc.tensor.matmul(YB[k % 2][:, t * D:(t + 1) * D], act_[:, k % 2, t * P:(t + 1) * P],
                                                down[:, k, :], start=True, stop=True)
                    last.then_inc(y_ready, 1)
                elif k == SH - 1:
                    pe.wait_ge(acc_done, g * (K - 1))
                    for t in range(TILES):
                        for j in range(SH):
                            last = nc.tensor.matmul(YB[1][:, t * D:(t + 1) * D], act_[:, j, t * P:(t + 1) * P],
                                                    down[:, j, :], start=(j == 0), stop=(j == SH - 1))
                    last.then_inc(y_ready, 1)

            def step(g, s, more):
                pe.wait_ge(xT_copied, nth(g))
                for k in range(K + 1):
                    if k < K:
                        if isinstance(g, int) and g == 0 or k % CH == 0:
                            pe.wait_ge(w_loaded[k // CH], 48)
                        if k >= 2:
                            pe.wait_ge(act_ready, nth(g, K, k - 2))
                        else:
                            pe.wait_ge(act_ready, g * K)
                        nc.tensor.matmul(GB_[k % 2], gate[:, k], xnT[:, s], start=True, stop=True).then_inc(g_ready, 1)
                        nc.tensor.matmul(UB[k % 2], up[:, k], xnT[:, s], start=True, stop=True).then_inc(u_ready, 1)
                    if k >= 1:
                        down_proj(g, k - 1)
                    if more and k == 6:
                        make_xT(g + 1, 1 - s)
                    if more and k == 8:
                        logits(g + 1, 1 - s)

            two_halves(pe, NG, prep, step)

        @block.vector
        def _(dve):
            V = nc.vector

            def norm_stats(g, s):
                for t in range(TILES):
                    last = V.bn_stats(stats[:, t, :], tiles_of(x_res, g, t, 1))
                last.then_inc(stats_done, 1)
                dve.wait_ge(stats_done, g + 1)
                dve.sem_inc(passed, 1)
                for t in range(TILES):
                    last = V.bn_aggr(mv[:, t, :], stats[:, t, :])
                last.then_inc(moments, 1)
                dve.wait_ge(moments, nth(g))
                V.tensor_scalar(veps[:, :], mv[:, :, 1], EPS, None, ALU.add).then_inc(var_eps, 1)

            def norm_apply(g, s):
                dve.wait_ge(rstd_done, nth(g))
                for t in range(TILES):
                    last = V.tensor_scalar(xn[:, s, t:t + 1, :], tiles_of(x_res, g, t, 1), mv[:, t, 0:1],
                                           rstd[:, t:t + 1], ALU.subtract, ALU.mult)
                last.then_inc(xn_ready, 1)

            def g4(t):
                return t[:, :].rearrange("p (t g) -> p t g", t=TILES)

            def groups_of(t):
                return t[:, :].rearrange("p (n c) -> p n c", c=4)

            def pairs(t, k):
                return t[:, :].rearrange("p (n c) -> p n c", c=2)[:, :, k]

            def route(g, s, parts):
                TG = TILES * 4

                def ge4(t):
                    return t[:, :].rearrange("p (n g j) -> p n g j", g=4, j=4)

                inner = lambda t: g4(t).unsqueeze(3).broadcast_to((P, TILES, 4, 4))
                other = lambda t: g4(t).unsqueeze(2).broadcast_to((P, TILES, 4, 4))
                t16 = lambda t: t[:, :].rearrange("p (t e) -> p t e", e=E)
                einner = lambda t: t16(t).unsqueeze(3).broadcast_to((P, TILES, E, E))
                eother = lambda t: t16(t).unsqueeze(2).broadcast_to((P, TILES, E, E))
                spread = lambda t: t[:, :].unsqueeze(2).broadcast_to((P, TG, 4))
                glow = C["glowmask"].rearrange("p (g j) -> p g j", j=4).unsqueeze(1).broadcast_to((P, TILES, 4, 4))
                elow = C["lowmask"].unsqueeze(1).broadcast_to((P, TILES, E * E))
                flat = lambda t: t[:, :, :, :].rearrange("p t e j -> p t (e j)")
                def before(n):
                    return nth(g, NR, n - 1)

                if 0 in parts:
                    dve.wait_ge(exp_done, nth(g))
                    V.tensor_scalar(one_ex[:, :], ex[:, :], 1.0, None, ALU.add).then_inc(routing, 1)
                    dve.wait_ge(routing, before(1))
                    V.reciprocal(score[:, :], one_ex[:, :]).then_inc(routing, 1)
                    dve.wait_ge(routing, before(2))
                    V.tensor_tensor(biased[:, :], score[:, :], C["rbias"], ALU.add).then_inc(routing, 1)
                    dve.wait_ge(routing, before(3))
                    V.tensor_tensor(hi2[:, :], pairs(biased, 0), pairs(biased, 1), ALU.max).then_inc(routing, 1)
                if 1 in parts:
                    dve.wait_ge(routing, before(4))
                    V.tensor_tensor(lo2[:, :], pairs(biased, 0), pairs(biased, 1), ALU.min).then_inc(routing, 1)
                    dve.wait_ge(routing, before(5))
                    V.tensor_tensor(top[:, :], pairs(hi2, 0), pairs(hi2, 1), ALU.max).then_inc(routing, 1)
                    dve.wait_ge(routing, before(6))
                    V.tensor_tensor(mid[:, :], pairs(hi2, 0), pairs(hi2, 1), ALU.min).then_inc(routing, 1)
                    dve.wait_ge(routing, before(7))
                    V.tensor_tensor(low[:, :], pairs(lo2, 0), pairs(lo2, 1), ALU.max).then_inc(routing, 1)
                if 2 in parts:
                    dve.wait_ge(routing, before(8))
                    V.tensor_tensor(sec[:, :], mid[:, :], low[:, :], ALU.max).then_inc(routing, 1)
                    dve.wait_ge(routing, before(9))
                    V.tensor_tensor(gsc[:, :], top[:, :], sec[:, :], ALU.add).then_inc(routing, 1)
                    dve.wait_ge(routing, before(10))
                    V.tensor_tensor(ge4(ggt), other(gsc), inner(gsc), ALU.is_gt).then_inc(routing, 1)
                    dve.wait_ge(routing, before(11))
                    V.tensor_tensor(ge4(geq), other(gsc), inner(gsc), ALU.is_equal).then_inc(routing, 1)
                if 3 in parts:
                    dve.wait_ge(routing, before(12))
                    V.tensor_tensor(ge4(gtie), ge4(geq), glow, ALU.mult).then_inc(routing, 1)
                    dve.wait_ge(routing, before(13))
                    V.tensor_tensor(gall[:, :], ggt[:, :], gtie[:, :], ALU.add).then_inc(routing, 1)
                    dve.wait_ge(routing, before(14))
                    V.tensor_reduce(grank[:, :], groups_of(gall), AX.X, ALU.add).then_inc(routing, 1)
                    dve.wait_ge(routing, before(15))
                    V.tensor_scalar(gin[:, :], grank[:, :], 2.0, None, ALU.is_lt).then_inc(routing, 1)
                if 4 in parts:
                    dve.wait_ge(routing, before(16))
                    V.tensor_scalar(gout[:, :], gin[:, :], -1.0, None, ALU.add).then_inc(routing, 1)
                    dve.wait_ge(routing, before(17))
                    V.tensor_tensor(groups_of(kept), groups_of(biased), spread(gin), ALU.mult).then_inc(routing, 1)
                    dve.wait_ge(routing, before(18))
                    V.tensor_tensor(groups_of(masked), groups_of(kept), spread(gout), ALU.add).then_inc(routing, 1)
                    dve.wait_ge(routing, before(19))
                    V.tensor_tensor(egt[:, :, :, :], eother(masked), einner(masked), ALU.is_gt).then_inc(routing, 1)
                if 5 in parts:
                    dve.wait_ge(routing, before(20))
                    V.tensor_tensor(eeq[:, :, :, :], eother(masked), einner(masked), ALU.is_equal).then_inc(routing, 1)
                    dve.wait_ge(routing, before(21))
                    V.tensor_tensor(flat(eeq), flat(eeq), elow, ALU.mult).then_inc(routing, 1)
                    dve.wait_ge(routing, before(22))
                    V.tensor_tensor(flat(egt), flat(egt), flat(eeq), ALU.add).then_inc(routing, 1)
                    dve.wait_ge(routing, before(23))
                    V.tensor_reduce(rank[:, :], egt[:, :, :, :].rearrange("p t e j -> p (t e) j"), AX.X,
                                    ALU.add).then_inc(routing, 1)
                if 6 in parts:
                    dve.wait_ge(routing, before(24))
                    V.scalar_tensor_tensor(w[:, :], rank[:, :], 4.0, score[:, :], ALU.is_lt,
                                           ALU.mult).then_inc(routing, 1)
                    dve.wait_ge(routing, before(25))
                    V.tensor_reduce(wsum[:, :], t16(w), AX.X, ALU.add).then_inc(routing, 1)
                    dve.wait_ge(routing, before(26))
                    V.tensor_scalar(wsume[:, :], wsum[:, :], 1e-20, None, ALU.add).then_inc(routing, 1)
                    dve.wait_ge(routing, before(27))
                    V.reciprocal(winv[:, :], wsume[:, :]).then_inc(routing, 1)
                if 7 in parts:
                    dve.wait_ge(routing, before(28))
                    V.scalar_tensor_tensor(comb[:, s], t16(w), 2.5, winv[:, :].unsqueeze(2).broadcast_to((P, TILES, E)), ALU.mult,
                                           ALU.mult).then_inc(routing, 1)

            def prep(g, s):
                norm_stats(g, s)
                norm_apply(g, s)
                route(g, s, range(8))

            def product(g, k):
                dve.wait_ge(u_ready, nth(g, K, k))
                dve.wait_ge(silu_done, nth(g, K, k))
                if k >= SH + 2:
                    dve.wait_ge(y_ready, nth(g, K - 1, k - SH - 1))
                elif k >= 2:
                    dve.wait_ge(y_ready, nth(g, K - 1, 0))
                else:
                    dve.wait_ge(y_ready, g * (K - 1))
                V.tensor_tensor(act_[:, k % 2], UB[k % 2], sg[:, k % 2], ALU.mult).then_inc(act_ready, 1)

            def accumulate(g, s, k):
                if k < SH - 1:
                    return
                n = k - SH + 1
                dve.wait_ge(y_ready, nth(g, K - 1, n))
                y = YB[k % 2].rearrange("p (t d) -> p t d", d=D)
                if n == 0:
                    dve.wait_ge(stored[s], g * 8 + (1 - 8 * s))
                    V.tensor_tensor(acc[:, s], y, tiles_of(x_res, g), ALU.add).then_inc(acc_done, 1)
                    return
                dve.wait_ge(acc_done, nth(g, K - 1, n - 1))
                if n == 1:
                    dve.wait_ge(routing, nth(g, NR, NR - 1))
                for t in range(TILES):
                    last = V.scalar_tensor_tensor(acc[:, s, t], y[:, t], comb[:, s, t, k - SH:k - SH + 1], acc[:, s, t],
                                                  ALU.mult, ALU.add)
                last.then_inc(acc_done, 1)

            def step(g, s, more):
                for k in range(K + 1):
                    if k < K:
                        product(g, k)
                    if k >= 1:
                        accumulate(g, s, k - 1)
                    if more and k == 3:
                        norm_stats(g + 1, 1 - s)
                    if more and k == 4:
                        norm_apply(g + 1, 1 - s)
                    if more and k >= 10:
                        route(g + 1, 1 - s, [k - 10])

            two_halves(dve, NG, prep, step)


def choice_phase(nc, ps, C, x_res, wqkv_in, woe_in):
    E, KC = 8, 8
    GT = 8
    NB = 2 * GT
    N = BATCH // NB
    ASCALE = float(D) ** -0.5

    with ExitStack() as ctx:
        def sb(name, shape, dt=F32):
            return ctx.enter_context(nc.sbuf_tensor("ch_" + name, shape, dt))

        sem = ctx.enter_context(Signals(nc, "ch_"))

        wqkv = sb("wqkv", [P, E, 3 * D])
        woe = sb("woe", [P, E, D])
        xn = sb("xn", [P, GT, D])
        stats = sb("stats", [P, GT, 6])
        mv = sb("mv", [P, GT, 2])
        veps = sb("veps", [P, GT])
        rstd = sb("rstd", [P, GT])
        xnT = sb("xnT", [P, GT * P])
        ex = sb("ex", [P, 4 * S])
        ex1 = sb("ex1", [P, 4 * S])
        gatev = sb("gatev", [P, 4 * S])
        m8 = sb("m8", [P, 4, 8])
        gt = sb("gt", [P, 4 * S])
        eq = sb("eq", [P, 4 * S])
        ngt = sb("ngt", [P, 4])
        ceq = sb("ceq", [P, 4 * S])
        tot = sb("tot", [P, 4 * S])
        tied = sb("tied", [P, 4 * S])
        chosen = sb("chosen", [P, 4 * S])
        count = sb("count", [P, 4 * S])
        slot = sb("slot", [P, 4 * S])
        slotT = sb("slotT", [P, GT, E])
        gateT = sb("gateT", [P, GT, E])
        pick = sb("pick", [P, GT, 2, E * KC])
        pickw = sb("pickw", [P, GT, 2, E * KC])
        trigT = sb("trigT", [P, E, NB, KC])
        xg = sb("xg", [P, 2, E, NB, KC])
        trig = sb("trig", [P, 2, E, P])
        pickT = sb("pickT", [P, 2, GT, P])
        qkv = sb("qkv", [P, E, 3, D])
        rot1 = sb("rot1", [P, 2, 4, 2, 64])
        rot2 = sb("rot2", [P, 2, 4, 2, 64])
        qT = sb("qT", [P, 2, 4 * P])
        kT = sb("kT", [P, 2, 4 * P])
        sm = sb("sm", [P, 2, 4, P])
        mx = sb("mx", [P, 2, 4])
        dif = sb("dif", [P, 2, 4, P])
        pe_ = sb("pe", [P, 2, 4, P])
        sums = sb("sums", [P, 2, 4])
        inv = sb("inv", [P, 2, 4])
        prob = sb("prob", [P, 2, 4, P])
        probT = sb("probT", [P, 2, 4, P])
        avT = sb("avT", [P, 2, 4, P])
        xpT = sb("xpT", [P, NB, E, KC])
        xp = sb("xp", [P, GT, D])

        def prep_bank(n):
            return ps[:, n % 2, :]

        def bank(n):
            return ps[:, 2 + n % 6, :]

        w_loaded = sem("w_loaded")
        pick_set = sem("pick_set")
        stats_done = sem("stats_done")
        moments = sem("moments")
        var_eps = sem("var_eps")
        rstd_done = sem("rstd_done")
        xn_ready = sem("xn_ready")
        NP = 13
        prep_ready = sem("prep_ready")
        prep_copied = sem("prep_copied")
        NC = 12
        choosing = sem("choosing")
        pick_ready = sem("pick_ready")
        pickw_ready = sem("pickw_ready")
        qkv_ready = sem("qkv_ready")
        qkv_copied = sem("qkv_copied")
        rotated1 = sem("rotated1")
        rotated2 = sem("rotated2")
        rotated = sem("rotated")
        qkT_ready = sem("qkT_ready")
        qkT_copied = sem("qkT_copied")
        s_ready = sem("s_ready")
        s_masked = sem("s_masked")
        max_done = sem("max_done")
        shifted = sem("shifted")
        e_ready = sem("e_ready")
        sum_done = sem("sum_done")
        inv_done = sem("inv_done")
        prob_ready = sem("prob_ready")
        probT_ready = sem("probT_ready")
        probT_copied = sem("probT_copied")
        av_ready = sem("av_ready")
        av_copied = sem("av_copied")
        xpT_ready = sem("xpT_ready")
        xpT_copied = sem("xpT_copied")
        xp_ready = sem("xp_ready")
        xp_copied = sem("xp_copied")
        out_ready = sem("out_ready")
        out_added = sem("out_added")

        def tiles(g, k=0, n=GT):
            return x_res[:, bass.ds(g * GT + k, n), :]

        passed = sem("passed")
        block = ctx.enter_context(nc.Block())

        @block.sync
        def _(sp):
            sp.dma_start(wqkv[:, :, :], wqkv_in).then_inc(w_loaded, 16)
            sp.dma_start(woe[:, :, :], woe_in).then_inc(w_loaded, 16)

        @block.gpsimd
        def _(pool):
            def prep(g, s):
                pool.wait_ge(var_eps, nth(g))
                nc.gpsimd.tensor_tensor(rstd[:, :], veps[:, :], C["mhalf"][:, :], ALU.pow).then_inc(rstd_done, 1)

            two_halves(pool, N, prep, lambda g, s, more: prep(g + 1, 1 - s) if more else None)

        @block.tensor
        def _(pe):
            def transpose4(out, tiles4, width=P):
                for n, t in enumerate(tiles4):
                    last = nc.tensor.transpose(out[0:width, n * P:(n + 1) * P], t, C["ident"])
                return last

            def round_(g, n):
                if n >= 2:
                    pe.wait_ge(prep_copied, nth(g, NP, n - 2))

            def make_xT(g, s):
                pe.wait_ge(xn_ready, nth(g))
                pe.wait_ge(prep_copied, g * NP)
                for n in (0, 1):
                    transpose4(prep_bank(n), [xn[:, 4 * n + t, :] for t in range(4)]).then_inc(prep_ready, 1)

            def make_logits(g, s):
                pe.wait_ge(prep_copied, nth(g, NP, 1))
                for q in range(4):
                    last = nc.tensor.matmul(prep_bank(2)[32 * q:32 * q + 32, 0:4 * S], C["wr"],
                                            xnT[:, :].rearrange("p (r q k) -> p q r k", q=4, k=S)[:, q],
                                            start=True, stop=True)
                last.then_inc(prep_ready, 1)

            def make_token_rows(g, s):
                pe.wait_ge(choosing, (g + 1) * NC)
                pe.wait_ge(prep_copied, g * NP + 2)
                pe.sem_inc(passed, 1)
                transpose4(prep_bank(3), [slot[:, r * S:(r + 1) * S] for r in range(4)], S).then_inc(prep_ready, 1)
                pe.wait_ge(prep_copied, g * NP + 3)
                pe.sem_inc(passed, 1)
                transpose4(prep_bank(4), [gatev[:, r * S:(r + 1) * S] for r in range(4)], S).then_inc(prep_ready, 1)

            def make_gathered(g, s):
                pe.wait_ge(pick_ready, nth(g))
                for n in (5, 6):
                    round_(g, n)
                    for t in range(4):
                        last = nc.tensor.matmul(prep_bank(n)[:, t * P:(t + 1) * P], xn[:, 4 * (n - 5) + t, :],
                                                pick[:, 4 * (n - 5) + t].rearrange("p b n -> p (b n)"),
                                                start=True, stop=True)
                    last.then_inc(prep_ready, 1)

            def make_trig(g, s):
                for n in (7, 8):
                    round_(g, n)
                    for t in range(4):
                        last = nc.tensor.matmul(prep_bank(n)[:, t * P:(t + 1) * P], C["trig"],
                                                pick[:, 4 * (n - 7) + t].rearrange("p b n -> p (b n)"),
                                                start=True, stop=True)
                    last.then_inc(prep_ready, 1)
                for n in (9, 10):
                    pe.wait_ge(prep_copied, nth(g, NP, 8))
                    round_(g, n)
                    transpose4(prep_bank(n), [trigT[:, 4 * (n - 9) + e].rearrange("p b k -> p (b k)") for e in range(4)]
                               ).then_inc(prep_ready, 1)

            def make_pickT(g, s):
                pe.wait_ge(pickw_ready, nth(g))
                for n in (11, 12):
                    round_(g, n)
                    transpose4(prep_bank(n), [pickw[:, 4 * (n - 11) + t].rearrange("p b n -> p (b n)") for t in range(4)]
                               ).then_inc(prep_ready, 1)

            def prep(g, s):
                make_xT(g, s)
                make_logits(g, s)
                make_token_rows(g, s)
                make_gathered(g, s)
                make_trig(g, s)
                make_pickT(g, s)

            def make_qkv(g, s, h):
                for e in range(4):
                    nc.tensor.matmul(bank(6 * h + e)[:, 0:3 * D], xg[:, s, 4 * h + e].rearrange("p b k -> p (b k)"),
                                     wqkv[:, 4 * h + e, :], start=True, stop=True).then_inc(qkv_ready, 1)

            def make_qkT(g, s, h):
                pe.wait_ge(rotated, nth(g, 2, h))
                if h == 0:
                    pe.wait_ge(out_added, g * 2)
                else:
                    pe.wait_ge(qkT_copied, nth(g, 2, 0))
                for n in (0, 1):
                    last = transpose4(bank(4 + 6 * h + n), [qkv[:, 4 * h + e, n, :] for e in range(4)])
                last.then_inc(qkT_ready, 1)

            def make_scores(g, s, h):
                pe.wait_ge(qkT_copied, nth(g, 2, h))
                for e in range(4):
                    cols = slice(e * P, (e + 1) * P)
                    last = nc.tensor.matmul(bank(12 + h)[:, cols], qT[:, h, cols], kT[:, h, cols], start=True, stop=True)
                last.then_inc(s_ready, 1)

            def make_probT(g, s, h):
                pe.wait_ge(prob_ready, nth(g, 2, h))
                transpose4(bank(14 + h), [prob[:, h, e] for e in range(4)]).then_inc(probT_ready, 1)

            def make_av(g, s, h):
                pe.wait_ge(probT_copied, nth(g, 2, h))
                for e in range(4):
                    last = nc.tensor.matmul(bank(16 + h)[:, e * P:(e + 1) * P], qkv[:, 4 * h + e, 2, :], probT[:, h, e],
                                            start=True, stop=True)
                last.then_inc(av_ready, 1)

            def make_xpT(g, s, h):
                pe.wait_ge(av_copied, nth(g, 2, h))
                for e in range(4):
                    last = nc.tensor.matmul(bank(18 + h)[:, e * P:(e + 1) * P], woe[:, 4 * h + e, :], avT[:, h, e],
                                            start=True, stop=True)
                last.then_inc(xpT_ready, 1)

            def make_xp(g, s):
                pe.wait_ge(xpT_copied, nth(g, 2, 1))
                for n in (0, 1):
                    transpose4(bank(20 + n), [xpT[:, 2 * (4 * n + t):2 * (4 * n + t) + 2].rearrange("p b e k -> p (b e k)")
                                              for t in range(4)]).then_inc(xp_ready, 1)

            def make_out(g, s):
                for n in (0, 1):
                    pe.wait_ge(xp_copied, nth(g, 2, n))
                    for t in range(4):
                        last = nc.tensor.matmul(bank(22 + n)[:, t * D:(t + 1) * D], pickT[:, s, 4 * n + t], xp[:, 4 * n + t],
                                                start=True, stop=True)
                    last.then_inc(out_ready, 1)

            def step(g, s, more):
                make_qkv(g, s, 0)
                if more:
                    make_xT(g + 1, 1 - s)
                make_qkT(g, s, 0)
                make_qkv(g, s, 1)
                if more:
                    make_logits(g + 1, 1 - s)
                make_qkT(g, s, 1)
                make_scores(g, s, 0)
                make_scores(g, s, 1)
                make_probT(g, s, 0)
                make_probT(g, s, 1)
                make_av(g, s, 0)
                make_av(g, s, 1)
                make_xpT(g, s, 0)
                make_xpT(g, s, 1)
                if more:
                    make_token_rows(g + 1, 1 - s)
                make_xp(g, s)
                if more:
                    make_gathered(g + 1, 1 - s)
                make_out(g, s)
                if more:
                    make_trig(g + 1, 1 - s)
                    make_pickT(g + 1, 1 - s)

            pe.wait_ge(w_loaded, 32)
            two_halves(pe, N, prep, step)

        @block.scalar
        def _(act):
            A = nc.scalar

            def copy_round(g, n, out, rows=P):
                act.wait_ge(prep_ready, nth(g, NP, n))
                return A.copy(out, prep_bank(n)[0:rows, :])

            def prep_front(g, s):
                for n in (0, 1):
                    copy_round(g, n, xnT[:, n * 512:(n + 1) * 512]).then_inc(prep_copied, 1)

            def prep_exp(g, s):
                act.wait_ge(prep_ready, nth(g, NP, 2))
                A.activation(ex[:, :], prep_bank(2)[:, 0:4 * S], ACT.Exp, scale=-1.0).then_inc(prep_copied, 1)

            def prep_token_rows(g, s):
                for n, dst in ((3, slotT), (4, gateT)):
                    act.wait_ge(prep_ready, nth(g, NP, n))
                    for bb in (0, 1):
                        last = A.copy(dst[64 * bb:64 * bb + 64, :, :],
                                      prep_bank(n)[0:S, :].rearrange("p (t b e) -> p t b e", b=2, e=32)[:, :, bb, 0:E])
                    last.then_inc(prep_copied, 1)

            def by_expert(dst, n):
                return dst.rearrange("p e b k -> p b e k")[:, 8 * n:8 * n + 8]

            def prep_gathered(g, s):
                for n in (5, 6):
                    act.wait_ge(prep_ready, nth(g, NP, n))
                    A.copy(by_expert(xg[:, s], n - 5), prep_bank(n).rearrange("p (b e k) -> p b e k", e=E, k=KC)
                           ).then_inc(prep_copied, 1)

            def prep_trig(g, s):
                for n in (7, 8):
                    act.wait_ge(prep_ready, nth(g, NP, n))
                    A.copy(by_expert(trigT[:, :, :, :], n - 7), prep_bank(n).rearrange("p (b e k) -> p b e k", e=E, k=KC)
                           ).then_inc(prep_copied, 1)
                for n in (9, 10):
                    copy_round(g, n, trig[:, s, 4 * (n - 9):4 * (n - 9) + 4].rearrange("p e n -> p (e n)")
                               ).then_inc(prep_copied, 1)
                for n in (11, 12):
                    copy_round(g, n, pickT[:, s, 4 * (n - 11):4 * (n - 11) + 4].rearrange("p t n -> p (t n)")
                               ).then_inc(prep_copied, 1)

            def prep(g, s):
                prep_front(g, s)
                prep_exp(g, s)
                prep_token_rows(g, s)
                prep_gathered(g, s)
                prep_trig(g, s)

            def copy_qkv(g, h):
                for e in range(4):
                    act.wait_ge(qkv_ready, nth(g, 8, 4 * h + e))
                    last = A.copy(qkv[:, 4 * h + e].rearrange("p c n -> p (c n)"), bank(6 * h + e)[:, 0:3 * D])
                    last.then_inc(qkv_copied, 1)

            def copy_qkT(g, h):
                act.wait_ge(qkT_ready, nth(g, 2, h))
                A.copy(qT[:, h], bank(4 + 6 * h))
                A.copy(kT[:, h], bank(5 + 6 * h)).then_inc(qkT_copied, 1)

            def exps(g, h):
                act.wait_ge(shifted, nth(g, 2, h))
                A.activation(pe_[:, h], dif[:, h], ACT.Exp, scale=ASCALE).then_inc(e_ready, 1)

            def copy4(g, h, ready, out, n, copied):
                act.wait_ge(ready, nth(g, 2, h))
                A.copy(out.rearrange("p e n -> p (e n)"), bank(n)).then_inc(copied, 1)

            def copy_xpT(g, h):
                act.wait_ge(xpT_ready, nth(g, 2, h))
                A.copy(xpT[:, :, :, :].rearrange("p b e k -> p e b k")[:, 4 * h:4 * h + 4],
                       bank(18 + h).rearrange("p (e b k) -> p e b k", e=4, k=KC)).then_inc(xpT_copied, 1)

            def step(g, s, more):
                copy_qkv(g, 0)
                if more:
                    prep_front(g + 1, 1 - s)
                copy_qkT(g, 0)
                copy_qkv(g, 1)
                if more:
                    prep_exp(g + 1, 1 - s)
                copy_qkT(g, 1)
                for h in (0, 1):
                    exps(g, h)
                for h in (0, 1):
                    copy4(g, h, probT_ready, probT[:, h], 14 + h, probT_copied)
                for h in (0, 1):
                    copy4(g, h, av_ready, avT[:, h], 16 + h, av_copied)
                for h in (0, 1):
                    copy_xpT(g, h)
                if more:
                    prep_token_rows(g + 1, 1 - s)
                for n in (0, 1):
                    copy4(g, n, xp_ready, xp[:, 4 * n:4 * n + 4], 20 + n, xp_copied)
                if more:
                    prep_gathered(g + 1, 1 - s)
                    prep_trig(g + 1, 1 - s)

            two_halves(act, N, prep, step)

        @block.vector
        def _(dve):
            V = nc.vector

            def norm(g, s):
                for t in range(GT):
                    last = V.bn_stats(stats[:, t, :], tiles(g, t, 1))
                last.then_inc(stats_done, 1)
                dve.wait_ge(stats_done, g + 1)
                dve.sem_inc(passed, 1)
                for t in range(GT):
                    last = V.bn_aggr(mv[:, t, :], stats[:, t, :])
                last.then_inc(moments, 1)
                dve.wait_ge(moments, nth(g))
                V.tensor_scalar(veps[:, :], mv[:, :, 1], EPS, None, ALU.add).then_inc(var_eps, 1)
                dve.wait_ge(rstd_done, nth(g))
                dve.wait_ge(prep_ready, g * NP)
                for t in range(GT):
                    last = V.tensor_scalar(xn[:, t:t + 1, :], tiles(g, t, 1), mv[:, t, 0:1], rstd[:, t:t + 1],
                                           ALU.subtract, ALU.mult)
                last.then_inc(xn_ready, 1)

            def choose(g, s):
                by_r = lambda t: t[:, :].rearrange("p (r k) -> p r k", k=S)
                wide = lambda t: t.unsqueeze(2).broadcast_to((P, 4, S))
                dve.wait_ge(prep_copied, nth(g, NP, 2))
                V.tensor_scalar(ex1[:, :], ex[:, :], 1.0, None, ALU.add).then_inc(choosing, 1)
                dve.wait_ge(choosing, nth(g, NC, 0))
                V.reciprocal(gatev[:, :], ex1[:, :]).then_inc(choosing, 1)
                dve.wait_ge(choosing, nth(g, NC, 1))
                dve.sem_inc(passed, 1)
                for r in range(4):
                    last = V.max(m8[:, r, :], gatev[:, r * S:(r + 1) * S])
                last.then_inc(choosing, 1)
                dve.wait_ge(choosing, nth(g, NC, 2))
                V.tensor_tensor(by_r(gt), by_r(gatev), wide(m8[:, :, 7]), ALU.is_gt).then_inc(choosing, 1)
                dve.wait_ge(choosing, nth(g, NC, 3))
                V.tensor_tensor(by_r(eq), by_r(gatev), wide(m8[:, :, 7]), ALU.is_equal).then_inc(choosing, 1)
                dve.wait_ge(choosing, nth(g, NC, 4))
                V.tensor_reduce(ngt[:, :], by_r(gt), AX.X, ALU.add).then_inc(choosing, 1)
                dve.wait_ge(choosing, nth(g, NC, 5))
                V.tensor_tensor_scan(ceq[:, :], C["resetmask"], eq[:, :], 0.0, ALU.mult, ALU.add).then_inc(choosing, 1)
                dve.wait_ge(choosing, nth(g, NC, 6))
                V.tensor_tensor(by_r(tot), by_r(ceq), wide(ngt[:, :]), ALU.add).then_inc(choosing, 1)
                dve.wait_ge(choosing, nth(g, NC, 7))
                V.scalar_tensor_tensor(tied[:, :], tot[:, :], float(KC), eq[:, :], ALU.is_le, ALU.mult).then_inc(choosing, 1)
                dve.wait_ge(choosing, nth(g, NC, 8))
                V.tensor_tensor(chosen[:, :], tied[:, :], gt[:, :], ALU.add).then_inc(choosing, 1)
                dve.wait_ge(choosing, nth(g, NC, 9))
                V.tensor_tensor_scan(count[:, :], C["resetmask"], chosen[:, :], 0.0, ALU.mult, ALU.add).then_inc(choosing, 1)
                dve.wait_ge(choosing, nth(g, NC, 10))
                V.tensor_tensor(slot[:, :], count[:, :], chosen[:, :], ALU.mult).then_inc(choosing, 1)

            def make_pick(g, s):
                dve.wait_ge(prep_copied, nth(g, NP, 4))
                iota = C["kiota"].rearrange("p (e k) -> p e k", k=KC).unsqueeze(1).broadcast_to((P, GT, E, KC))
                view = lambda t, b, r: t[r, :, b, :].rearrange("p t (e k) -> p t e k", k=KC)
                wide = lambda t, r: t[r].unsqueeze(3).broadcast_to((64, GT, E, KC))
                for b in (0, 1):
                    r = slice(64 * b, 64 * b + 64)
                    last = V.tensor_tensor(view(pick, b, r), wide(slotT, r), iota[r], ALU.is_equal)
                last.then_inc(pick_ready, 1)
                dve.wait_ge(pick_ready, nth(g))
                for b in (0, 1):
                    r = slice(64 * b, 64 * b + 64)
                    last = V.tensor_tensor(view(pickw, b, r), view(pick, b, r), wide(gateT, r), ALU.mult)
                last.then_inc(pickw_ready, 1)

            def prep(g, s):
                norm(g, s)
                choose(g, s)
                make_pick(g, s)

            def rotate(g, s, h):
                dve.wait_ge(qkv_copied, nth(g, 8, 4 * h + 3))
                es = slice(4 * h, 4 * h + 4)
                cos2 = trig[:, s, es, 0:64].unsqueeze(2).broadcast_to((P, 4, 2, 64))
                sins = [trig[:, s, es, 64 + 32 * j:96 + 32 * j].unsqueeze(2).broadcast_to((P, 4, 2, 32)) for j in (0, 1)]
                V.tensor_tensor(rot1[:, h], qkv[:, es, 0:2, 0:64], cos2, ALU.mult).then_inc(rotated1, 1)
                V.tensor_tensor(rot2[:, h, :, :, 0:32], qkv[:, es, 0:2, 32:64], sins[0], ALU.mult)
                V.tensor_tensor(rot2[:, h, :, :, 32:64], qkv[:, es, 0:2, 0:32], sins[1], ALU.mult).then_inc(rotated2, 1)
                dve.wait_ge(rotated1, nth(g, 2, h))
                dve.wait_ge(rotated2, nth(g, 2, h))
                V.tensor_tensor(qkv[:, es, 0:2, 0:64], rot1[:, h], rot2[:, h], ALU.add).then_inc(rotated, 1)

            def shift(g, h):
                dve.wait_ge(s_ready, nth(g, 2, h))
                V.tensor_tensor(sm[:, h], bank(12 + h).rearrange("p (e n) -> p e n", n=P),
                                C["negmask"].unsqueeze(1).broadcast_to((P, 4, P)), ALU.add).then_inc(s_masked, 1)
                dve.wait_ge(s_masked, nth(g, 2, h))
                V.tensor_reduce(mx[:, h], sm[:, h], AX.X, ALU.max).then_inc(max_done, 1)
                dve.wait_ge(max_done, nth(g, 2, h))
                V.tensor_tensor(dif[:, h], sm[:, h], mx[:, h].unsqueeze(2).broadcast_to((P, 4, P)), ALU.subtract
                                ).then_inc(shifted, 1)

            def normalise(g, h):
                dve.wait_ge(e_ready, nth(g, 2, h))
                V.tensor_reduce(sums[:, h], pe_[:, h], AX.X, ALU.add).then_inc(sum_done, 1)
                dve.wait_ge(sum_done, nth(g, 2, h))
                V.reciprocal(inv[:, h], sums[:, h]).then_inc(inv_done, 1)
                dve.wait_ge(inv_done, nth(g, 2, h))
                V.tensor_tensor(prob[:, h], pe_[:, h], inv[:, h].unsqueeze(2).broadcast_to((P, 4, P)), ALU.mult
                                ).then_inc(prob_ready, 1)

            def add_out(g, s):
                for n in (0, 1):
                    dve.wait_ge(out_ready, nth(g, 2, n))
                    xs = tiles(g, 4 * n, 4)
                    V.tensor_tensor(xs, bank(22 + n).rearrange("p (t d) -> p t d", d=D), xs, ALU.add
                                    ).then_inc(out_added, 1)

            def step(g, s, more):
                if more:
                    norm(g + 1, 1 - s)
                dve.wait_ge(prep_copied, nth(g, NP, 10))
                rotate(g, s, 0)
                rotate(g, s, 1)
                shift(g, 0)
                shift(g, 1)
                normalise(g, 0)
                normalise(g, 1)
                if more:
                    choose(g + 1, 1 - s)
                    make_pick(g + 1, 1 - s)
                add_out(g, s)

            V.memset(pick[:, :, :, :], 0.0)
            V.memset(pickw[:, :, :, :], 0.0).then_inc(pick_set, 1)
            dve.wait_ge(pick_set, 1)
            two_halves(dve, N, prep, step)


def setup_phase(nc, ps, C, pack_in, q_mask, pack, work):
    with ExitStack() as ctx:
        sem = ctx.enter_context(Signals(nc, "setup_"))

        pack_loaded = sem("pack_loaded")
        qmask_loaded = sem("qmask_loaded")
        consts_set = sem("consts_set")
        qbias_done = sem("qbias_done")
        qany_done = sem("qany_done")
        qscale_diag = sem("qscale_diag")
        qscale_ready = sem("qscale_ready")
        qscale_copied = sem("qscale_copied")
        block = ctx.enter_context(nc.Block())

        @block.sync
        def _(sp):
            sp.dma_start(pack[:, :], pack_in).then_inc(pack_loaded, 16)
            for r in (0, 1):
                sp.dma_start(work["qmi"][64 * r:64 * r + 64, :], q_mask).then_inc(qmask_loaded, 16)

        @block.tensor
        def _(pe):
            pe.wait_ge(qscale_diag, 1)
            nc.tensor.matmul(ps[:, 1, 0:64], work["ones"][0:64, :], work["diag"][0:64, :], start=True, stop=True
                             ).then_inc(qscale_ready, 1)

        @block.vector
        def _(dve):
            nc.vector.memset(C["mhalf"][:, :], -0.5)
            nc.vector.memset(C["half"][:, :], 0.5)
            nc.vector.memset(C["oneb"][0:64, 0:64], 1.0 / 64)
            nc.vector.memset(C["oneb"][0:64, 64:128], 0.0)
            nc.vector.memset(C["oneb"][64:128, 0:64], 0.0)
            nc.vector.memset(C["oneb"][64:128, 64:128], 1.0 / 64)
            nc.vector.memset(work["ones"][:, :], 1.0).then_inc(consts_set, 1)
            dve.wait_ge(pack_loaded, 16)
            for b in (0, 1):
                nc.vector.tensor_copy(C["identb"][:, S * b:S * b + S], C["ident"][0:S, 0:S]).then_inc(consts_set, 1)
            dve.wait_ge(qmask_loaded, 32)
            nc.vector.tensor_scalar(C["qmask"][:, :], work["qmi"][:, :], 0.0, NEG, ALU.is_equal, ALU.mult
                                    ).then_inc(qbias_done, 1)
            dve.wait_ge(qbias_done, 1)
            nc.vector.tensor_reduce(work["any"][:, 0:1], C["qmask"][:, :], AX.X, ALU.max).then_inc(qany_done, 1)
            dve.wait_ge(qany_done, 1)
            nc.vector.tensor_scalar(work["any"][:, 1:2], work["any"][:, 0:1], 0.0, SCALE, ALU.is_equal, ALU.mult
                                    ).then_inc(qany_done, 1)
            dve.wait_ge(qany_done, 2)
            nc.vector.tensor_scalar(work["diag"][0:64, :], C["ident"][0:64, 0:64], work["any"][0:64, 1:2], None, ALU.mult
                                    ).then_inc(qscale_diag, 1)
            dve.wait_ge(qscale_ready, 1)
            nc.vector.tensor_copy(C["qscale"][:, :], ps[:, 1, 0:64]).then_inc(qscale_copied, 1)


def build(nc, x_in, ctx_in, q_mask, key_mask, pack_in, wqkv_in, woe_in, gate_in, up_in, down_in, out):
    with ExitStack() as ctx:
        def sb(name, shape, dt=F32):
            return ctx.enter_context(nc.sbuf_tensor(name, shape, dt))

        ps = ctx.enter_context(nc.psum_tensor("ps", [P, 8, 512], F32))
        pack = sb("pack", [P, PACK])
        x_res = sb("x_res", [P, NG * TILES, D])
        C = {"pack": pack}
        for n, (at, w) in COLS.items():
            C[n] = pack[:, at:at + w]
        C["identb"] = sb("identb", [S, P], BF16)
        C["oneb"] = sb("oneb", [P, P], BF16)
        C["mhalf"] = sb("mhalf", [P, 8])
        C["half"] = sb("half", [P, 8])
        C["qmask"] = sb("qmask", [P, S], BF16)
        C["qscale"] = sb("qscale", [P, S])
        work = {"qmi": sb("qmi", [P, S], I32), "ones": sb("ones", [P, P]), "any": sb("qany", [P, 2]),
                "diag": sb("qdiag", [P, S])}
        setup_phase(nc, ps, C, pack_in, q_mask, pack, work)
        attention_phase(nc, ps, C, x_res, None, x_in, ctx_in, q_mask, key_mask, 0)
        choice_phase(nc, ps, C, x_res, wqkv_in, woe_in)
        y_res = sb("y_res", [P, NG * TILES, D])
        attention_phase(nc, ps, C, x_res, y_res, x_in, ctx_in, q_mask, key_mask, 1)
        attention_phase(nc, ps, C, x_res, y_res, x_in, ctx_in, q_mask, key_mask, 2)
        relu_phase(nc, ps, C, x_res, y_res)
        experts_phase(nc, ps, C, x_res, gate_in, up_in, down_in, out)


def kernel(**inputs):
    import concourse.bacc as bacc
    from concourse.bass_utils import run_bass_kernel_spmd

    a = {k: np.ascontiguousarray(v) for k, v in inputs.items()}
    pack = np.zeros((P, PACK), np.float32)

    def put(name, v, off=0):
        v = np.asarray(v, np.float32)
        v = v.reshape(v.shape[0], -1)
        at = COLS[name][0] + off
        pack[:v.shape[0], at:at + v.shape[1]] = v

    attn = [("L0_xattn_W{}", "L0_xattn_b{}", True), ("L1_xattn_sa_w{}", "L1_xattn_sa_b{}", False),
            ("L1_xattn_ca_w{}", "L1_xattn_ca_b{}", False)]
    for i, (w, b, flip) in enumerate(attn):
        for n, c in enumerate("qkv"):
            m = a[w.format(c)]
            put(f"a{i}", m.T if flip else m, n * D)
        m = a[w.format("o")]
        put(f"a{i}", m.T if flip else m, 3 * D)
        put(f"a{i}", np.broadcast_to(a[b.format("o")], (P, D)), 4 * D)
        for n, c in enumerate("qkv"):
            put(f"a{i}", a[b.format(c)][:, None], 5 * D + n)
    put("ident", np.eye(P))
    put("headmask", (np.arange(P)[:, None] // DH % HH == np.arange(HH)[None]) * 1.0)
    for n in ("g1", "b1", "g2", "b2", "g3", "b3"):
        put(n, np.broadcast_to(a["L1_xattn_" + n], (P, D)))
    put("wr", a["L0_ffn_Wr"].T)
    row = np.arange(P)
    put("negmask", np.where((row[:, None] // 8 == row // 8) & (row[:, None] >= row), 0.0, -1e30))
    put("kiota", np.broadcast_to(np.arange(64) % 8 + 1, (P, 64)))
    put("resetmask", np.broadcast_to(np.arange(256) % 64 > 0, (P, 256)))
    angle = ((row % S)[:, None].astype(np.float32)
             * (1.0 / 10000.0 ** (np.arange(32, dtype=np.float32) * 2.0 / 64)).astype(np.float32))
    put("trig", np.concatenate([np.cos(angle), np.cos(angle), -np.sin(angle), np.sin(angle)], 1))
    put("ff2b", np.broadcast_to(a["L1_xattn_ff_b2"], (P, D)))
    put("ff1", a["L1_xattn_ff_w1"])
    put("ff1b", a["L1_xattn_ff_b1"].reshape(4, P).T)
    put("ff2", a["L1_xattn_ff_w2"].reshape(4, P, D).transpose(1, 0, 2))
    put("router", a["L1_ffn_router_w"].T)
    put("rbias", np.broadcast_to(np.tile(a["L1_ffn_bias"], TILES), (P, 64)))
    put("lowmask", np.broadcast_to(np.tril(np.ones((16, 16)), -1).reshape(1, -1), (P, 256)))
    put("glowmask", np.broadcast_to(np.tril(np.ones((4, 4)), -1).reshape(1, -1), (P, 16)))

    def experts(name, shared):
        return np.concatenate([shared, a["L1_ffn_" + name]]).transpose(1, 0, 2).copy()

    arrays = {
        "x": a["x"].reshape(-1, D), "ctx": a["ctx_1024"].reshape(-1, D), "q_mask": a["mask_SxS2_ik0"],
        "key_mask": a["mask_Bx1x1xS2_if1"].reshape(BATCH, S), "pack": pack,
        "wqkv": a["L0_ffn_Wqkv"].transpose(1, 0, 2).copy(), "woe": a["L0_ffn_Wo"].transpose(1, 0, 2).copy(),
        "gate": experts("gate_w", a["L1_ffn_sh_gate_w"].reshape(D, 2, D).transpose(1, 0, 2)),
        "up": experts("up_w", a["L1_ffn_sh_up_w"].reshape(D, 2, D).transpose(1, 0, 2)),
        "down": experts("down_w", a["L1_ffn_sh_down_w"].reshape(2, D, D)),
    }
    nc = bacc.Bacc("TRN2", target_bir_lowering=False, num_devices=1)
    args = [nc.dram_tensor("in_" + n, v.shape, mybir.dt.from_np(v.dtype), kind="ExternalInput").ap() for n, v in arrays.items()]
    out = nc.dram_tensor("out", (BATCH * S, D), F32, kind="ExternalOutput").ap()
    build(nc, *args, out)
    r = run_bass_kernel_spmd(nc, [{"in_" + n: v for n, v in arrays.items()}], core_ids=[0])
    return r.results[0]["out"].reshape(BATCH, S, D)
```

```python
from contextlib import ExitStack

import numpy as np

import concourse.bass as bass
from concourse import mybir

F32 = mybir.dt.float32
BF16 = mybir.dt.bfloat16
I32 = mybir.dt.int32
F32R = mybir.dt.float32r
ALU = mybir.AluOpType
ACT = mybir.ActivationFunctionType
AX = mybir.AxisListType

P = 128
D = 128
S = 64
BATCH = 128
H = 16
DH = D // H
TILES = 4
GB = 2 * TILES
TOK = TILES * P
NG = BATCH // GB
UNITS = 2 * TILES
HH = H // 2
NEG = -1.0e9
SCALE = float(DH) ** -0.5
EPS = 1e-5

ATTN_W = 5 * D + 3
COLS = {}
_at = 0
for _n, _w in [("a0", ATTN_W), ("a1", ATTN_W), ("a2", ATTN_W), ("ident", P), ("headmask", HH),
               ("g1", D), ("b1", D), ("g2", D), ("b2", D), ("g3", D), ("b3", D), ("ff2b", D),
               ("negmask", P), ("kiota", 64), ("resetmask", 256), ("trig", P), ("wr", 32),
               ("ff1", 4 * D), ("ff1b", 4), ("ff2", 4 * D), ("router", 16), ("rbias", 64),
               ("lowmask", 256), ("glowmask", 16)]:
    COLS[_n] = (_at, _w)
    _at += _w
PACK = _at


class Signals:

    def __init__(self, nc, prefix):
        self.nc, self.prefix, self.taken = nc, prefix, []

    def __enter__(self):
        return self

    def __exit__(self, *_):
        self.nc.clear_and_free_semaphores(self.taken)
        self.nc.all_engine_barrier()

    def __call__(self, name):
        self.taken.append(self.nc.alloc_semaphore(self.prefix + name))
        return self.taken[-1]


def attention_phase(nc, ps, C, x_res, y_res, x_in, ctx_in, q_mask, key_mask, a, ahead=()):
    cross = a != 1
    load_x = a == 0
    pre_norm = a != 2
    post_norm = a != 0

    with ExitStack() as ctx:
        def sb(name, shape, dt=F32):
            return ctx.enter_context(nc.sbuf_tensor(f"{name}{a}", shape, dt))

        sem = ctx.enter_context(Signals(nc, f"a{a}_"))

        base = COLS[f"a{a}"][0]
        pk = C["pack"]
        wq, wk, wv, wo, bo = (pk[:, base + i * D:base + (i + 1) * D] for i in range(5))
        bq, bk, bv = (pk[:, base + 5 * D + i:base + 5 * D + i + 1] for i in range(3))
        ident, headmask = C["ident"], C["headmask"]

        xn = sb("xn", [P, 2, TILES, D])
        xb = sb("xb", [P, 2, TILES, D])
        qd = sb("qd", [P, 2, 2, TOK])
        kblk = sb("kblk", [P, 2, GB, HH, S])
        vblk = sb("vblk", [P, 2, GB, HH, 32])
        srcT = sb("srcT", [P, TOK])
        ctxT = sb("ctxT", [P, TOK]) if cross else srcT
        ksb = sb("ksb", [P, TOK])
        stats = sb("stats", [P, TILES, 6])
        mv = sb("mv", [P, TILES, 2])
        veps = sb("veps", [P, TILES])
        rstd = sb("rstd", [P, TILES])
        mx = sb("mx", [P, 2, HH])
        sh = sb("sh", [P, 2, HH * S])
        ex = sb("ex", [P, 2, 4, P])
        inv = sb("inv", [P, 2, 2 * H])
        on = sb("on", [P, 2, 2, D])
        onT = sb("onT", [P, 2, 2 * P])
        if cross:
            cin = sb("cin", [P, 2, TILES, D])
        if a == 2:
            kmi = sb("kmi", [P, 2, GB, S], I32)
            kmb = sb("kmb", [P, 2, GB, S], BF16)
            kany = sb("kany", [P, 2, GB])
            qsc = sb("qsc", [P, 2, GB])
        if post_norm:
            t1 = sb("t1", [P, 2, 2, D])
            st2 = sb("st2", [P, 2, 2, 6])
            mv2 = sb("mv2", [P, 2, 2, 2])
            sd2 = sb("sd2", [P, 2, 2])
            se2 = sb("se2", [P, 2, 2])
            rs2 = sb("rs2", [P, 2, 2])
            z2 = sb("z2", [P, 2, 2, D])
            zg2 = sb("zg2", [P, 2, 2, D])
            gam, bet = C[f"g{a}"], C[f"b{a}"]

        SB = [ps[:, i, :] for i in (0, 1)]
        TB = [ps[:, i, :] for i in (2, 3)]
        OB = [ps[:, i, :] for i in (4, 5)]
        PREP = ps[:, 6, :]
        PROJ = ps[:, 7, :]

        rounds = ["cT", "k", "xT", "q", "v0", "v1"] if cross else ["xT", "k", "q", "v0", "v1"]
        slots = dict(zip(rounds, (0, 1, 2, 3, 6, 7) if cross else (2, 3, 4, 6, 7)))
        NP = len(rounds)
        k_slot = slots["k"]
        spread_by_act = {j: k_slot + 1 + j for j in range(4)}
        spread_by_dve = {4: k_slot + 1, 5: k_slot + 2, 6: k_slot + 3}
        spread_by_pool = (7,)
        nr = rounds.index

        x_loaded = [sem(f"x_loaded{s}_") for s in (0, 1)]
        c_loaded = [sem(f"c_loaded{s}_") for s in (0, 1)]
        m_loaded = [sem(f"m_loaded{s}_") for s in (0, 1)]
        vblk_set = sem("vblk_set")
        act_spread = sem("act_spread")
        dve_spread = sem("dve_spread")
        pool_spread = sem("pool_spread")
        stats_done = sem("stats_done")
        moments = sem("moments")
        var_eps = sem("var_eps")
        rstd_done = sem("rstd_done")
        xn_ready = sem("xn_ready")
        xb_ready = sem("xb_ready")
        kmask_bias = sem("kmask_bias")
        kmask_any = sem("kmask_any")
        kmask_ready = sem("kmask_ready")
        prep_ready = sem("prep_ready")
        prep_copied = sem("prep_copied")
        s_ready = sem("s_ready")
        max_done = sem("max_done")
        shifted = sem("shifted")
        t_ready = sem("t_ready")
        e_ready = sem("e_ready")
        o_ready = sem("o_ready")
        inverted = sem("inverted")
        divided = sem("divided")
        onT_ready = sem("onT_ready")
        onT_copied = sem("onT_copied")
        proj_ready = sem("proj_ready")
        resid_done = sem("resid_done")
        stats2_done = sem("stats2_done")
        moments2 = sem("moments2")
        std2 = sem("std2")
        std2_eps = sem("std2_eps")
        rstd2 = sem("rstd2")
        z_done = sem("z_done")
        zg_done = sem("zg_done")
        y_done = sem("y_done")

        def by_batch(t):
            return t.rearrange("p (b k) -> p b k", k=S)

        def swapped(t, b):
            return t.rearrange("p (t b) k -> p b t k", b=2)[:, 1 - b]

        def loaded(g, s):
            return g * 8 + (16 - 8 * s)

        passed = sem("passed")
        block = ctx.enter_context(nc.Block())

        @block.sync
        def _(sp):
            def loads(g, s):
                if load_x:
                    sp.dma_start(tiles_of(x_res, g),
                                 x_in[bass.ds(g * TOK, TOK), :].rearrange("(t p) d -> p t d", p=P)
                                 ).then_inc(x_loaded[s], 16)
                if cross:
                    sp.dma_start(cin[:, s], ctx_in[bass.ds(g * TOK, TOK), :].rearrange("(t p) d -> p t d", p=P)
                                 ).then_inc(c_loaded[s], 16)
                if a == 2:
                    km = key_mask[bass.ds(g * GB, GB), :]
                    sp.dma_start(kmi[0:64, s], km.partition_broadcast(64)).then_inc(m_loaded[s], 16)
                    for b in (0, 1):
                        sp.dma_start(swapped(kmi[64:128, s], b),
                                     km.rearrange("(t b) k -> b t k", b=2)[b].partition_broadcast(64)
                                     ).then_inc(m_loaded[s], 16)

            if cross:
                loads(0, 0)
                loads(1, 1)
                for buffer, array, loaded_ahead in ahead:
                    sp.dma_start(buffer, array).then_inc(loaded_ahead, 16)
                with sp.Fori(0, NG // 2 - 1) as i:
                    for s in (0, 1):
                        sp.wait_ge(prep_ready, nth(i * 2 + s, NP, nr("cT")))
                        sp.sem_inc(passed, 1)
                        if a == 2:
                            sp.wait_ge(kmask_bias, nth(i * 2 + s))
                            sp.sem_inc(passed, 1)
                        loads(i * 2 + (s + 2), s)

        @block.gpsimd
        def _(pool):
            def rows_of(g):
                return tiles_of(x_res if a == 0 else y_res, g)

            def inputs_of(g, s, first):
                if pre_norm:
                    pool.wait_ge(var_eps, nth(g))
                    nc.gpsimd.tensor_tensor(rstd[:, :], veps[:, :], C["mhalf"][:, 0:TILES], ALU.pow
                                            ).then_inc(rstd_done, 1)
                else:
                    if not first:
                        pool.wait_ge(prep_ready, nth(g - 2, NP, nr("xT")))
                        pool.sem_inc(passed, 1)
                    nc.gpsimd.tensor_copy(xn[:, s], rows_of(g)).then_inc(xn_ready, 1)

            def with_bias(g, s, first):
                if a == 1:
                    pool.wait_ge(xn_ready, nth(g))
                if not first:
                    pool.wait_ge(resid_done, g * 2 - 2)
                if a == 1 or not first:
                    pool.sem_inc(passed, 1)
                nc.gpsimd.tensor_tensor(xb[:, s], xn[:, s] if a == 1 else rows_of(g), across(bo, TILES), ALU.add
                                        ).then_inc(xb_ready, 1)

            def spread_keys(g, s):
                pool.wait_ge(prep_copied, nth(g, NP, nr("k")))
                pool.sem_inc(passed, 1)
                for j in spread_by_pool:
                    last = nc.gpsimd.tensor_scalar(kblk[:, s, :, j, :], by_batch(ksb[:, :]), headmask[:, j:j + 1],
                                                   None, ALU.mult)
                last.then_inc(pool_spread, 1)

            def finish(g, m):
                if post_norm:
                    pool.wait_ge(moments2, nth(g, 2, m))
                    nc.gpsimd.tensor_tensor(sd2[:, m, :], mv2[:, m, :, 1], C["half"][:, 0:2], ALU.pow
                                            ).then_inc(std2, 1)
                    pool.wait_ge(z_done, nth(g, 2, m))
                    nc.gpsimd.tensor_tensor(zg2[:, m], z2[:, m], across(gam, 2), ALU.mult).then_inc(zg_done, 1)
                    pool.wait_ge(zg_done, nth(g, 2, m))
                    pool.sem_inc(passed, 1)
                    nc.gpsimd.tensor_tensor(tiles_of(y_res, g, 2 * m, 2), zg2[:, m], across(bet, 2), ALU.add
                                            ).then_inc(y_done, 1)

            def step(g, s, first, more):
                if more:
                    inputs_of(g + 1, 1 - s, first)
                if not first:
                    finish(g - 1, 0)
                if more:
                    spread_keys(g + 1, 1 - s)
                    with_bias(g + 1, 1 - s, first)
                if not first:
                    finish(g - 1, 1)
                if not more:
                    finish(g, 0)
                    finish(g, 1)

            def prep(g, s):
                inputs_of(g, s, True)
                spread_keys(g, s)
                with_bias(g, s, True)

            pipelined(pool, NG, prep, step)

        @block.scalar
        def _(act):
            def copy_round(g, n, out):
                act.wait_ge(prep_ready, nth(g, NP, n))
                nc.scalar.copy(out, PREP).then_inc(prep_copied, 1)

            def copy_k(g, s):
                act.wait_ge(prep_ready, nth(g, NP, nr("k")))
                nc.scalar.activation(ksb[0:64, :], PREP[0:64, :], ACT.Identity, bias=bk[0:64])
                for b in (0, 1):
                    last = nc.scalar.activation(swapped(by_batch(ksb[64:128, :]), b),
                                                PREP[64:128, :].rearrange("p (t b k) -> p b t k", b=2, k=S)[:, b],
                                                ACT.Identity, bias=bk[64:128])
                last.then_inc(prep_copied, 1)

            def spread_key(g, s, j):
                if j == 0:
                    act.wait_ge(prep_copied, nth(g, NP, nr("k")))
                nc.scalar.activation(kblk[:, s, :, j, :], by_batch(ksb[:, :]), ACT.Copy, scale=headmask[:, j:j + 1]
                                     ).then_inc(act_spread, 1)

            def copy_v(g, s, h):
                act.wait_ge(prep_ready, nth(g, NP, nr(f"v{h}")))
                for j in (0, 1):
                    rows = slice(64 * j, 64 * j + 64)
                    last = nc.scalar.copy(
                        vblk[rows, s, 4 * h:4 * h + 4, :, 16 * j:16 * j + DH].rearrange("p b r e -> p (b r) e"),
                        PREP[rows, :].rearrange("p (b e) -> p b e", e=2 * DH)[:, :, DH * j:DH * j + DH])
                last.then_inc(prep_copied, 1)

            def prep_slot(g, s, v):
                if v == slots.get("cT"):
                    copy_round(g, nr("cT"), ctxT[:, :])
                if v == slots["xT"]:
                    copy_round(g, nr("xT"), srcT[:, :])
                if v == slots["k"]:
                    copy_k(g, s)
                for j in spread_by_act:
                    if v == spread_by_act[j]:
                        spread_key(g, s, j)
                for h in (0, 1):
                    if v == slots[f"v{h}"]:
                        copy_v(g, s, h)

            def exps(g, u):
                act.wait_ge(t_ready, nth(g, UNITS, u))
                nc.scalar.activation(ex[:, u % 2], TB[u % 2].rearrange("p (c n) -> p c n", n=P), ACT.Exp
                                     ).then_inc(e_ready, 1)

            def copy_onT(g, m):
                act.wait_ge(onT_ready, nth(g, 2, m))
                nc.scalar.activation(onT[:, m], OB[m][:, 0:2 * P], ACT.Identity, bias=bv).then_inc(onT_copied, 1)

            def prep(g, s):
                for v in range(UNITS):
                    prep_slot(g, s, v)

            def step(g, s, first, more):
                for v in range(UNITS):
                    if v > 0:
                        exps(g, v - 1)
                    elif not first:
                        exps(g - 1, UNITS - 1)
                    if v == 2 and not first:
                        copy_onT(g - 1, 1)
                    if v == 6:
                        copy_onT(g, 0)
                    if more:
                        prep_slot(g + 1, 1 - s, v)
                if not more:
                    exps(g, UNITS - 1)
                    copy_onT(g, 1)

            act.wait_ge(vblk_set, 3)
            pipelined(act, NG, prep, step)

        @block.vector
        def _(dve):
            def norm_stats(g, s):
                if not pre_norm:
                    return
                if load_x:
                    dve.wait_ge(x_loaded[s], loaded(g, s))
                for t in range(TILES):
                    last = nc.vector.bn_stats(stats[:, t, :], tiles_of(x_res, g, t, 1))
                last.then_inc(stats_done, 1)
                dve.wait_ge(stats_done, nth(g))
                dve.sem_inc(passed, 1)
                for t in range(TILES):
                    last = nc.vector.bn_aggr(mv[:, t, :], stats[:, t, :])
                last.then_inc(moments, 1)
                dve.wait_ge(moments, nth(g))
                nc.vector.tensor_scalar(veps[:, :], mv[:, :, 1], EPS, None, ALU.add).then_inc(var_eps, 1)

            def norm_apply(g, s):
                if not pre_norm:
                    return
                dve.wait_ge(rstd_done, nth(g))
                for t in range(TILES):
                    last = nc.vector.tensor_scalar(xn[:, s, t:t + 1, :], tiles_of(x_res, g, t, 1), mv[:, t, 0:1],
                                                   rstd[:, t:t + 1], ALU.subtract, ALU.mult)
                last.then_inc(xn_ready, 1)

            def key_mask_of_next(g, s):
                if a != 2:
                    return
                dve.wait_ge(m_loaded[s], loaded(g, s) * 3)
                nc.vector.tensor_scalar(kmb[:, s], kmi[:, s], 0.0, NEG, ALU.is_equal, ALU.mult).then_inc(kmask_bias, 1)
                dve.wait_ge(kmask_bias, nth(g))
                nc.vector.tensor_reduce(kany[:, s], kmb[:, s], AX.X, ALU.max).then_inc(kmask_any, 1)
                dve.wait_ge(kmask_any, nth(g))
                nc.vector.tensor_scalar(qsc[:, s], kany[:, s], 0.0, SCALE, ALU.is_equal, ALU.mult
                                        ).then_inc(kmask_ready, 1)

            def copy_q(g, s, halves=(0, 1)):
                if 0 in halves:
                    if a == 2:
                        dve.wait_ge(kmask_ready, nth(g))
                    dve.wait_ge(prep_ready, nth(g, NP, nr("q")))
                pr = PREP.rearrange("p (t b k) -> p b t k", b=2, k=S)
                for half in halves:
                    rows = slice(64 * half, 64 * half + 64)
                    for w in (0, 1):
                        b = w ^ half
                        out = qd[rows, s, w].rearrange("p (t b k) -> p b t k", b=2, k=S)[:, b]
                        if a == 0:
                            last = nc.vector.tensor_scalar(out, pr[rows, b], bq[rows], SCALE, ALU.add, ALU.mult)
                            continue
                        if a == 1:
                            sc = C["qscale"][rows, :].unsqueeze(1).broadcast_to((64, TILES, S))
                        else:
                            sc = qsc[rows, s].rearrange("p (t b) -> p b t", b=2)[:, w].unsqueeze(2
                                                                                   ).broadcast_to((64, TILES, S))
                        last = nc.vector.scalar_tensor_tensor(out, pr[rows, b], bq[rows], sc, ALU.add, ALU.mult)
                if 1 in halves:
                    last.then_inc(prep_copied, 1)

            def spread_key(g, s, j):
                if j == min(spread_by_dve):
                    dve.wait_ge(prep_copied, nth(g, NP, nr("k")))
                    dve.sem_inc(passed, 1)
                nc.vector.tensor_scalar(kblk[:, s, :, j, :], by_batch(ksb[:, :]), headmask[:, j:j + 1], None, ALU.mult
                                        ).then_inc(dve_spread, 1)

            def shift(g, u):
                dve.wait_ge(s_ready, nth(g, UNITS, u))
                sc = SB[u % 2].rearrange("p (h k) -> p h k", k=S)
                nc.vector.tensor_reduce(mx[:, u % 2], sc, AX.X, ALU.max).then_inc(max_done, 1)
                dve.wait_ge(max_done, nth(g, UNITS, u))
                nc.vector.tensor_tensor(sh[:, u % 2].rearrange("p (h k) -> p h k", k=S), sc,
                                        mx[:, u % 2].unsqueeze(2).broadcast_to((P, HH, S)), ALU.subtract
                                        ).then_inc(shifted, 1)

            def divide(g, m):
                o = OB[m].rearrange("p (h e) -> p h e", e=16)
                dve.wait_ge(o_ready, nth(g, 2, m))
                nc.vector.reciprocal(inv[:, m], o[:, :, DH]).then_inc(inverted, 1)
                dve.wait_ge(inverted, nth(g, 2, m))
                nc.vector.tensor_tensor(on[:, m].rearrange("p t (h e) -> p (t h) e", e=DH), o[:, :, 0:DH],
                                        inv[:, m].unsqueeze(2).broadcast_to((P, 2 * H, DH)), ALU.mult
                                        ).then_inc(divided, 1)

            def residual(g, s, m):
                if m == 0:
                    dve.wait_ge(xb_ready, nth(g))
                dve.wait_ge(proj_ready, nth(g, 2, m))
                pr = PROJ[:, 256 * m:256 * m + 256].rearrange("p (t d) -> p t d", d=D)
                xs = xb[:, s, 2 * m:2 * m + 2, :]
                if not post_norm:
                    nc.vector.tensor_tensor(tiles_of(x_res, g, 2 * m, 2), pr, xs, ALU.add).then_inc(resid_done, 1)
                    return
                nc.vector.tensor_tensor(t1[:, m], pr, xs, ALU.add).then_inc(resid_done, 1)
                dve.wait_ge(resid_done, nth(g, 2, m))
                for t in (0, 1):
                    last = nc.vector.bn_stats(st2[:, m, t, :], t1[:, m, t, :])
                last.then_inc(stats2_done, 1)
                dve.wait_ge(stats2_done, nth(g, 2, m))
                dve.sem_inc(passed, 1)
                for t in (0, 1):
                    last = nc.vector.bn_aggr(mv2[:, m, t, :], st2[:, m, t, :])
                last.then_inc(moments2, 1)

            def normalise(g, m):
                if not post_norm:
                    return
                dve.wait_ge(std2, nth(g, 2, m))
                nc.vector.tensor_scalar(se2[:, m], sd2[:, m], EPS, None, ALU.add).then_inc(std2_eps, 1)
                dve.wait_ge(std2_eps, nth(g, 2, m))
                nc.vector.reciprocal(rs2[:, m], se2[:, m]).then_inc(rstd2, 1)
                dve.wait_ge(rstd2, nth(g, 2, m))
                for t in (0, 1):
                    last = nc.vector.tensor_scalar(z2[:, m, t, :], t1[:, m, t, :], mv2[:, m, t, 0:1],
                                                   rs2[:, m, t:t + 1], ALU.subtract, ALU.mult)
                last.then_inc(z_done, 1)

            def prep(g, s):
                norm_stats(g, s)
                key_mask_of_next(g, s)
                norm_apply(g, s)
                for j in spread_by_dve:
                    spread_key(g, s, j)
                copy_q(g, s)

            def step(g, s, first, more):
                for v in range(UNITS):
                    if not first:
                        if v == 0:
                            residual(g - 1, 1 - s, 0)
                        if v == 2:
                            divide(g - 1, 1)
                        if v == 4:
                            residual(g - 1, 1 - s, 1)
                    if v == 6:
                        divide(g, 0)
                    if more and not cross and v == slots["q"] + 1:
                        copy_q(g + 1, 1 - s)
                    shift(g, v)
                    if more and cross:
                        for half in (0, 1):
                            if v == slots["q"] + 1 + half:
                                copy_q(g + 1, 1 - s, (half,))
                    if more and v == 0:
                        norm_stats(g + 1, 1 - s)
                        key_mask_of_next(g + 1, 1 - s)
                    if more and v == 1:
                        norm_apply(g + 1, 1 - s)
                    for j in spread_by_dve:
                        if more and v == spread_by_dve[j]:
                            spread_key(g + 1, 1 - s, j)
                    if not first:
                        if v == 2:
                            normalise(g - 1, 0)
                        if v == 6:
                            normalise(g - 1, 1)
                if not more:
                    divide(g, 1)
                    residual(g, s, 0)
                    normalise(g, 0)
                    residual(g, s, 1)
                    normalise(g, 1)

            nc.vector.memset(qd[:, :, :, :], 0.0)
            nc.vector.memset(vblk[:, :, :, :, :], 0.0).then_inc(vblk_set, 1)
            dve.wait_ge(vblk_set, 1)
            nc.vector.memset(vblk[0:64, :, :, :, DH:DH + 1], 1.0).then_inc(vblk_set, 1)
            nc.vector.memset(vblk[64:128, :, :, :, 16 + DH:17 + DH], 1.0).then_inc(vblk_set, 1)
            pipelined(dve, NG, prep, step)

        @block.tensor
        def _(pe):
            def prep_slot(g, s, v, start):
                n = [nr(r) for r in rounds if slots[r] == v]
                if not n:
                    return
                n = n[0]
                what = rounds[n]
                if n > 0:
                    pe.wait_ge(prep_copied, nth(g, NP, n - 1))
                elif not start:
                    pe.wait_ge(prep_copied, g * NP)
                if what == "xT":
                    pe.wait_ge(xn_ready, nth(g))
                    for t in range(TILES):
                        last = nc.tensor.transpose(PREP[:, t * P:(t + 1) * P], xn[:, s, t, :], ident)
                elif what == "cT":
                    pe.wait_ge(c_loaded[s], loaded(g, s))
                    for t in range(TILES):
                        last = nc.tensor.transpose(PREP[:, t * P:(t + 1) * P], cin[:, s, t, :], ident)
                elif what == "k":
                    last = nc.tensor.matmul(PREP, wk, ctxT[:, :], start=True, stop=True)
                elif what == "q":
                    last = nc.tensor.matmul(PREP, wq, srcT[:, :], start=True, stop=True)
                else:
                    h = int(what[1])
                    for b in range(4):
                        for j in (0, 1):
                            last = nc.tensor.matmul(PREP[64 * j:64 * j + 64, b * D:(b + 1) * D],
                                                    ctxT[:, (4 * h + b) * S:(4 * h + b + 1) * S], wv,
                                                    start=True, stop=True)
                last.then_inc(prep_ready, 1)

            def scores(g, s, u):
                t, w = u // 2, u % 2
                if u == 0:
                    pe.wait_ge(prep_copied, nth(g, NP, nr("q")))
                    pe.sem_inc(passed, 1)
                    pe.wait_ge(act_spread, (g + 1) * len(spread_by_act))
                    pe.sem_inc(passed, 1)
                    pe.wait_ge(dve_spread, (g + 1) * len(spread_by_dve))
                    pe.sem_inc(passed, 1)
                    pe.wait_ge(pool_spread, g + 1)
                    pe.sem_inc(passed, 1)
                last = nc.tensor.matmul(SB[w], qd[:, s, w, t * P:(t + 1) * P],
                                        kblk[:, s, 2 * t + w].rearrange("p h k -> p (h k)"), start=True, stop=a == 0)
                if a == 1:
                    last = nc.tensor.matmul(SB[w], C["identb"][:, :],
                                            C["qmask"][0:S, :].unsqueeze(1).broadcast_to((S, HH, S)),
                                            start=False, stop=True)
                if a == 2:
                    last = nc.tensor.matmul(SB[w], C["oneb"][:, :],
                                            kmb[:, s, 2 * t, :].unsqueeze(1).broadcast_to((P, HH, S)),
                                            start=False, stop=True)
                last.then_inc(s_ready, 1)

            def transposes(g, u):
                pe.wait_ge(shifted, nth(g, UNITS, u))
                for c in range(4):
                    last = nc.tensor.transpose(TB[u % 2][:, c * P:(c + 1) * P], sh[:, u % 2, c * P:(c + 1) * P], ident)
                last.then_inc(t_ready, 1)

            def weigh(g, s, u, first):
                t, w = u // 2, u % 2
                m = t // 2
                if u % 4 == 0 and not (first and m == 0):
                    pe.wait_ge(onT_copied, g * 2 + (m - 1))
                if u == 0:
                    pe.wait_ge(prep_copied, (g + 1) * NP)
                pe.wait_ge(e_ready, nth(g, UNITS, u))
                for c in range(4):
                    for bb in (0, 1):
                        r = w ^ bb
                        col = ((t % 2) * H + r * HH + 2 * c) * 16
                        last = nc.tensor.matmul(OB[m][64 * bb:64 * bb + 64, col:col + 32],
                                                ex[:, u % 2, c, bb * S:(bb + 1) * S],
                                                vblk[:, s, 2 * t + bb, 4 * r + c, :], start=True, stop=True)
                if u % 4 == 3:
                    last.then_inc(o_ready, 1)

            def make_onT(g, m):
                pe.wait_ge(divided, nth(g, 2, m))
                for t in (0, 1):
                    last = nc.tensor.transpose(OB[m][:, t * P:(t + 1) * P], on[:, m, t, :], ident)
                last.then_inc(onT_ready, 1)

            def project(g, m, first=False):
                if not (first and m == 0):
                    pe.wait_ge(resid_done, g * 2 + m)
                pe.wait_ge(onT_copied, nth(g, 2, m))
                for t in (0, 1):
                    last = nc.tensor.matmul(PROJ[:, (2 * m + t) * D:(2 * m + t + 1) * D], onT[:, m, t * P:(t + 1) * P],
                                            wo, start=True, stop=True)
                last.then_inc(proj_ready, 1)

            def prep(g, s):
                for v in range(UNITS):
                    prep_slot(g, s, v, True)

            def step(g, s, first, more):
                for v in range(UNITS):
                    scores(g, s, v)
                    if v > 0:
                        transposes(g, v - 1)
                    elif not first:
                        transposes(g - 1, UNITS - 1)
                    if v > 1:
                        weigh(g, s, v - 2, first)
                    elif not first:
                        weigh(g - 1, 1 - s, UNITS - 2 + v, False)
                    if more:
                        prep_slot(g + 1, 1 - s, v, False)
                    if not first:
                        if v == 2:
                            make_onT(g - 1, 1)
                        if v == 3:
                            project(g - 1, 1)
                    if v == 6:
                        make_onT(g, 0)
                    if v == 7:
                        project(g, 0, first)
                if not more:
                    transposes(g, UNITS - 1)
                    weigh(g, s, UNITS - 2, False)
                    weigh(g, s, UNITS - 1, False)
                    make_onT(g, 1)
                    project(g, 1)

            pipelined(pe, NG, prep, step)


def pipelined(eng, n, prep, step):
    prep(0, 0)
    step(0, 0, True, True)
    with eng.Fori(0, n // 2 - 1) as i:
        for s in (1, 0):
            step(i * 2 + (2 - s), s, False, True)
    step(n - 1, 1, False, False)


def two_halves(eng, n, prep, step):
    prep(0, 0)
    step(0, 0, True)
    with eng.Fori(0, n // 2 - 1) as i:
        for s in (1, 0):
            step(i * 2 + (2 - s), s, True)
    step(n - 1, 1, False)


def nth(g, n=1, k=0):
    return g * n + (k + 1)


def tiles_of(t, g, k=0, n=TILES):
    return t[:, bass.ds(g * TILES + k, n), :]


def across(row, n):
    return row.unsqueeze(1).broadcast_to((P, n, D))


def relu_phase(nc, ps, C, x_res, y_res, ahead):
    F = 4
    with ExitStack() as ctx:
        def sb(name, shape, dt=F32):
            return ctx.enter_context(nc.sbuf_tensor("ff_" + name, shape, dt))

        sem = ctx.enter_context(Signals(nc, "ff_"))

        w1 = C["ff1"].rearrange("p (c n) -> p c n", c=F)
        b1 = C["ff1b"]
        w2 = C["ff2"].rearrange("p (c n) -> p c n", c=F)
        yn = sb("yn", [P, 2, TILES, D])
        yT = sb("yT", [P, 2, TOK])
        hT = sb("hT", [P, F, TOK])
        yb = sb("yb", [P, 2, TILES, D])
        t1 = sb("t1", [P, TILES, D])
        st = sb("st", [P, TILES, 6])
        mv = sb("mv", [P, TILES, 2])
        sd = sb("sd", [P, TILES])
        se = sb("se", [P, TILES])
        rs = sb("rs", [P, TILES])
        z = sb("z", [P, TILES, D])
        zg = sb("zg", [P, TILES, D])
        zb = sb("zb", [P, 2, TILES, D])
        HB = [ps[:, i, :] for i in range(4)]
        OUTB = [ps[:, i, :] for i in (4, 5)]
        XB = [ps[:, i, :] for i in (6, 7)]

        yn_ready = sem("yn_ready")
        yb_ready = sem("yb_ready")
        yT_ready = sem("yT_ready")
        yT_copied = sem("yT_copied")
        h_ready = sem("h_ready")
        relu_done = sem("relu_done")
        out_ready = sem("out_ready")
        summed = sem("summed")
        stats_done = sem("stats_done")
        moments = sem("moments")
        std_done = sem("std_done")
        std_eps = sem("std_eps")
        rstd_done = sem("rstd_done")
        z_done = sem("z_done")
        zg_done = sem("zg_done")
        zb_done = sem("zb_done")
        x_done = sem("x_done")
        passed = sem("passed")
        block = ctx.enter_context(nc.Block())

        @block.sync
        def _(sp):
            for buffer, array, loaded_ahead in ahead:
                sp.dma_start(buffer, array).then_inc(loaded_ahead, 16)

        @block.gpsimd
        def _(pool):
            def prep(g, s):
                nc.gpsimd.tensor_tensor(yb[:, s], tiles_of(y_res, g), across(C["ff2b"], TILES), ALU.add
                                        ).then_inc(yb_ready, 1)

            def step(g, s, first, more):
                pool.wait_ge(moments, nth(g))
                nc.gpsimd.tensor_tensor(sd[:, :], mv[:, :, 1], C["half"][:, 0:TILES], ALU.pow).then_inc(std_done, 1)
                if more:
                    prep(g + 1, 1 - s)
                pool.wait_ge(z_done, nth(g))
                nc.gpsimd.tensor_tensor(zg[:, :, :], z[:, :, :], across(C["g3"], TILES), ALU.mult).then_inc(zg_done, 1)
                pool.wait_ge(zg_done, nth(g))
                pool.sem_inc(passed, 1)
                if not first:
                    pool.wait_ge(x_done, g)
                    pool.sem_inc(passed, 1)
                nc.gpsimd.tensor_tensor(zb[:, s], zg[:, :, :], across(C["b3"], TILES), ALU.add).then_inc(zb_done, 1)

            pipelined(pool, NG, prep, step)

        @block.scalar
        def _(act):
            def copy_rows(g, s):
                nc.scalar.copy(yn[:, s], tiles_of(y_res, g)).then_inc(yn_ready, 1)

            def copy_yT(g, s):
                act.wait_ge(yT_ready, nth(g))
                nc.scalar.copy(yT[:, s], XB[s]).then_inc(yT_copied, 1)

            def prep(g, s):
                copy_rows(g, s)
                copy_yT(g, s)

            def step(g, s, first, more):
                if more:
                    copy_rows(g + 1, 1 - s)
                for c in range(F):
                    act.wait_ge(h_ready, nth(g, F, c))
                    if c == 0 and not first:
                        act.wait_ge(out_ready, g)
                    nc.scalar.activation(hT[:, c], HB[c], ACT.Relu, bias=b1[:, c:c + 1]).then_inc(relu_done, 1)
                if more:
                    copy_yT(g + 1, 1 - s)

            pipelined(act, NG, prep, step)

        @block.tensor
        def _(pe):
            def prep(g, s):
                pe.wait_ge(yn_ready, nth(g))
                for t in range(TILES):
                    last = nc.tensor.transpose(XB[s][:, t * P:(t + 1) * P], yn[:, s, t, :], C["ident"])
                last.then_inc(yT_ready, 1)

            def step(g, s, first, more):
                pe.wait_ge(yT_copied, nth(g))
                for c in range(F):
                    nc.tensor.matmul(HB[c], w1[:, c], yT[:, s], start=True, stop=True).then_inc(h_ready, 1)
                if more:
                    prep(g + 1, 1 - s)
                if not first:
                    pe.wait_ge(summed, g)
                for t in range(TILES):
                    for c in range(F):
                        if t == 0:
                            pe.wait_ge(relu_done, nth(g, F, c))
                        last = nc.tensor.matmul(OUTB[s][:, t * D:(t + 1) * D], hT[:, c, t * P:(t + 1) * P], w2[:, c],
                                                start=(c == 0), stop=(c == F - 1))
                last.then_inc(out_ready, 1)

            pipelined(pe, NG, prep, step)

        @block.vector
        def _(dve):
            def add_to_x(g, s):
                dve.wait_ge(zb_done, nth(g))
                xs = tiles_of(x_res, g)
                nc.vector.tensor_tensor(xs, zb[:, s], xs, ALU.add).then_inc(x_done, 1)

            def step(g, s, first, more):
                if not first:
                    dve.wait_ge(z_done, g)
                dve.wait_ge(out_ready, nth(g))
                dve.wait_ge(yb_ready, nth(g))
                nc.vector.tensor_tensor(t1[:, :, :], OUTB[s].rearrange("p (t d) -> p t d", d=D), yb[:, s], ALU.add
                                        ).then_inc(summed, 1)
                dve.wait_ge(summed, nth(g))
                for t in range(TILES):
                    last = nc.vector.bn_stats(st[:, t, :], t1[:, t, :])
                last.then_inc(stats_done, 1)
                dve.wait_ge(stats_done, nth(g))
                dve.sem_inc(passed, 1)
                for t in range(TILES):
                    last = nc.vector.bn_aggr(mv[:, t, :], st[:, t, :])
                last.then_inc(moments, 1)
                if not first:
                    add_to_x(g - 1, 1 - s)
                dve.wait_ge(std_done, nth(g))
                nc.vector.tensor_scalar(se[:, :], sd[:, :], EPS, None, ALU.add).then_inc(std_eps, 1)
                dve.wait_ge(std_eps, nth(g))
                nc.vector.reciprocal(rs[:, :], se[:, :]).then_inc(rstd_done, 1)
                dve.wait_ge(rstd_done, nth(g))
                for t in range(TILES):
                    last = nc.vector.tensor_scalar(z[:, t, :], t1[:, t, :], mv[:, t, 0:1], rs[:, t:t + 1],
                                                   ALU.subtract, ALU.mult)
                last.then_inc(z_done, 1)
                if not more:
                    add_to_x(g, s)

            pipelined(dve, NG, lambda g, s: None, step)


E, SH = 16, 2
K = E + SH
CH = 3


def experts_phase(nc, ps, C, x_res, gate, up, down, w_loaded, out):
    with ExitStack() as ctx:
        def sb(name, shape, dt=F32):
            return ctx.enter_context(nc.sbuf_tensor("moe_" + name, shape, dt))

        sem = ctx.enter_context(Signals(nc, "moe_"))

        gate_hi = sb("gate_hi", [P, K, D], F32R)
        gate_lo = sb("gate_lo", [P, K, D], F32R)
        up_hi = sb("up_hi", [P, K, D], F32R)
        up_lo = sb("up_lo", [P, K, D], F32R)
        x_hi = sb("x_hi", [P, 2, TOK], F32R)
        x_lo = sb("x_lo", [P, 2, TOK], F32R)
        xn = sb("xn", [P, 2, TILES, D])
        xnT = sb("xnT", [P, 2, TOK])
        stats = sb("stats", [P, TILES, 6])
        mv = sb("mv", [P, TILES, 2])
        veps = sb("veps", [P, TILES])
        rstd = sb("rstd", [P, TILES])
        sg = sb("sg", [P, 2, TOK])
        act_ = sb("act", [P, 3, TOK])
        acc = sb("acc", [P, 2, TILES, D])
        OTHERS = (5, 7, 9, 12)
        part = sb("part", [P, len(OTHERS), TILES, D])
        TE = TILES * E
        ex = sb("ex", [P, TE])
        one_ex = sb("one_ex", [P, TE])
        score = sb("score", [P, TE])
        biased = sb("biased", [P, TE])
        hi2 = sb("hi2", [P, TE // 2])
        lo2 = sb("lo2", [P, TE // 2])
        top = sb("top", [P, TILES * 4])
        mid = sb("mid", [P, TILES * 4])
        low = sb("low", [P, TILES * 4])
        sec = sb("sec", [P, TILES * 4])
        gsc = sb("gsc", [P, TILES * 4])
        ggt = sb("ggt", [P, TILES * 4 * 4])
        geq = sb("geq", [P, TILES * 4 * 4])
        gtie = sb("gtie", [P, TILES * 4 * 4])
        gall = sb("gall", [P, TILES * 4 * 4])
        grank = sb("grank", [P, TILES * 4])
        gin = sb("gin", [P, TILES * 4])
        gout = sb("gout", [P, TILES * 4])
        kept = sb("kept", [P, TE])
        masked = sb("masked", [P, TE])
        egt = sb("egt", [P, TILES, E, E])
        eeq = sb("eeq", [P, TILES, E, E])
        rank = sb("rank", [P, TE])
        w = sb("w", [P, TE])
        wsum = sb("wsum", [P, TILES])
        wsume = sb("wsume", [P, TILES])
        winv = sb("winv", [P, TILES])
        comb = sb("comb", [P, 2, TILES, E])

        GB_ = [ps[:, i, :] for i in (0, 1)]
        UB = [ps[:, i, :] for i in (2, 3)]
        YB = [ps[:, i, :] for i in (4, 5)]
        XB = ps[:, 6, :]
        RB = ps[:, 7, 0:TE]
        w_high = sem("w_high")
        w_split = sem("w_split")
        x_high = sem("x_high")
        x_split = sem("x_split")
        stats_done = sem("stats_done")
        moments = sem("moments")
        var_eps = sem("var_eps")
        rstd_done = sem("rstd_done")
        xn_ready = sem("xn_ready")
        xT_ready = sem("xT_ready")
        xT_copied = sem("xT_copied")
        logits_ready = sem("logits_ready")
        exp_done = sem("exp_done")
        NR = 29
        routing = sem("routing")
        comb_ready = sem("comb_ready")
        g_ready = sem("g_ready")
        u_ready = sem("u_ready")
        silu_done = sem("silu_done")
        act_ready = sem("act_ready")
        y_ready = sem("y_ready")
        acc_done = sem("acc_done")
        part_added = sem("part_added")
        totals = sem("totals")
        stored = [sem(f"stored{s}_") for s in (0, 1)]
        def one_by_one(t):
            return t[:, :].rearrange("p (t e) -> p t e", e=E).unsqueeze(3).broadcast_to((P, TILES, E, E))

        def all_others(t):
            return t[:, :].rearrange("p (t e) -> p t e", e=E).unsqueeze(2).broadcast_to((P, TILES, E, E))

        def by_tile(t):
            return t[:, :, :, :].rearrange("p t e j -> p t (e j)")

        def before(g, n):
            return nth(g, NR, n - 1)

        passed = sem("passed")
        block = ctx.enter_context(nc.Block())

        @block.sync
        def _(sp):
            for s in (0, 1):
                sp.sem_inc(stored[s], 1)
            with sp.Fori(0, NG // 2) as i:
                for s in (0, 1):
                    g = i * 2 + s
                    sp.wait_ge(totals, nth(g))
                    sp.dma_start(out[bass.ds(g * TOK, TOK), :].rearrange("(t p) d -> p t d", p=P), acc[:, s]
                                 ).then_inc(stored[s], 16)
            for s in (0, 1):
                sp.wait_ge(stored[s], 16 * (NG // 2) + 1)

        @block.gpsimd
        def _(pool):
            def prep(g, s):
                pool.wait_ge(var_eps, nth(g))
                nc.gpsimd.tensor_tensor(rstd[:, :], veps[:, :], C["mhalf"][:, 0:TILES], ALU.pow).then_inc(rstd_done, 1)
                low_rows(g, s)

            def low_rows(g, s):
                pool.wait_ge(x_high, nth(g))
                pool.wait_ge(xT_copied, nth(g))
                nc.gpsimd.tensor_tensor(x_lo[:, s], xnT[:, s], x_hi[:, s], ALU.subtract).then_inc(x_split, 1)

            def rank_experts(g):
                pool.wait_ge(routing, before(g, 21))
                nc.gpsimd.tensor_tensor(by_tile(eeq), by_tile(eeq),
                                        C["lowmask"].unsqueeze(1).broadcast_to((P, TILES, E * E)), ALU.mult
                                        ).then_inc(routing, 1)
                pool.wait_ge(routing, before(g, 22))
                nc.gpsimd.tensor_tensor(by_tile(egt), by_tile(egt), by_tile(eeq), ALU.add).then_inc(routing, 1)

            def split_weights():
                for i in range(K // CH):
                    part = slice(i * CH, (i + 1) * CH)
                    pool.wait_ge(w_high, i + 1)
                    nc.gpsimd.tensor_tensor(gate_lo[:, part], gate[:, part], gate_hi[:, part], ALU.subtract)
                    nc.gpsimd.tensor_tensor(up_lo[:, part], up[:, part], up_hi[:, part], ALU.subtract
                                            ).then_inc(w_split, 1)

            def add_part(g, j):
                if j > 1:
                    pool.wait_ge(part_added, nth(g, len(OTHERS) - 1, j - 2))
                pool.wait_ge(acc_done, nth(g, K - 1, OTHERS[j] - SH + 1))
                nc.gpsimd.tensor_tensor(part[:, 0], part[:, 0], part[:, j], ALU.add).then_inc(part_added, 1)

            def total(g, s):
                pool.wait_ge(part_added, (g + 1) * (len(OTHERS) - 1))
                pool.wait_ge(acc_done, (g + 1) * (K - 1))
                nc.gpsimd.tensor_tensor(acc[:, s], acc[:, s], part[:, 0], ALU.add).then_inc(totals, 1)

            def first_prep(g, s):
                prep(g, s)
                split_weights()
                rank_experts(g)

            def step(g, s, first, more):
                if more:
                    pool.wait_ge(var_eps, nth(g + 1))
                    nc.gpsimd.tensor_tensor(rstd[:, :], veps[:, :], C["mhalf"][:, 0:TILES], ALU.pow
                                            ).then_inc(rstd_done, 1)
                if not first:
                    total(g - 1, 1 - s)
                if more:
                    low_rows(g + 1, 1 - s)
                add_part(g, 1)
                if more:
                    rank_experts(g + 1)
                add_part(g, 2)
                add_part(g, 3)
                if not more:
                    total(g, s)

            pipelined(pool, NG, first_prep, step)

        @block.scalar
        def _(act):
            def copy_xT(g, s):
                act.wait_ge(xT_ready, nth(g))
                nc.scalar.copy(x_hi[:, s], XB).then_inc(x_high, 1)
                nc.scalar.copy(xnT[:, s], XB).then_inc(xT_copied, 1)

            def route_exp(g, s):
                act.wait_ge(logits_ready, nth(g))
                nc.scalar.activation(ex[:, :], RB, ACT.Exp, scale=-1.0).then_inc(exp_done, 1)

            def high_weights():
                for i in range(K // CH):
                    part = slice(i * CH, (i + 1) * CH)
                    act.wait_ge(w_loaded[i], 48)
                    nc.scalar.copy(gate_hi[:, part], gate[:, part])
                    nc.scalar.copy(up_hi[:, part], up[:, part]).then_inc(w_high, 1)

            def prep(g, s):
                copy_xT(g, s)
                high_weights()
                route_exp(g, s)

            def weigh_expert(g, s, j, first):
                k = OTHERS[j]
                n = k - SH + 1
                if j == 0:
                    act.wait_ge(routing, nth(g, NR, NR - 1))
                    if not first:
                        act.wait_ge(totals, g)
                act.wait_ge(y_ready, nth(g, K - 1, n))
                act.wait_ge(acc_done, nth(g, K - 1, n - 1))
                for t in range(TILES):
                    last = nc.scalar.activation(part[:, j, t], YB[k % 2][:, t * D:(t + 1) * D], ACT.Copy,
                                                scale=comb[:, s, t, k - SH:k - SH + 1])
                last.then_inc(acc_done, 1)

            def step(g, s, first, more):
                for k in range(K):
                    act.wait_ge(g_ready, nth(g, K, k))
                    nc.scalar.activation(sg[:, k % 2], GB_[k % 2], ACT.Silu).then_inc(silu_done, 1)
                    if k - 3 in OTHERS:
                        weigh_expert(g, s, OTHERS.index(k - 3), first)
                    if more and k == 3:
                        copy_xT(g + 1, 1 - s)
                    if more and k == 5:
                        route_exp(g + 1, 1 - s)

            pipelined(act, NG, prep, step)

        @block.tensor
        def _(pe):
            def make_xT(g, s):
                pe.wait_ge(xn_ready, nth(g))
                for t in range(TILES):
                    last = nc.tensor.transpose(XB[:, t * P:(t + 1) * P], xn[:, s, t, :], C["ident"])
                last.then_inc(xT_ready, 1)

            def logits(g, s):
                pe.wait_ge(xT_copied, nth(g))
                for t in range(TILES):
                    last = nc.tensor.matmul(RB[:, t * E:(t + 1) * E], xnT[:, s, t * P:(t + 1) * P], C["router"],
                                            start=True, stop=True)
                last.then_inc(logits_ready, 1)

            def prep(g, s):
                make_xT(g, s)
                logits(g, s)

            def down_proj(g, k, first):
                pe.wait_ge(act_ready, nth(g, K, k))
                if k >= SH:
                    if k >= SH + 1:
                        pe.wait_ge(acc_done, nth(g, K - 1, k - SH - 1))
                    for t in range(TILES):
                        last = nc.tensor.matmul(YB[k % 2][:, t * D:(t + 1) * D], act_[:, k % 3, t * P:(t + 1) * P],
                                                down[:, k, :], start=True, stop=True)
                    last.then_inc(y_ready, 1)
                elif k == SH - 1:
                    if not first:
                        pe.wait_ge(acc_done, g * (K - 1))
                    for t in range(TILES):
                        for j in range(SH):
                            last = nc.tensor.matmul(YB[1][:, t * D:(t + 1) * D], act_[:, j, t * P:(t + 1) * P],
                                                    down[:, j, :], start=(j == 0), stop=(j == SH - 1))
                    last.then_inc(y_ready, 1)

            def product(out, hi, lo, x, y):
                nc.tensor.matmul(out, hi, y, start=True, stop=False)
                nc.tensor.matmul(out, lo, x, start=False, stop=False)
                return nc.tensor.matmul(out, hi, x, start=False, stop=True)

            def step(g, s, first, more):
                pe.wait_ge(x_split, nth(g))
                for k in range(K):
                    if first and k % CH == 0:
                        pe.wait_ge(w_split, k // CH + 1)
                    if k >= 2:
                        pe.wait_ge(act_ready, nth(g, K, k - 2))
                    elif not first:
                        pe.wait_ge(act_ready, g * K + (k - 1))
                    product(GB_[k % 2], gate_hi[:, k], gate_lo[:, k], x_hi[:, s], x_lo[:, s]).then_inc(g_ready, 1)
                    product(UB[k % 2], up_hi[:, k], up_lo[:, k], x_hi[:, s], x_lo[:, s]).then_inc(u_ready, 1)
                    if k >= 2:
                        down_proj(g, k - 2, first)
                    elif not first:
                        down_proj(g - 1, K - 2 + k, False)
                    if more and k == 3:
                        make_xT(g + 1, 1 - s)
                    if more and k == 5:
                        logits(g + 1, 1 - s)
                if not more:
                    down_proj(g, K - 2, False)
                    down_proj(g, K - 1, False)

            pipelined(pe, NG, prep, step)

        @block.vector
        def _(dve):
            V = nc.vector

            def norm_stats(g, s):
                for t in range(TILES):
                    last = V.bn_stats(stats[:, t, :], tiles_of(x_res, g, t, 1))
                last.then_inc(stats_done, 1)
                dve.wait_ge(stats_done, g + 1)
                dve.sem_inc(passed, 1)
                for t in range(TILES):
                    last = V.bn_aggr(mv[:, t, :], stats[:, t, :])
                last.then_inc(moments, 1)
                dve.wait_ge(moments, nth(g))
                V.tensor_scalar(veps[:, :], mv[:, :, 1], EPS, None, ALU.add).then_inc(var_eps, 1)

            def norm_apply(g, s):
                dve.wait_ge(rstd_done, nth(g))
                for t in range(TILES):
                    last = V.tensor_scalar(xn[:, s, t:t + 1, :], tiles_of(x_res, g, t, 1), mv[:, t, 0:1],
                                           rstd[:, t:t + 1], ALU.subtract, ALU.mult)
                last.then_inc(xn_ready, 1)

            def g4(t):
                return t[:, :].rearrange("p (t g) -> p t g", t=TILES)

            def groups_of(t):
                return t[:, :].rearrange("p (n c) -> p n c", c=4)

            def pairs(t, k):
                return t[:, :].rearrange("p (n c) -> p n c", c=2)[:, :, k]

            def route(g, s, parts):
                TG = TILES * 4

                def ge4(t):
                    return t[:, :].rearrange("p (n g j) -> p n g j", g=4, j=4)

                inner = lambda t: g4(t).unsqueeze(3).broadcast_to((P, TILES, 4, 4))
                other = lambda t: g4(t).unsqueeze(2).broadcast_to((P, TILES, 4, 4))
                t16 = lambda t: t[:, :].rearrange("p (t e) -> p t e", e=E)
                spread = lambda t: t[:, :].unsqueeze(2).broadcast_to((P, TG, 4))
                glow = C["glowmask"].rearrange("p (g j) -> p g j", j=4).unsqueeze(1).broadcast_to((P, TILES, 4, 4))
                if 0 in parts:
                    dve.wait_ge(exp_done, nth(g))
                    V.tensor_scalar(one_ex[:, :], ex[:, :], 1.0, None, ALU.add).then_inc(routing, 1)
                    dve.wait_ge(routing, before(g, 1))
                    V.reciprocal(score[:, :], one_ex[:, :]).then_inc(routing, 1)
                    dve.wait_ge(routing, before(g, 2))
                    V.tensor_tensor(biased[:, :], score[:, :], C["rbias"], ALU.add).then_inc(routing, 1)
                    dve.wait_ge(routing, before(g, 3))
                    V.tensor_tensor(hi2[:, :], pairs(biased, 0), pairs(biased, 1), ALU.max).then_inc(routing, 1)
                if 1 in parts:
                    dve.wait_ge(routing, before(g, 4))
                    V.tensor_tensor(lo2[:, :], pairs(biased, 0), pairs(biased, 1), ALU.min).then_inc(routing, 1)
                    dve.wait_ge(routing, before(g, 5))
                    V.tensor_tensor(top[:, :], pairs(hi2, 0), pairs(hi2, 1), ALU.max).then_inc(routing, 1)
                    dve.wait_ge(routing, before(g, 6))
                    V.tensor_tensor(mid[:, :], pairs(hi2, 0), pairs(hi2, 1), ALU.min).then_inc(routing, 1)
                    dve.wait_ge(routing, before(g, 7))
                    V.tensor_tensor(low[:, :], pairs(lo2, 0), pairs(lo2, 1), ALU.max).then_inc(routing, 1)
                if 2 in parts:
                    dve.wait_ge(routing, before(g, 8))
                    V.tensor_tensor(sec[:, :], mid[:, :], low[:, :], ALU.max).then_inc(routing, 1)
                    dve.wait_ge(routing, before(g, 9))
                    V.tensor_tensor(gsc[:, :], top[:, :], sec[:, :], ALU.add).then_inc(routing, 1)
                    dve.wait_ge(routing, before(g, 10))
                    V.tensor_tensor(ge4(ggt), other(gsc), inner(gsc), ALU.is_gt).then_inc(routing, 1)
                    dve.wait_ge(routing, before(g, 11))
                    V.tensor_tensor(ge4(geq), other(gsc), inner(gsc), ALU.is_equal).then_inc(routing, 1)
                if 3 in parts:
                    dve.wait_ge(routing, before(g, 12))
                    V.tensor_tensor(ge4(gtie), ge4(geq), glow, ALU.mult).then_inc(routing, 1)
                    dve.wait_ge(routing, before(g, 13))
                    V.tensor_tensor(gall[:, :], ggt[:, :], gtie[:, :], ALU.add).then_inc(routing, 1)
                    dve.wait_ge(routing, before(g, 14))
                    V.tensor_reduce(grank[:, :], groups_of(gall), AX.X, ALU.add).then_inc(routing, 1)
                    dve.wait_ge(routing, before(g, 15))
                    V.tensor_scalar(gin[:, :], grank[:, :], 2.0, None, ALU.is_lt).then_inc(routing, 1)
                if 4 in parts:
                    dve.wait_ge(routing, before(g, 16))
                    V.tensor_scalar(gout[:, :], gin[:, :], -1.0, None, ALU.add).then_inc(routing, 1)
                    dve.wait_ge(routing, before(g, 17))
                    V.tensor_tensor(groups_of(kept), groups_of(biased), spread(gin), ALU.mult).then_inc(routing, 1)
                    dve.wait_ge(routing, before(g, 18))
                    V.tensor_tensor(groups_of(masked), groups_of(kept), spread(gout), ALU.add).then_inc(routing, 1)
                    dve.wait_ge(routing, before(g, 19))
                    V.tensor_tensor(egt[:, :, :, :], all_others(masked), one_by_one(masked),
                                    ALU.is_gt).then_inc(routing, 1)
                if 5 in parts:
                    dve.wait_ge(routing, before(g, 20))
                    V.tensor_tensor(eeq[:, :, :, :], all_others(masked), one_by_one(masked),
                                    ALU.is_equal).then_inc(routing, 1)
                if 6 in parts:
                    dve.wait_ge(routing, before(g, 23))
                    V.tensor_reduce(rank[:, :], egt[:, :, :, :].rearrange("p t e j -> p (t e) j"), AX.X,
                                    ALU.add).then_inc(routing, 1)
                    dve.wait_ge(routing, before(g, 24))
                    V.scalar_tensor_tensor(w[:, :], rank[:, :], 4.0, score[:, :], ALU.is_lt,
                                           ALU.mult).then_inc(routing, 1)
                    dve.wait_ge(routing, before(g, 25))
                    V.tensor_reduce(wsum[:, :], t16(w), AX.X, ALU.add).then_inc(routing, 1)
                if 7 in parts:
                    dve.wait_ge(routing, before(g, 26))
                    V.tensor_scalar(wsume[:, :], wsum[:, :], 1e-20, None, ALU.add).then_inc(routing, 1)
                    dve.wait_ge(routing, before(g, 27))
                    V.reciprocal(winv[:, :], wsume[:, :]).then_inc(routing, 1)
                    dve.wait_ge(routing, before(g, 28))
                    V.scalar_tensor_tensor(comb[:, s], t16(w), 2.5,
                                            winv[:, :].unsqueeze(2).broadcast_to((P, TILES, E)), ALU.mult,
                                           ALU.mult).then_inc(routing, 1)

            def prep(g, s):
                norm_stats(g, s)
                norm_apply(g, s)
                route(g, s, range(8))

            def product(g, k, first):
                dve.wait_ge(u_ready, nth(g, K, k))
                dve.wait_ge(silu_done, nth(g, K, k))
                if k >= SH + 3:
                    dve.wait_ge(y_ready, nth(g, K - 1, k - SH - 2))
                elif k >= 3:
                    dve.wait_ge(y_ready, nth(g, K - 1, 0))
                elif not first:
                    dve.wait_ge(y_ready, g * (K - 1) + (k - 2))
                V.tensor_tensor(act_[:, k % 3], UB[k % 2], sg[:, k % 2], ALU.mult).then_inc(act_ready, 1)

            def accumulate(g, s, k):
                if k < SH - 1 or k in OTHERS:
                    return
                n = k - SH + 1
                dve.wait_ge(y_ready, nth(g, K - 1, n))
                y = YB[k % 2].rearrange("p (t d) -> p t d", d=D)
                if n == 0:
                    dve.wait_ge(stored[s], g * 8 + (1 - 8 * s))
                    V.tensor_tensor(acc[:, s], y, tiles_of(x_res, g), ALU.add).then_inc(acc_done, 1)
                    return
                dve.wait_ge(acc_done, nth(g, K - 1, n - 1))
                if n == 1:
                    dve.wait_ge(routing, nth(g, NR, NR - 1))
                for t in range(TILES):
                    last = V.scalar_tensor_tensor(acc[:, s, t], y[:, t], comb[:, s, t, k - SH:k - SH + 1], acc[:, s, t],
                                                  ALU.mult, ALU.add)
                last.then_inc(acc_done, 1)

            ROUTE_SLOTS = (6, 7, 8, 9, 10, 11, 14, 16)

            def step(g, s, first, more):
                for k in range(K):
                    if k >= 3:
                        accumulate(g, s, k - 3)
                    elif not first:
                        accumulate(g - 1, 1 - s, K - 3 + k)
                    product(g, k, first)
                    if more and k == 0:
                        norm_stats(g + 1, 1 - s)
                    if more and k == 2:
                        norm_apply(g + 1, 1 - s)
                    for part, at in enumerate(ROUTE_SLOTS):
                        if more and k == at:
                            route(g + 1, 1 - s, [part])
                if not more:
                    for k in range(K - 3, K):
                        accumulate(g, s, k)

            pipelined(dve, NG, prep, step)


def choice_phase(nc, ps, C, x_res, wqkv, woe, w_loaded):
    E, KC = 8, 8
    GT = 8
    NB = 2 * GT
    N = BATCH // NB
    ASCALE = float(D) ** -0.5

    with ExitStack() as ctx:
        def sb(name, shape, dt=F32):
            return ctx.enter_context(nc.sbuf_tensor("ch_" + name, shape, dt))

        sem = ctx.enter_context(Signals(nc, "ch_"))

        xn = sb("xn", [P, GT, D])
        stats = sb("stats", [P, GT, 6])
        mv = sb("mv", [P, GT, 2])
        veps = sb("veps", [P, GT])
        rstd = sb("rstd", [P, GT])
        xnT = sb("xnT", [P, GT * P])
        ex = sb("ex", [P, 4 * S])
        ex1 = sb("ex1", [P, 4 * S])
        gatev = sb("gatev", [P, 4 * S])
        m8 = sb("m8", [P, 4, 8])
        gt = sb("gt", [P, 4 * S])
        eq = sb("eq", [P, 4 * S])
        ngt = sb("ngt", [P, 4])
        ceq = sb("ceq", [P, 4 * S])
        tot = sb("tot", [P, 4 * S])
        tied = sb("tied", [P, 4 * S])
        chosen = sb("chosen", [P, 4 * S])
        count = sb("count", [P, 4 * S])
        slot = sb("slot", [P, 4 * S])
        slotT = sb("slotT", [P, GT, E])
        gateT = sb("gateT", [P, GT, E])
        pick = sb("pick", [P, GT, 2, E * KC])
        pickw = sb("pickw", [P, GT, 2, E * KC])
        trigT = sb("trigT", [P, E, NB, KC])
        xg = sb("xg", [P, 2, E, NB, KC])
        trig = sb("trig", [P, 2, E, P])
        pickT = sb("pickT", [P, 2, GT, P])
        qkv = sb("qkv", [P, E, 3, D])
        rot1 = sb("rot1", [P, 2, 4, 2, 64])
        rot2 = sb("rot2", [P, 2, 4, 2, 64])
        qT = sb("qT", [P, 2, 4 * P])
        kT = sb("kT", [P, 2, 4 * P])
        sm = sb("sm", [P, 2, 4, P])
        mx = sb("mx", [P, 2, 4])
        dif = sb("dif", [P, 2, 4, P])
        pe_ = sb("pe", [P, 2, 4, P])
        sums = sb("sums", [P, 2, 4])
        inv = sb("inv", [P, 2, 4])
        prob = sb("prob", [P, 2, 4, P])
        probT = sb("probT", [P, 2, 4, P])
        avT = sb("avT", [P, 2, 4, P])
        xpT = sb("xpT", [P, NB, E, KC])
        xp = sb("xp", [P, GT, D])

        def prep_bank(n):
            return ps[:, n % 2, :]

        def bank(n):
            return ps[:, 2 + n % 6, :]

        pick_set = sem("pick_set")
        stats_done = sem("stats_done")
        moments = sem("moments")
        var_eps = sem("var_eps")
        rstd_done = sem("rstd_done")
        xn_ready = sem("xn_ready")
        NP = 13
        prep_ready = sem("prep_ready")
        prep_copied = sem("prep_copied")
        NC = 12
        choosing = sem("choosing")
        pick_ready = sem("pick_ready")
        pickw_ready = sem("pickw_ready")
        qkv_ready = sem("qkv_ready")
        qkv_copied = sem("qkv_copied")
        rotated1 = sem("rotated1")
        rotated2 = sem("rotated2")
        rotated = sem("rotated")
        qkT_ready = sem("qkT_ready")
        qkT_copied = sem("qkT_copied")
        s_ready = sem("s_ready")
        s_masked = sem("s_masked")
        max_done = sem("max_done")
        shifted = sem("shifted")
        e_ready = sem("e_ready")
        sum_done = sem("sum_done")
        inv_done = sem("inv_done")
        prob_ready = sem("prob_ready")
        probT_ready = sem("probT_ready")
        probT_copied = sem("probT_copied")
        av_ready = sem("av_ready")
        av_copied = sem("av_copied")
        xpT_ready = sem("xpT_ready")
        xpT_copied = sem("xpT_copied")
        xp_ready = sem("xp_ready")
        xp_copied = sem("xp_copied")
        out_ready = sem("out_ready")
        out_added = sem("out_added")

        def tiles(g, k=0, n=GT):
            return x_res[:, bass.ds(g * GT + k, n), :]

        passed = sem("passed")
        block = ctx.enter_context(nc.Block())

        @block.gpsimd
        def _(pool):
            def prep(g, s):
                pool.wait_ge(var_eps, nth(g))
                nc.gpsimd.tensor_tensor(rstd[:, :], veps[:, :], C["mhalf"][:, :], ALU.pow).then_inc(rstd_done, 1)

            two_halves(pool, N, prep, lambda g, s, more: prep(g + 1, 1 - s) if more else None)

        @block.tensor
        def _(pe):
            def transpose4(out, tiles4, width=P):
                for n, t in enumerate(tiles4):
                    last = nc.tensor.transpose(out[0:width, n * P:(n + 1) * P], t, C["ident"])
                return last

            def round_(g, n):
                if n >= 2:
                    pe.wait_ge(prep_copied, nth(g, NP, n - 2))

            def make_xT(g, s, start=False):
                pe.wait_ge(xn_ready, nth(g))
                if not start:
                    pe.wait_ge(prep_copied, g * NP)
                for n in (0, 1):
                    transpose4(prep_bank(n), [xn[:, 4 * n + t, :] for t in range(4)]).then_inc(prep_ready, 1)

            def make_logits(g, s):
                pe.wait_ge(prep_copied, nth(g, NP, 1))
                for q in range(4):
                    last = nc.tensor.matmul(prep_bank(2)[32 * q:32 * q + 32, 0:4 * S], C["wr"],
                                            xnT[:, :].rearrange("p (r q k) -> p q r k", q=4, k=S)[:, q],
                                            start=True, stop=True)
                last.then_inc(prep_ready, 1)

            def make_token_rows(g, s):
                pe.wait_ge(choosing, (g + 1) * NC)
                pe.wait_ge(prep_copied, g * NP + 2)
                pe.sem_inc(passed, 1)
                transpose4(prep_bank(3), [slot[:, r * S:(r + 1) * S] for r in range(4)], S).then_inc(prep_ready, 1)
                pe.wait_ge(prep_copied, g * NP + 3)
                pe.sem_inc(passed, 1)
                transpose4(prep_bank(4), [gatev[:, r * S:(r + 1) * S] for r in range(4)], S).then_inc(prep_ready, 1)

            def make_gathered(g, s):
                pe.wait_ge(pick_ready, nth(g))
                for n in (5, 6):
                    round_(g, n)
                    for t in range(4):
                        last = nc.tensor.matmul(prep_bank(n)[:, t * P:(t + 1) * P], xn[:, 4 * (n - 5) + t, :],
                                                pick[:, 4 * (n - 5) + t].rearrange("p b n -> p (b n)"),
                                                start=True, stop=True)
                    last.then_inc(prep_ready, 1)

            def make_trig(g, s):
                for n in (7, 8):
                    round_(g, n)
                    for t in range(4):
                        last = nc.tensor.matmul(prep_bank(n)[:, t * P:(t + 1) * P], C["trig"],
                                                pick[:, 4 * (n - 7) + t].rearrange("p b n -> p (b n)"),
                                                start=True, stop=True)
                    last.then_inc(prep_ready, 1)
                for n in (9, 10):
                    pe.wait_ge(prep_copied, nth(g, NP, 8))
                    round_(g, n)
                    transpose4(prep_bank(n), [trigT[:, 4 * (n - 9) + e].rearrange("p b k -> p (b k)") for e in range(4)]
                               ).then_inc(prep_ready, 1)

            def make_pickT(g, s):
                pe.wait_ge(pickw_ready, nth(g))
                for n in (11, 12):
                    round_(g, n)
                    transpose4(prep_bank(n),
                               [pickw[:, 4 * (n - 11) + t].rearrange("p b n -> p (b n)") for t in range(4)]
                               ).then_inc(prep_ready, 1)

            def prep(g, s):
                make_xT(g, s, start=True)
                make_logits(g, s)
                make_token_rows(g, s)
                make_gathered(g, s)
                make_trig(g, s)
                make_pickT(g, s)

            def make_qkv(g, s, h, first=False):
                if h == 0 and not first:
                    pe.wait_ge(av_copied, g * 2)
                for e in range(4):
                    if h == 1:
                        pe.wait_ge(qkv_copied, nth(g, 8, e))
                    nc.tensor.matmul(bank(6 * h + e)[:, 0:3 * D], xg[:, s, 4 * h + e].rearrange("p b k -> p (b k)"),
                                     wqkv[:, 4 * h + e, :], start=True, stop=True).then_inc(qkv_ready, 1)

            def make_qkT(g, s, h):
                pe.wait_ge(rotated, nth(g, 2, h))
                if h == 1:
                    pe.wait_ge(qkT_copied, nth(g, 2, 0))
                for n in (0, 1):
                    last = transpose4(bank(4 + 6 * h + n), [qkv[:, 4 * h + e, n, :] for e in range(4)])
                last.then_inc(qkT_ready, 1)

            def make_scores(g, s, h):
                pe.wait_ge(qkT_copied, nth(g, 2, h))
                for e in range(4):
                    cols = slice(e * P, (e + 1) * P)
                    last = nc.tensor.matmul(bank(12 + h)[:, cols], qT[:, h, cols], kT[:, h, cols], start=True,
                                            stop=True)
                last.then_inc(s_ready, 1)

            def make_probT(g, s, h):
                pe.wait_ge(prob_ready, nth(g, 2, h))
                transpose4(bank(4 + h), [prob[:, h, e] for e in range(4)]).then_inc(probT_ready, 1)

            def make_av(g, s, h):
                pe.wait_ge(probT_copied, nth(g, 2, h))
                for e in range(4):
                    last = nc.tensor.matmul(bank(h)[:, e * P:(e + 1) * P], qkv[:, 4 * h + e, 2, :], probT[:, h, e],
                                            start=True, stop=True)
                last.then_inc(av_ready, 1)

            def make_xpT(g, s, h):
                pe.wait_ge(av_copied, nth(g, 2, h))
                for e in range(4):
                    last = nc.tensor.matmul(bank(2 + h)[:, e * P:(e + 1) * P], woe[:, 4 * h + e, :], avT[:, h, e],
                                            start=True, stop=True)
                last.then_inc(xpT_ready, 1)

            def make_xp(g, s):
                pe.wait_ge(xpT_copied, nth(g, 2, 1))
                for n in (0, 1):
                    transpose4(bank(4 + n),
                               [xpT[:, 2 * (4 * n + t):2 * (4 * n + t) + 2].rearrange("p b e k -> p (b e k)")
                                              for t in range(4)]).then_inc(xp_ready, 1)

            def make_out(g, s):
                for n in (0, 1):
                    pe.wait_ge(xp_copied, nth(g, 2, n))
                    for t in range(4):
                        last = nc.tensor.matmul(bank(2 + n)[:, t * D:(t + 1) * D], pickT[:, s, 4 * n + t],
                                                xp[:, 4 * n + t], start=True, stop=True)
                    last.then_inc(out_ready, 1)

            def make_results(g, s):
                make_xpT(g, s, 0)
                make_xpT(g, s, 1)
                make_xp(g, s)
                make_out(g, s)

            def step(g, s, first, more):
                make_qkv(g, s, 0, first)
                if more:
                    make_xT(g + 1, 1 - s)
                make_qkv(g, s, 1)
                make_qkT(g, s, 0)
                if more:
                    make_logits(g + 1, 1 - s)
                make_qkT(g, s, 1)
                make_scores(g, s, 0)
                make_scores(g, s, 1)
                if not first:
                    make_results(g - 1, 1 - s)
                make_probT(g, s, 0)
                make_probT(g, s, 1)
                make_av(g, s, 0)
                make_av(g, s, 1)
                if more:
                    make_token_rows(g + 1, 1 - s)
                    make_gathered(g + 1, 1 - s)
                    make_trig(g + 1, 1 - s)
                    make_pickT(g + 1, 1 - s)
                else:
                    pe.wait_ge(out_added, g * 2)
                    make_results(g, s)

            pe.wait_ge(w_loaded, 32)
            pipelined(pe, N, prep, step)

        @block.scalar
        def _(act):
            A = nc.scalar

            def copy_round(g, n, out, rows=P):
                act.wait_ge(prep_ready, nth(g, NP, n))
                return A.copy(out, prep_bank(n)[0:rows, :])

            def prep_front(g, s):
                for n in (0, 1):
                    copy_round(g, n, xnT[:, n * 512:(n + 1) * 512]).then_inc(prep_copied, 1)

            def prep_exp(g, s):
                act.wait_ge(prep_ready, nth(g, NP, 2))
                A.activation(ex[:, :], prep_bank(2)[:, 0:4 * S], ACT.Exp, scale=-1.0).then_inc(prep_copied, 1)

            def prep_token_rows(g, s):
                for n, dst in ((3, slotT), (4, gateT)):
                    act.wait_ge(prep_ready, nth(g, NP, n))
                    for bb in (0, 1):
                        last = A.copy(dst[64 * bb:64 * bb + 64, :, :],
                                      prep_bank(n)[0:S, :].rearrange("p (t b e) -> p t b e", b=2, e=32)[:, :, bb, 0:E])
                    last.then_inc(prep_copied, 1)

            def by_expert(dst, n):
                return dst.rearrange("p e b k -> p b e k")[:, 8 * n:8 * n + 8]

            def prep_gathered(g, s):
                for n in (5, 6):
                    act.wait_ge(prep_ready, nth(g, NP, n))
                    A.copy(by_expert(xg[:, s], n - 5), prep_bank(n).rearrange("p (b e k) -> p b e k", e=E, k=KC)
                           ).then_inc(prep_copied, 1)

            def prep_trig(g, s):
                for n in (7, 8):
                    act.wait_ge(prep_ready, nth(g, NP, n))
                    A.copy(by_expert(trigT[:, :, :, :], n - 7),
                           prep_bank(n).rearrange("p (b e k) -> p b e k", e=E, k=KC)
                           ).then_inc(prep_copied, 1)
                for n in (9, 10):
                    copy_round(g, n, trig[:, s, 4 * (n - 9):4 * (n - 9) + 4].rearrange("p e n -> p (e n)")
                               ).then_inc(prep_copied, 1)

            def prep_pickT(g, s):
                for n in (11, 12):
                    copy_round(g, n, pickT[:, s, 4 * (n - 11):4 * (n - 11) + 4].rearrange("p t n -> p (t n)")
                               ).then_inc(prep_copied, 1)

            def prep(g, s):
                prep_front(g, s)
                prep_exp(g, s)
                prep_token_rows(g, s)
                prep_gathered(g, s)
                prep_trig(g, s)
                prep_pickT(g, s)

            def copy_qkv(g, h):
                for e in range(4):
                    act.wait_ge(qkv_ready, nth(g, 8, 4 * h + e))
                    last = A.copy(qkv[:, 4 * h + e].rearrange("p c n -> p (c n)"), bank(6 * h + e)[:, 0:3 * D])
                    last.then_inc(qkv_copied, 1)

            def copy_qkT(g, h):
                act.wait_ge(qkT_ready, nth(g, 2, h))
                A.copy(qT[:, h], bank(4 + 6 * h))
                A.copy(kT[:, h], bank(5 + 6 * h)).then_inc(qkT_copied, 1)

            def exps(g, h):
                act.wait_ge(shifted, nth(g, 2, h))
                A.activation(pe_[:, h], dif[:, h], ACT.Exp, scale=ASCALE).then_inc(e_ready, 1)

            def copy4(g, h, ready, out, n, copied):
                act.wait_ge(ready, nth(g, 2, h))
                A.copy(out.rearrange("p e n -> p (e n)"), bank(n)).then_inc(copied, 1)

            def copy_xpT(g, h):
                act.wait_ge(xpT_ready, nth(g, 2, h))
                A.copy(xpT[:, :, :, :].rearrange("p b e k -> p e b k")[:, 4 * h:4 * h + 4],
                       bank(2 + h).rearrange("p (e b k) -> p e b k", e=4, k=KC)).then_inc(xpT_copied, 1)

            def copy_results(g):
                for h in (0, 1):
                    copy_xpT(g, h)
                for n in (0, 1):
                    copy4(g, n, xp_ready, xp[:, 4 * n:4 * n + 4], 4 + n, xp_copied)

            def step(g, s, first, more):
                copy_qkv(g, 0)
                if more:
                    prep_front(g + 1, 1 - s)
                copy_qkv(g, 1)
                copy_qkT(g, 0)
                if more:
                    prep_exp(g + 1, 1 - s)
                copy_qkT(g, 1)
                if not first:
                    for h in (0, 1):
                        copy_xpT(g - 1, h)
                exps(g, 0)
                if not first:
                    for n in (0, 1):
                        copy4(g - 1, n, xp_ready, xp[:, 4 * n:4 * n + 4], 4 + n, xp_copied)
                exps(g, 1)
                for h in (0, 1):
                    copy4(g, h, probT_ready, probT[:, h], 4 + h, probT_copied)
                for h in (0, 1):
                    copy4(g, h, av_ready, avT[:, h], h, av_copied)
                if more:
                    prep_token_rows(g + 1, 1 - s)
                    prep_gathered(g + 1, 1 - s)
                    prep_trig(g + 1, 1 - s)
                    prep_pickT(g + 1, 1 - s)
                else:
                    copy_results(g)

            pipelined(act, N, prep, step)

        @block.vector
        def _(dve):
            V = nc.vector

            def norm(g, s):
                for t in range(GT):
                    last = V.bn_stats(stats[:, t, :], tiles(g, t, 1))
                last.then_inc(stats_done, 1)
                dve.wait_ge(stats_done, g + 1)
                dve.sem_inc(passed, 1)
                for t in range(GT):
                    last = V.bn_aggr(mv[:, t, :], stats[:, t, :])
                last.then_inc(moments, 1)
                dve.wait_ge(moments, nth(g))
                V.tensor_scalar(veps[:, :], mv[:, :, 1], EPS, None, ALU.add).then_inc(var_eps, 1)
                dve.wait_ge(rstd_done, nth(g))
                dve.wait_ge(prep_ready, g * NP)
                for t in range(GT):
                    last = V.tensor_scalar(xn[:, t:t + 1, :], tiles(g, t, 1), mv[:, t, 0:1], rstd[:, t:t + 1],
                                           ALU.subtract, ALU.mult)
                last.then_inc(xn_ready, 1)

            def choose(g, s, part):
                by_r = lambda t: t[:, :].rearrange("p (r k) -> p r k", k=S)
                wide = lambda t: t.unsqueeze(2).broadcast_to((P, 4, S))
                if part == 0:
                    dve.wait_ge(prep_copied, nth(g, NP, 2))
                    V.tensor_scalar(ex1[:, :], ex[:, :], 1.0, None, ALU.add).then_inc(choosing, 1)
                    dve.wait_ge(choosing, nth(g, NC, 0))
                    V.reciprocal(gatev[:, :], ex1[:, :]).then_inc(choosing, 1)
                    dve.wait_ge(choosing, nth(g, NC, 1))
                    dve.sem_inc(passed, 1)
                    for r in range(4):
                        last = V.max(m8[:, r, :], gatev[:, r * S:(r + 1) * S])
                    last.then_inc(choosing, 1)
                if part == 1:
                    dve.wait_ge(choosing, nth(g, NC, 2))
                    V.tensor_tensor(by_r(gt), by_r(gatev), wide(m8[:, :, 7]), ALU.is_gt).then_inc(choosing, 1)
                    dve.wait_ge(choosing, nth(g, NC, 3))
                    V.tensor_tensor(by_r(eq), by_r(gatev), wide(m8[:, :, 7]), ALU.is_equal).then_inc(choosing, 1)
                    dve.wait_ge(choosing, nth(g, NC, 4))
                    V.tensor_reduce(ngt[:, :], by_r(gt), AX.X, ALU.add).then_inc(choosing, 1)
                if part == 2:
                    dve.wait_ge(choosing, nth(g, NC, 5))
                    V.tensor_tensor_scan(ceq[:, :], C["resetmask"], eq[:, :], 0.0, ALU.mult,
                                         ALU.add).then_inc(choosing, 1)
                    dve.wait_ge(choosing, nth(g, NC, 6))
                    V.tensor_tensor(by_r(tot), by_r(ceq), wide(ngt[:, :]), ALU.add).then_inc(choosing, 1)
                    dve.wait_ge(choosing, nth(g, NC, 7))
                    V.scalar_tensor_tensor(tied[:, :], tot[:, :], float(KC), eq[:, :], ALU.is_le,
                                           ALU.mult).then_inc(choosing, 1)
                if part == 3:
                    dve.wait_ge(choosing, nth(g, NC, 8))
                    V.tensor_tensor(chosen[:, :], tied[:, :], gt[:, :], ALU.add).then_inc(choosing, 1)
                    dve.wait_ge(choosing, nth(g, NC, 9))
                    V.tensor_tensor_scan(count[:, :], C["resetmask"], chosen[:, :], 0.0, ALU.mult,
                                         ALU.add).then_inc(choosing, 1)
                    dve.wait_ge(choosing, nth(g, NC, 10))
                    V.tensor_tensor(slot[:, :], count[:, :], chosen[:, :], ALU.mult).then_inc(choosing, 1)

            def make_pick(g, s):
                dve.wait_ge(prep_copied, nth(g, NP, 4))
                iota = C["kiota"].rearrange("p (e k) -> p e k", k=KC).unsqueeze(1).broadcast_to((P, GT, E, KC))
                view = lambda t, b, r: t[r, :, b, :].rearrange("p t (e k) -> p t e k", k=KC)
                wide = lambda t, r: t[r].unsqueeze(3).broadcast_to((64, GT, E, KC))
                for b in (0, 1):
                    r = slice(64 * b, 64 * b + 64)
                    last = V.tensor_tensor(view(pick, b, r), wide(slotT, r), iota[r], ALU.is_equal)
                last.then_inc(pick_ready, 1)
                dve.wait_ge(pick_ready, nth(g))
                for b in (0, 1):
                    r = slice(64 * b, 64 * b + 64)
                    last = V.tensor_tensor(view(pickw, b, r), view(pick, b, r), wide(gateT, r), ALU.mult)
                last.then_inc(pickw_ready, 1)

            def prep(g, s):
                norm(g, s)
                for part in range(4):
                    choose(g, s, part)
                make_pick(g, s)

            def rotate(g, s, h):
                dve.wait_ge(qkv_copied, nth(g, 8, 4 * h + 3))
                es = slice(4 * h, 4 * h + 4)
                cos2 = trig[:, s, es, 0:64].unsqueeze(2).broadcast_to((P, 4, 2, 64))
                sins = [trig[:, s, es, 64 + 32 * j:96 + 32 * j].unsqueeze(2).broadcast_to((P, 4, 2, 32))
                        for j in (0, 1)]
                V.tensor_tensor(rot1[:, h], qkv[:, es, 0:2, 0:64], cos2, ALU.mult).then_inc(rotated1, 1)
                V.tensor_tensor(rot2[:, h, :, :, 0:32], qkv[:, es, 0:2, 32:64], sins[0], ALU.mult)
                V.tensor_tensor(rot2[:, h, :, :, 32:64], qkv[:, es, 0:2, 0:32], sins[1], ALU.mult).then_inc(rotated2, 1)
                dve.wait_ge(rotated1, nth(g, 2, h))
                dve.wait_ge(rotated2, nth(g, 2, h))
                V.tensor_tensor(qkv[:, es, 0:2, 0:64], rot1[:, h], rot2[:, h], ALU.add).then_inc(rotated, 1)

            def shift(g, h):
                dve.wait_ge(s_ready, nth(g, 2, h))
                V.tensor_tensor(sm[:, h], bank(12 + h).rearrange("p (e n) -> p e n", n=P),
                                C["negmask"].unsqueeze(1).broadcast_to((P, 4, P)), ALU.add).then_inc(s_masked, 1)
                dve.wait_ge(s_masked, nth(g, 2, h))
                V.tensor_reduce(mx[:, h], sm[:, h], AX.X, ALU.max).then_inc(max_done, 1)
                dve.wait_ge(max_done, nth(g, 2, h))
                V.tensor_tensor(dif[:, h], sm[:, h], mx[:, h].unsqueeze(2).broadcast_to((P, 4, P)), ALU.subtract
                                ).then_inc(shifted, 1)

            def normalise(g, h):
                dve.wait_ge(e_ready, nth(g, 2, h))
                V.tensor_reduce(sums[:, h], pe_[:, h], AX.X, ALU.add).then_inc(sum_done, 1)
                dve.wait_ge(sum_done, nth(g, 2, h))
                V.reciprocal(inv[:, h], sums[:, h]).then_inc(inv_done, 1)
                dve.wait_ge(inv_done, nth(g, 2, h))
                V.tensor_tensor(prob[:, h], pe_[:, h], inv[:, h].unsqueeze(2).broadcast_to((P, 4, P)), ALU.mult
                                ).then_inc(prob_ready, 1)

            def add_out(g):
                for n in (0, 1):
                    dve.wait_ge(out_ready, nth(g, 2, n))
                    xs = tiles(g, 4 * n, 4)
                    V.tensor_tensor(xs, bank(2 + n).rearrange("p (t d) -> p t d", d=D), xs, ALU.add
                                    ).then_inc(out_added, 1)

            def step(g, s, first, more):
                if more:
                    norm(g + 1, 1 - s)
                dve.wait_ge(prep_copied, nth(g, NP, 10))
                rotate(g, s, 0)
                rotate(g, s, 1)
                if more:
                    choose(g + 1, 1 - s, 0)
                shift(g, 0)
                if more:
                    choose(g + 1, 1 - s, 1)
                shift(g, 1)
                normalise(g, 0)
                normalise(g, 1)
                if more:
                    choose(g + 1, 1 - s, 2)
                    choose(g + 1, 1 - s, 3)
                if not first:
                    add_out(g - 1)
                if more:
                    make_pick(g + 1, 1 - s)
                else:
                    add_out(g)

            V.memset(pick[:, :, :, :], 0.0)
            V.memset(pickw[:, :, :, :], 0.0).then_inc(pick_set, 1)
            dve.wait_ge(pick_set, 1)
            pipelined(dve, N, prep, step)


def setup_phase(nc, ps, C, pack_in, q_mask, pack, work):
    with ExitStack() as ctx:
        sem = ctx.enter_context(Signals(nc, "setup_"))

        pack_loaded = sem("pack_loaded")
        qmask_loaded = sem("qmask_loaded")
        consts_set = sem("consts_set")
        qbias_done = sem("qbias_done")
        qany_done = sem("qany_done")
        qscale_diag = sem("qscale_diag")
        qscale_ready = sem("qscale_ready")
        qscale_copied = sem("qscale_copied")
        block = ctx.enter_context(nc.Block())

        @block.sync
        def _(sp):
            sp.dma_start(pack[:, :], pack_in).then_inc(pack_loaded, 16)
            for r in (0, 1):
                sp.dma_start(work["qmi"][64 * r:64 * r + 64, :], q_mask).then_inc(qmask_loaded, 16)

        @block.tensor
        def _(pe):
            pe.wait_ge(qscale_diag, 1)
            nc.tensor.matmul(ps[:, 1, 0:64], work["ones"][0:64, :], work["diag"][0:64, :], start=True, stop=True
                             ).then_inc(qscale_ready, 1)

        @block.vector
        def _(dve):
            nc.vector.memset(C["mhalf"][:, :], -0.5)
            nc.vector.memset(C["half"][:, :], 0.5)
            nc.vector.memset(C["oneb"][0:64, 0:64], 1.0 / 64)
            nc.vector.memset(C["oneb"][0:64, 64:128], 0.0)
            nc.vector.memset(C["oneb"][64:128, 0:64], 0.0)
            nc.vector.memset(C["oneb"][64:128, 64:128], 1.0 / 64)
            nc.vector.memset(work["ones"][:, :], 1.0).then_inc(consts_set, 1)
            dve.wait_ge(pack_loaded, 16)
            for b in (0, 1):
                nc.vector.tensor_copy(C["identb"][:, S * b:S * b + S], C["ident"][0:S, 0:S]).then_inc(consts_set, 1)
            dve.wait_ge(qmask_loaded, 32)
            nc.vector.tensor_scalar(C["qmask"][:, :], work["qmi"][:, :], 0.0, NEG, ALU.is_equal, ALU.mult
                                    ).then_inc(qbias_done, 1)
            dve.wait_ge(qbias_done, 1)
            nc.vector.tensor_reduce(work["any"][:, 0:1], C["qmask"][:, :], AX.X, ALU.max).then_inc(qany_done, 1)
            dve.wait_ge(qany_done, 1)
            nc.vector.tensor_scalar(work["any"][:, 1:2], work["any"][:, 0:1], 0.0, SCALE, ALU.is_equal, ALU.mult
                                    ).then_inc(qany_done, 1)
            dve.wait_ge(qany_done, 2)
            nc.vector.tensor_scalar(work["diag"][0:64, :], C["ident"][0:64, 0:64], work["any"][0:64, 1:2], None,
                                    ALU.mult
                                    ).then_inc(qscale_diag, 1)
            dve.wait_ge(qscale_ready, 1)
            nc.vector.tensor_copy(C["qscale"][:, :], ps[:, 1, 0:64]).then_inc(qscale_copied, 1)


def build(nc, x_in, ctx_in, q_mask, key_mask, pack_in, wqkv_in, woe_in, gate_in, up_in, down_in, out):
    with ExitStack() as ctx:
        def sb(name, shape, dt=F32):
            return ctx.enter_context(nc.sbuf_tensor(name, shape, dt))

        ps = ctx.enter_context(nc.psum_tensor("ps", [P, 8, 512], F32))
        pack = sb("pack", [P, PACK])
        x_res = sb("x_res", [P, NG * TILES, D])
        C = {"pack": pack}
        for n, (at, w) in COLS.items():
            C[n] = pack[:, at:at + w]
        C["identb"] = sb("identb", [S, P], BF16)
        C["oneb"] = sb("oneb", [P, P], BF16)
        C["mhalf"] = sb("mhalf", [P, 8])
        C["half"] = sb("half", [P, 8])
        C["qmask"] = sb("qmask", [P, S], BF16)
        C["qscale"] = sb("qscale", [P, S])
        work = {"qmi": sb("qmi", [P, S], I32), "ones": sb("ones", [P, P]), "any": sb("qany", [P, 2]),
                "diag": sb("qdiag", [P, S])}
        setup_phase(nc, ps, C, pack_in, q_mask, pack, work)
        with ExitStack() as early:
            wqkv = early.enter_context(nc.sbuf_tensor("wqkv", [P, 8, 3 * D], F32))
            woe = early.enter_context(nc.sbuf_tensor("woe", [P, 8, D], F32))
            chosen_w_loaded = ctx.enter_context(nc.semaphore("chosen_w_loaded"))
            attention_phase(nc, ps, C, x_res, None, x_in, ctx_in, q_mask, key_mask, 0,
                            [(wqkv[:, :, :], wqkv_in, chosen_w_loaded), (woe[:, :, :], woe_in, chosen_w_loaded)])
            choice_phase(nc, ps, C, x_res, wqkv, woe, chosen_w_loaded)
        y_res = sb("y_res", [P, NG * TILES, D])
        attention_phase(nc, ps, C, x_res, y_res, x_in, ctx_in, q_mask, key_mask, 1)
        attention_phase(nc, ps, C, x_res, y_res, x_in, ctx_in, q_mask, key_mask, 2)
        gate, up, down = (sb(n, [P, K, D]) for n in ("gate", "up", "down"))
        w_loaded = [ctx.enter_context(nc.semaphore(f"w_loaded{i}")) for i in range(K // CH)]
        relu_phase(nc, ps, C, x_res, y_res,
                   [(buffer[:, i * CH:(i + 1) * CH, :], array[:, i * CH:(i + 1) * CH, :], w_loaded[i])
                    for i in range(K // CH) for buffer, array in ((gate, gate_in), (up, up_in), (down, down_in))])
        experts_phase(nc, ps, C, x_res, gate, up, down, w_loaded, out)


def kernel(**inputs):
    import concourse.bacc as bacc
    from concourse.bass_utils import run_bass_kernel_spmd

    a = {k: np.ascontiguousarray(v) for k, v in inputs.items()}
    pack = np.zeros((P, PACK), np.float32)

    def put(name, v, off=0):
        v = np.asarray(v, np.float32)
        v = v.reshape(v.shape[0], -1)
        at = COLS[name][0] + off
        pack[:v.shape[0], at:at + v.shape[1]] = v

    attn = [("L0_xattn_W{}", "L0_xattn_b{}", True), ("L1_xattn_sa_w{}", "L1_xattn_sa_b{}", False),
            ("L1_xattn_ca_w{}", "L1_xattn_ca_b{}", False)]
    for i, (w, b, flip) in enumerate(attn):
        for n, c in enumerate("qkv"):
            m = a[w.format(c)]
            put(f"a{i}", m.T if flip else m, n * D)
        m = a[w.format("o")]
        put(f"a{i}", m.T if flip else m, 3 * D)
        put(f"a{i}", np.broadcast_to(a[b.format("o")], (P, D)), 4 * D)
        for n, c in enumerate("qkv"):
            put(f"a{i}", a[b.format(c)][:, None], 5 * D + n)
    put("ident", np.eye(P))
    put("headmask", (np.arange(P)[:, None] // DH % HH == np.arange(HH)[None]) * 1.0)
    for n in ("g1", "b1", "g2", "b2", "g3", "b3"):
        put(n, np.broadcast_to(a["L1_xattn_" + n], (P, D)))
    put("wr", a["L0_ffn_Wr"].T)
    row = np.arange(P)
    put("negmask", np.where((row[:, None] // 8 == row // 8) & (row[:, None] >= row), 0.0, -1e30))
    put("kiota", np.broadcast_to(np.arange(64) % 8 + 1, (P, 64)))
    put("resetmask", np.broadcast_to(np.arange(256) % 64 > 0, (P, 256)))
    angle = ((row % S)[:, None].astype(np.float32)
             * (1.0 / 10000.0 ** (np.arange(32, dtype=np.float32) * 2.0 / 64)).astype(np.float32))
    put("trig", np.concatenate([np.cos(angle), np.cos(angle), -np.sin(angle), np.sin(angle)], 1))
    put("ff2b", np.broadcast_to(a["L1_xattn_ff_b2"], (P, D)))
    put("ff1", a["L1_xattn_ff_w1"])
    put("ff1b", a["L1_xattn_ff_b1"].reshape(4, P).T)
    put("ff2", a["L1_xattn_ff_w2"].reshape(4, P, D).transpose(1, 0, 2))
    put("router", a["L1_ffn_router_w"].T)
    put("rbias", np.broadcast_to(np.tile(a["L1_ffn_bias"], TILES), (P, 64)))
    put("lowmask", np.broadcast_to(np.tril(np.ones((16, 16)), -1).reshape(1, -1), (P, 256)))
    put("glowmask", np.broadcast_to(np.tril(np.ones((4, 4)), -1).reshape(1, -1), (P, 16)))

    def experts(name, shared):
        return np.concatenate([shared, a["L1_ffn_" + name]]).transpose(1, 0, 2).copy()

    arrays = {
        "x": a["x"].reshape(-1, D), "ctx": a["ctx_1024"].reshape(-1, D), "q_mask": a["mask_SxS2_ik0"],
        "key_mask": a["mask_Bx1x1xS2_if1"].reshape(BATCH, S), "pack": pack,
        "wqkv": a["L0_ffn_Wqkv"].transpose(1, 0, 2).copy(), "woe": a["L0_ffn_Wo"].transpose(1, 0, 2).copy(),
        "gate": experts("gate_w", a["L1_ffn_sh_gate_w"].reshape(D, 2, D).transpose(1, 0, 2)),
        "up": experts("up_w", a["L1_ffn_sh_up_w"].reshape(D, 2, D).transpose(1, 0, 2)),
        "down": experts("down_w", a["L1_ffn_sh_down_w"].reshape(2, D, D)),
    }
    nc = bacc.Bacc("TRN2", target_bir_lowering=False, num_devices=1)
    args = [nc.dram_tensor("in_" + n, v.shape, mybir.dt.from_np(v.dtype), kind="ExternalInput").ap()
            for n, v in arrays.items()]
    out = nc.dram_tensor("out", (BATCH * S, D), F32, kind="ExternalOutput").ap()
    build(nc, *args, out)
    r = run_bass_kernel_spmd(nc, [{"in_" + n: v for n, v in arrays.items()}], core_ids=[0])
    return r.results[0]["out"].reshape(BATCH, S, D)
```
